# Optimizing a Trainium2 kernel written in Bass

```python
import numpy as np
import jax
import jax.numpy as jnp

def _softmax(x, axis=-1):
    return jax.nn.softmax(x, axis=axis)

def _gelu(x):
    return jax.nn.gelu(x, approximate=True)

def _silu(x):
    return jax.nn.silu(x)

def _sigmoid(x):
    return jax.nn.sigmoid(x)

def _layernorm(x, axis=-1, eps=1e-05):
    m = jnp.mean(x, axis=axis, keepdims=True)
    v = jnp.var(x, axis=axis, keepdims=True)
    return (x - m) / jnp.sqrt(v + eps)

def _scatter_add(tgt, idx, src, axis=0):
    return tgt.at[idx].add(src)

def _segment_sum(src, seg, n):
    return jax.ops.segment_sum(src, seg, n)
kernel_name = 'mk_gnn_resnorm_d4_gnn_r64_70d48a'

def setup_inputs(seed: int=0):
    np.random.seed(seed)
    _w = jnp.asarray

    def _rec_inputs():
        import jax
        import jax.numpy as jnp
        _gk = jax.random.key(seed)
        x = -0.000202 + 1 * jax.random.normal(jax.random.fold_in(_gk, 1), (50000, 128), jnp.float32)
        src = jax.random.randint(jax.random.fold_in(_gk, 2), (25000,), 0, 50000, jnp.int32)
        dst = jnp.minimum((50000 * jax.random.uniform(jax.random.fold_in(_gk, 3), (25000,)) ** 2.0).astype(jnp.int32), 49999)
        _o = jnp.argsort(dst, stable=True)
        src = src[_o]
        dst = dst[_o]
        edge_type_1344 = jax.random.randint(jax.random.fold_in(_gk, 15), (25000,), 0, 1344, jnp.int32)
        edge_type_9 = jax.random.randint(jax.random.fold_in(_gk, 16), (25000,), 0, 9, jnp.int32)
        edge_weight1 = jax.random.uniform(jax.random.fold_in(_gk, 17), (25000, 1), jnp.float32, 0.0, 0.999998)
        return (x, src, dst, edge_type_1344, edge_type_9, edge_weight1)
    x, src, dst, edge_type_1344, edge_type_9, edge_weight1 = _rec_inputs()

    def _L0_gnn_setup():
        import jax, jax.numpy as jnp
        import numpy as np
        N_NODES, N_EDGES, N_RELS, N_BASES, DIM = (50000, 6250, 1344, 4, 128)
        BN_EPS = 1e-05
        key = jax.random.key(seed)
        ks = jax.random.split(key, 7)
        return {'node_feats': jax.random.normal(ks[0], (N_NODES, DIM), jnp.float32), 'src': jax.random.randint(ks[1], (N_EDGES,), 0, N_NODES, dtype=jnp.int32), 'dst': jax.random.randint(ks[2], (N_EDGES,), 0, N_NODES, dtype=jnp.int32), 'etype': jax.random.randint(ks[3], (N_EDGES,), 0, N_RELS, dtype=jnp.int32), 'norm': jax.random.uniform(ks[4], (N_EDGES, 1), jnp.float32), 'basis': jax.random.normal(ks[5], (N_BASES, DIM, DIM), jnp.float32) * 0.05, 'comp': jax.random.normal(ks[6], (N_RELS, N_BASES), jnp.float32), 'bias': jnp.zeros((DIM,), jnp.float32), 'gamma': jnp.ones((DIM,), jnp.float32), 'beta': jnp.zeros((DIM,), jnp.float32)}
    _L0_gnn_all = _L0_gnn_setup()
    _L0_gnn_in = {k: v for k, v in _L0_gnn_all.items() if k in ('basis', 'comp', 'bias', 'gamma', 'beta')}
    del _L0_gnn_all

    def _L1_gnn_setup():
        import jax, jax.numpy as jnp
        import numpy as np
        N_NODES = 50000
        key = jax.random.key(seed)
        k1, k2, k3, k4, k5 = jax.random.split(key, 5)
        x = jax.random.normal(k1, (N_NODES, 128), dtype=jnp.float32)
        edge_index = jax.random.randint(k2, (25000, 2), 0, N_NODES, dtype=jnp.int64)
        W_neigh = jax.random.normal(k3, (128, 128), dtype=jnp.float32) * (1.0 / np.sqrt(128))
        W_self = jax.random.normal(k4, (128, 128), dtype=jnp.float32) * (1.0 / np.sqrt(128))
        b = jax.random.normal(k5, (128,), dtype=jnp.float32) * 0.01
        return {'x': x, 'edge_index': edge_index, 'W_neigh': W_neigh, 'W_self': W_self, 'b': b}
    _L1_gnn_all = _L1_gnn_setup()
    _L1_gnn_in = {k: v for k, v in _L1_gnn_all.items() if k in ('W_neigh', 'W_self', 'b')}
    del _L1_gnn_all

    def _L2_gnn_setup():
        import jax, jax.numpy as jnp
        import numpy as np
        NUM_EDGE_TYPES = 8
        HIDDEN = 128
        N_NODES = 50000
        N_EDGES = 9375

        def _gru_cell(x, h, W_ih, W_hh, b_ih, b_hh):
            H = h.shape[-1]
            gi = x @ W_ih.T + b_ih
            gh = h @ W_hh.T + b_hh
            i_r, i_z, i_n = (gi[:, :H], gi[:, H:2 * H], gi[:, 2 * H:])
            h_r, h_z, h_n = (gh[:, :H], gh[:, H:2 * H], gh[:, 2 * H:])
            r = jax.nn.sigmoid(i_r + h_r)
            z = jax.nn.sigmoid(i_z + h_z)
            n = jnp.tanh(i_n + r * h_n)
            return (1.0 - z) * n + z * h
        key = jax.random.key(seed)
        ks = jax.random.split(key, 10)
        H = HIDDEN
        h = jax.random.normal(ks[0], (N_NODES, H), dtype=jnp.float32)
        edge_index = jax.random.randint(ks[1], (2, N_EDGES), 0, N_NODES, dtype=jnp.int32)
        edge_type = jax.random.randint(ks[2], (N_EDGES,), 0, NUM_EDGE_TYPES + 1, dtype=jnp.int32)
        s = 1.0 / np.sqrt(H)
        W_msg = jax.random.uniform(ks[3], (H, H), jnp.float32, -s, s)
        b_msg = jax.random.uniform(ks[4], (H,), jnp.float32, -s, s)
        edge_embed = jax.random.normal(ks[5], (NUM_EDGE_TYPES + 1, H), dtype=jnp.float32)
        W_ih = jax.random.uniform(ks[6], (3 * H, H), jnp.float32, -s, s)
        W_hh = jax.random.uniform(ks[7], (3 * H, H), jnp.float32, -s, s)
        b_ih = jax.random.uniform(ks[8], (3 * H,), jnp.float32, -s, s)
        b_hh = jax.random.uniform(ks[9], (3 * H,), jnp.float32, -s, s)
        return {'h': h, 'edge_index': edge_index, 'edge_type': edge_type, 'num_nodes': N_NODES, 'W_msg': W_msg, 'b_msg': b_msg, 'edge_embed': edge_embed, 'W_ih': W_ih, 'W_hh': W_hh, 'b_ih': b_ih, 'b_hh': b_hh}
    _L2_gnn_all = _L2_gnn_setup()
    _L2_gnn_in = {k: v for k, v in _L2_gnn_all.items() if k in ('W_msg', 'b_msg', 'edge_embed', 'W_ih', 'W_hh', 'b_ih', 'b_hh')}
    del _L2_gnn_all

    def _L3_gnn_setup():
        import jax, jax.numpy as jnp
        import numpy as np
        N_NODES = 10000
        N_EDGES = 10000
        D_IN = 128
        D_OUT = 128
        key = jax.random.key(seed)
        ks = jax.random.split(key, 8)
        x = jax.random.normal(ks[0], (N_NODES, D_IN), dtype=jnp.float32)
        edge_index = jax.random.randint(ks[1], (2, N_EDGES), 0, N_NODES, dtype=jnp.int64)
        batch = jnp.zeros((N_NODES,), dtype=jnp.int64)
        s_in = 1.0 / np.sqrt(D_IN)
        s_out = 1.0 / np.sqrt(D_OUT)
        W_lin = jax.random.uniform(ks[2], (D_OUT, D_IN), jnp.float32, -s_in, s_in)
        b_lin = jax.random.uniform(ks[3], (D_OUT,), jnp.float32, -s_in, s_in)
        W_gate = jax.random.uniform(ks[4], (1, D_IN), jnp.float32, -s_in, s_in)
        b_gate = jax.random.uniform(ks[5], (1,), jnp.float32, -s_in, s_in)
        W_out = jax.random.uniform(ks[6], (D_OUT, D_OUT), jnp.float32, -s_out, s_out)
        b_out = jax.random.uniform(ks[7], (D_OUT,), jnp.float32, -s_out, s_out)
        return {'x': x, 'edge_index': edge_index, 'batch': batch, 'W_lin': W_lin, 'b_lin': b_lin, 'W_gate': W_gate, 'b_gate': b_gate, 'W_out': W_out, 'b_out': b_out}
    _L3_gnn_all = _L3_gnn_setup()
    _L3_gnn_in = {k: v for k, v in _L3_gnn_all.items() if k in ('W_lin', 'b_lin', 'W_gate', 'b_gate', 'W_out', 'b_out')}
    del _L3_gnn_all
    return {'x': x, 'src': src, 'dst': dst, 'edge_type_1344': edge_type_1344, 'edge_type_9': edge_type_9, 'edge_weight1': edge_weight1, 'L0_gnn_basis': _L0_gnn_in['basis'], 'L0_gnn_comp': _L0_gnn_in['comp'], 'L0_gnn_bias': _L0_gnn_in['bias'], 'L0_gnn_gamma': _L0_gnn_in['gamma'], 'L0_gnn_beta': _L0_gnn_in['beta'], 'L1_gnn_W_neigh': _L1_gnn_in['W_neigh'], 'L1_gnn_W_self': _L1_gnn_in['W_self'], 'L1_gnn_b': _L1_gnn_in['b'], 'L2_gnn_W_msg': _L2_gnn_in['W_msg'], 'L2_gnn_b_msg': _L2_gnn_in['b_msg'], 'L2_gnn_edge_embed': _L2_gnn_in['edge_embed'], 'L2_gnn_W_ih': _L2_gnn_in['W_ih'], 'L2_gnn_W_hh': _L2_gnn_in['W_hh'], 'L2_gnn_b_ih': _L2_gnn_in['b_ih'], 'L2_gnn_b_hh': _L2_gnn_in['b_hh'], 'L3_gnn_W_lin': _L3_gnn_in['W_lin'], 'L3_gnn_b_lin': _L3_gnn_in['b_lin'], 'L3_gnn_W_gate': _L3_gnn_in['W_gate'], 'L3_gnn_b_gate': _L3_gnn_in['b_gate'], 'L3_gnn_W_out': _L3_gnn_in['W_out'], 'L3_gnn_b_out': _L3_gnn_in['b_out']}

def reference(x, src, dst, edge_type_1344, edge_type_9, edge_weight1, L0_gnn_basis, L0_gnn_comp, L0_gnn_bias, L0_gnn_gamma, L0_gnn_beta, L1_gnn_W_neigh, L1_gnn_W_self, L1_gnn_b, L2_gnn_W_msg, L2_gnn_b_msg, L2_gnn_edge_embed, L2_gnn_W_ih, L2_gnn_W_hh, L2_gnn_b_ih, L2_gnn_b_hh, L3_gnn_W_lin, L3_gnn_b_lin, L3_gnn_W_gate, L3_gnn_b_gate, L3_gnn_W_out, L3_gnn_b_out):
    import jax
    import jax.numpy as jnp

    def _L0_gnn_ref(node_feats, src, dst, etype, norm, basis, comp, bias, gamma, beta):
        import jax, jax.numpy as jnp
        import numpy as np
        N_NODES, N_EDGES, N_RELS, N_BASES, DIM = (50000, 6250, 1344, 4, 128)
        BN_EPS = 1e-05
        n = node_feats.shape[0]
        hb = jnp.einsum('ni,bio->nbo', node_feats, basis)
        msg = jnp.einsum('eb,ebo->eo', comp[etype], hb[src]) * norm
        agg = jax.ops.segment_sum(msg, dst, num_segments=n)
        h = jax.nn.relu(agg + bias)
        h = h + node_feats
        mean = jnp.mean(h, axis=0)
        var = jnp.var(h, axis=0)
        h = (h - mean) * jax.lax.rsqrt(var + BN_EPS) * gamma + beta
        return jax.nn.relu(h)

    def _L1_gnn_ref(x, edge_index, W_neigh, W_self, b):
        import jax, jax.numpy as jnp
        import numpy as np
        N_NODES = 50000
        n = x.shape[0]
        src = edge_index[:, 0]
        dst = edge_index[:, 1]
        agg_sum = jax.ops.segment_sum(x[dst], src, num_segments=n)
        agg_sum = agg_sum + jax.ops.segment_sum(x[src], dst, num_segments=n)
        ones = jnp.ones((edge_index.shape[0],), dtype=x.dtype)
        deg = jax.ops.segment_sum(ones, src, num_segments=n)
        deg = deg + jax.ops.segment_sum(ones, dst, num_segments=n)
        agg_mean = agg_sum / jnp.maximum(deg, 1.0)[:, None]
        return agg_mean @ W_neigh + x @ W_self + b

    def _L2_gnn_ref(h, edge_index, edge_type, num_nodes, W_msg, b_msg, edge_embed, W_ih, W_hh, b_ih, b_hh):
        import jax, jax.numpy as jnp
        import numpy as np
        NUM_EDGE_TYPES = 8
        HIDDEN = 128
        N_NODES = 50000
        N_EDGES = 9375

        def _gru_cell(x, h, W_ih, W_hh, b_ih, b_hh):
            H = h.shape[-1]
            gi = x @ W_ih.T + b_ih
            gh = h @ W_hh.T + b_hh
            i_r, i_z, i_n = (gi[:, :H], gi[:, H:2 * H], gi[:, 2 * H:])
            h_r, h_z, h_n = (gh[:, :H], gh[:, H:2 * H], gh[:, 2 * H:])
            r = jax.nn.sigmoid(i_r + h_r)
            z = jax.nn.sigmoid(i_z + h_z)
            n = jnp.tanh(i_n + r * h_n)
            return (1.0 - z) * n + z * h
        src = edge_index[0]
        dst = edge_index[1]
        src_h = h[src] @ W_msg.T + b_msg
        emb = edge_embed[jnp.clip(edge_type, 0, NUM_EDGE_TYPES)]
        msg = src_h + emb
        messages = jax.ops.segment_sum(msg, dst, num_segments=num_nodes)
        h_new = _gru_cell(messages, h[:num_nodes], W_ih, W_hh, b_ih, b_hh)
        result = jnp.zeros_like(h).at[:num_nodes].set(h_new)
        return result

    def _L3_gnn_ref(x, edge_index, batch, W_lin, b_lin, W_gate, b_gate, W_out, b_out):
        import jax, jax.numpy as jnp
        import numpy as np
        N_NODES = 10000
        N_EDGES = 10000
        D_IN = 128
        D_OUT = 128
        row, col = (edge_index[0], edge_index[1])
        n = x.shape[0]
        messages = x[col]
        gate = messages @ W_gate.T + b_gate
        h = messages @ W_lin.T + b_lin
        g = gate[:, 0]
        seg_max = jax.ops.segment_max(g, row, num_segments=n)
        e = jnp.exp(g - seg_max[row])
        denom = jax.ops.segment_sum(e, row, num_segments=n) + 1e-16
        attn = (e / denom[row])[:, None]
        pooled = jax.ops.segment_sum(attn * h, row, num_segments=n)
        return pooled @ W_out.T + b_out
    edge_index = jnp.stack([src, dst])
    edge_index_t = jnp.stack([src, dst], axis=1)
    batch0 = jnp.zeros((50000,), jnp.int32)
    x = _layernorm(x + _L0_gnn_ref(x, src, dst, edge_type_1344, edge_weight1, L0_gnn_basis, L0_gnn_comp, L0_gnn_bias, L0_gnn_gamma, L0_gnn_beta), axis=-1)
    x = _layernorm(x + _L1_gnn_ref(x, edge_index_t, L1_gnn_W_neigh, L1_gnn_W_self, L1_gnn_b), axis=-1)
    x = _layernorm(x + _L2_gnn_ref(x, edge_index, edge_type_9, 50000, L2_gnn_W_msg, L2_gnn_b_msg, L2_gnn_edge_embed, L2_gnn_W_ih, L2_gnn_W_hh, L2_gnn_b_ih, L2_gnn_b_hh), axis=-1)
    x = _layernorm(x + _L3_gnn_ref(x, edge_index, batch0, L3_gnn_W_lin, L3_gnn_b_lin, L3_gnn_W_gate, L3_gnn_b_gate, L3_gnn_W_out, L3_gnn_b_out), axis=-1)
    return x

_drawn_inputs = setup_inputs


def setup_inputs(seed=0):
    import zlib

    import numpy as np

    out = dict(_drawn_inputs(seed))
    spreads = {'L0_gnn_bias': (0.0, 0.597), 'L0_gnn_gamma': (1.0, 0.2), 'L0_gnn_beta': (0.0, 0.1)}
    factors = {'L1_gnn_b': 8.0,
     'L2_gnn_b_msg': 6.443,
     'L2_gnn_b_ih': 3.177,
     'L2_gnn_b_hh': 4.981,
     'L3_gnn_b_lin': 3.324}
    for name, (base, spread) in spreads.items():
        noise = np.random.default_rng([zlib.crc32(name.encode()), seed]).standard_normal(out[name].shape)
        drawn = base * np.exp(spread * noise) if base else spread * noise
        out[name] = jnp.asarray(drawn.astype(out[name].dtype))
    for name, factor in factors.items():
        out[name] = (out[name] * factor).astype(out[name].dtype)
    return out
```

```python
import struct
from contextlib import ExitStack

import concourse.bass as bass
from concourse import mybir

F32 = mybir.dt.float32
BF16 = mybir.dt.bfloat16
I32 = mybir.dt.int32
U16 = mybir.dt.uint16
ALU = mybir.AluOpType
ACT = mybir.ActivationFunctionType

P = 128
N = 50000
E = 25000
D = 128
EPS = 1e-5
TYPES = 9
RELS, BASES = 1344, 4

G = 8
BLOCK = P * G
BLOCKS = -(-N // BLOCK)
NPAD = BLOCKS * BLOCK
TILES = BLOCKS * G
HALVES = TILES // 4
TAIL = (N - (BLOCKS - 1) * BLOCK) // G
LAST = NPAD - 1

ECOLS = -(-E // P)
ELAST = E - (P - 1) * ECOLS
ETILES = ECOLS
MTILES = -(-2 * E // P)
MCOLS = 392

SCOLS = 256
DST, SRC, REV = 0, 1, 2
SHIFT_D = 512
CENTRE, SHIFT_S = 25088, 256

RING = 28
SET = RING // 2
LAG = 6
FLIGHT = 7
MSG = D + TYPES
XROW = D + 1
PAIRS = TILES // 2
SPAN = 2
SPAN_ALL = 3
NCNT = 200
ENTRY = 4


def float_of(bits):
    return struct.unpack("<f", struct.pack("<I", bits))[0]


PAD_D = float_of((LAST + SHIFT_D) << 15)
PAD_S = float_of((LAST - CENTRE + SHIFT_S) << 16)


def runs(count):
    whole = count // 16 * 16
    return [(a, b) for a, b in ((0, whole), (whole, count)) if b > a]


class Half:

    def __init__(self, i, u):
        self.i, self.u = i, u

    @property
    def k(self):
        return self.i * 4 + self.u

    def minus(self, lag):
        return Half(self.i + (self.u - lag) // 4, (self.u - lag) % 4)

    def live(self):
        return not isinstance(self.i, int) or 0 <= self.k < HALVES

    def landed(self):
        return self.i * 16 + 16


def each_half(eng, stage, lag):
    peeled = -(-(lag + 4) // 4)
    for k in range(4 * peeled):
        stage(Half(k // 4, k % 4))
    with eng.Fori(peeled, HALVES // 4) as i:
        for u in range(4):
            stage(Half(i, u))
    for k in range(HALVES // 4 * 4, HALVES + lag):
        stage(Half(k // 4, k % 4))


def wait(eng, sem, value):
    if not isinstance(value, int) or value > 0:
        eng.wait_ge(sem, value)


def build(nc, x_in, src_in, dst_in, rel_in, type_in, weight_in, basis_in, comp_in, bias0_in, gamma_in,
          beta_in, wneigh_in, wself_in, b1_in, wmsg_in, bmsg_in, emb_in, wih_in, whh_in, bih_in, bhh_in,
          wlin_in, blin_in, wgate_in, bgate_in, wout_in, bout_in, out):
    with ExitStack() as ctx:
        def sb(name, shape, dt=F32):
            return ctx.enter_context(nc.sbuf_tensor(name, shape, dt))

        def sem(name):
            return ctx.enter_context(nc.semaphore(name))

        x1_rows = nc.dram_tensor("x1_rows", [NPAD, D], F32).ap()
        x2_rows = nc.dram_tensor("x2_rows", [NPAD, D], F32).ap()
        x3_rows = nc.dram_tensor("x3_rows", [NPAD, D], F32).ap()
        ht_halves = nc.dram_tensor("ht_halves", [HALVES, P, 512], F32).ap()
        payload_rows = nc.dram_tensor("payload_rows", [P * ECOLS, 8], F32).ap()

        wide = [ctx.enter_context(nc.psum_tensor(f"wide{n}", [P, 4, 256], F32)) for n in range(2)]
        bank = [ctx.enter_context(nc.psum_tensor(f"bank{n}", [P, 512], F32)) for n in range(4)]

        ident = sb("ident", [P, P])
        ones = sb("ones", [P, P])
        iota = sb("iota", [P, BLOCK])
        block_base = sb("block_base", [P, 64])
        eps_col = sb("eps_col", [P, 1])
        key_dst = sb("key_dst", [P, ETILES])
        key_src = sb("key_src", [P, ETILES])
        key_all = sb("key_all", [P, MCOLS])
        at_edge = sb("at_edge", [P, ETILES], I32)
        edge_data = sb("edge_data", [P, ETILES, 8])
        at_dst = sb("at_dst", [P, ETILES], I32)
        at_all = sb("at_all", [P, MCOLS], I32)
        pairs_dst = sb("pairs_dst", [1, NCNT * ENTRY], U16)
        pairs_src = sb("pairs_src", [1, NCNT * ENTRY], U16)
        pairs_all = sb("pairs_all", [1, NCNT * ENTRY], U16)
        type_counts = sb("type_counts", [P, TILES, TYPES])
        ring = sb("ring", [P, RING, XROW])
        ring_at = sb("ring_at", [P, RING], I32)
        basis = sb("basis", [P, BASES * D])
        column = sb("column", [P, 16])
        xb = sb("xb", [P, 4, 4 * D])
        yb = sb("yb", [P, 4, 4 * D])
        ob = sb("ob", [P, 4, 4 * D])
        pair = [sb(f"pair{n}", [P, 2, 4 * D]) for n in range(3)]
        selector = sb("selector", [P, 2, SPAN_ALL * 2 * P])
        more_selector = sb("more_selector", [P, 2 * P])
        key_rel = sb("key_rel", [P, 2, MCOLS])
        moments = ob[:, :, :].rearrange("p a b -> p (a b)")[:, 0:(HALVES - 2 + 8) * 6].rearrange(
            "p (n s) -> p n s", s=6)
        tile_stats = sb("tile_stats", [P, 4, 4, 6])
        mean_var = sb("mean_var", [P, 4, 4, 2])
        root = sb("root", [P, 4, 4])
        inverse = sb("inverse", [P, 4, 4])
        offset = sb("offset", [P, 4, 4])
        big = sb("big", [P, ETILES * MSG])
        messages = big[:, :].rearrange("p (e f) -> p e f", f=MSG)

        def part(offset, *shape):
            size = 1
            for n in shape:
                size *= n
            piece = big[:, offset:offset + size]
            if len(shape) == 2:
                piece = piece.rearrange("p (a b) -> p a b", a=shape[0])
            if len(shape) == 3:
                piece = piece.rearrange("p (a b c) -> p a b c", a=shape[0], b=shape[1])
            return piece, offset + size

        landed = [sem(f"landed{j}") for j in range(FLIGHT)]

        raw_rel, at = part(0, ECOLS)
        raw_src, at = part(at, ECOLS)
        raw_dst, at = part(at, ECOLS)
        raw_type, at = part(at, ECOLS)
        weight, at = part(at, ECOLS)
        coef, at = part(at, ECOLS, BASES)
        payload_out, at = part(at, ECOLS, 8)
        keys0, at = part(at, 3 * SCOLS)
        keys1, at = part(at, 3 * SCOLS)
        position, at = part(at, 3 * SCOLS)
        gray, at = part(at, 3 * SCOLS)
        flips, at = part(at, 3 * SCOLS)
        edge_no, at = part(at, ECOLS)
        place, at = part(at, 2, ECOLS)
        scratch, at = part(at, 4, MCOLS)
        table_dst, at = part(at, SCOLS)
        table_src, at = part(at, SCOLS)
        table_all, at = part(at, 2 * SCOLS)
        last_keys, at = part(at, 8)
        last_tile, at = part(at, 8)
        last_work, at = part(at, 3, 8)
        before, at = part(at, 2, NCNT)
        pair_work, at = part(at, 6, NCNT)
        coef_ring, at = part(at, RING, BASES)
        assert at <= ETILES * MSG
        sign_mask = sb("sign_mask", [P, MCOLS], I32)
        keys = [keys0, keys1]

        def ints(piece):
            return piece.bitcast(I32)

        zeroed = sem("zeroed")
        raw_in = sem("raw_in")
        iotas = sem("iotas")
        vector_chain = sem("vector_chain")
        turn = sem("turn")
        turned = sem("turned")
        moved = sem("moved")
        tables = sem("tables")
        comparing = sem("comparing")
        compared = sem("compared")
        indices = sem("indices")
        coefs_arrived = sem("coefs_arrived")
        coef_moved = sem("coef_moved")
        pool_chain = sem("pool_chain")
        payload_made = sem("payload_made")
        payload_stored = sem("payload_stored")

        steps = [("flip", None, DST)]
        for m in range(1, 17):
            first = DST if m < 16 else SRC
            if m > 8:
                steps.append(("turn", None, DST))
                for bit in range(m - 1, 6, -1):
                    steps.append(("compare", 256 if bit == 15 else 1 << (bit - 8) if bit > 7 else P, first))
                steps.append(("turn", None, first))
            for bit in range(min(m - 1, 7 if m < 9 else 6), -1, -1):
                steps.append(("compare", 1 << bit, first))
            if m < 16:
                steps.append(("flip", m, DST))
        steps.append(("turn", None, SRC))
        turns = [(n % 2, first) for n, (kind, _, first) in enumerate(steps) if kind == "turn"]
        SPLIT = len(turns) - 3
        FINAL = len(turns) - 1

        counts = ((0, 2, pairs_dst, ETILES, SPAN), (2, 4, pairs_src, ETILES, SPAN),
                  (4, 8, pairs_all, MTILES, SPAN_ALL))

        TURNS = RING // FLIGHT

        def gather_rounds(pool, rounds, rows, index_of, slot_of, free, arrived, base, after=None):
            def one_round(i):
                for j in range(RING):
                    first = isinstance(i, int)
                    if j % SET == 0:
                        s = j // SET
                        pool.tensor_copy(ring_at[:, j:j + SET], index_of(i, s)).then_inc(indices, 1)
                        pool.wait_ge(indices, i * 2 + (2 * base + s + 1))
                    free(i, j)
                    if j >= LAG or not first:
                        pool.wait_ge(landed[(j - LAG) % FLIGHT],
                                     i * (16 * TURNS) + 16 * (base * TURNS + (j - LAG) // FLIGHT + 1))
                        pool.sem_inc(arrived, 1)
                    pool.indirect_dma_start(
                        out=slot_of(j), out_offset=None, in_=rows,
                        in_offset=bass.IndirectOffsetOnAxis(ap=ring_at[:, j:j + 1], axis=0),
                    ).then_inc(landed[j % FLIGHT], 16)
                    if after and j >= LAG:
                        after(i, j - LAG)
                    elif after and not first:
                        after(i - 1, j - LAG + RING)

            one_round(0)
            with pool.Fori(1, rounds) as i:
                one_round(i)
            for j in range(RING - LAG, RING):
                pool.wait_ge(landed[j % FLIGHT], 16 * ((rounds - 1 + base) * TURNS + j // FLIGHT + 1))
                pool.sem_inc(arrived, 1)
                if after:
                    after(rounds - 1, j)

        with nc.Block() as block:

            @block.sync
            def _(sp):
                sp.wait_ge(zeroed, 1)
                for piece, source in ((raw_rel, rel_in), (raw_src, src_in), (raw_dst, dst_in), (raw_type, type_in),
                                      (weight, weight_in.rearrange("e o -> (e o)"))):
                    piece = piece if source.dtype == F32 else ints(piece)
                    for a, b in runs(P - 1):
                        sp.dma_start(piece[a:b, :],
                                     source[a * ECOLS:b * ECOLS].rearrange("(p c) -> p c", c=ECOLS)).then_inc(raw_in, 16)
                    sp.dma_start(piece[P - 1:P, 0:ELAST],
                                 source[(P - 1) * ECOLS:E].rearrange("(p c) -> p c", p=1)).then_inc(raw_in, 16)
                sp.wait_ge(payload_made, 1)
                sp.dma_start(payload_rows.rearrange("(p c) f -> p (c f)", c=ECOLS),
                             payload_out.rearrange("p c f -> p (c f)")).then_inc(payload_stored, 16)
                sp.wait_ge(payload_stored, 16)

            @block.gpsimd
            def _(pool):
                pool.memset(big[:, 0:5 * ECOLS], 0.0).then_inc(zeroed, 1)
                pool.iota(ints(position)[:, 0:SCOLS], [[1, SCOLS]], base=0, channel_multiplier=SCOLS)
                pool.iota(ints(position)[:, SCOLS:2 * SCOLS], [[1, SCOLS]], base=0, channel_multiplier=SCOLS)
                pool.iota(ints(position)[:, 2 * SCOLS:3 * SCOLS], [[1, SCOLS]], base=P * SCOLS,
                          channel_multiplier=SCOLS)
                pool.iota(ints(edge_no), [[1, ECOLS]], base=0, channel_multiplier=ECOLS).then_inc(iotas, 1)
                pool.memset(ident[:, :], 0.0).then_inc(pool_chain, 1)
                pool.wait_ge(pool_chain, 1)
                pool.affine_select(out=ident[:, :], in_=ident[:, :], compare_op=ALU.not_equal, fill=1.0, base=0,
                                   pattern=[[-1, P]], channel_multiplier=1)
                pool.memset(ones[:, :], 1.0)
                pool.memset(eps_col[:, :], EPS)
                pool.memset(ring[:, :, D:XROW], 1.0)
                pool.iota(iota[:, :], [[1, BLOCK]], base=0, channel_multiplier=0,
                          allow_small_or_imprecise_dtypes=True)
                pool.iota(block_base[:, :], [[BLOCK, 64]], base=0, channel_multiplier=0,
                          allow_small_or_imprecise_dtypes=True).then_inc(iotas, 1)
                pool.memset(payload_out, 0.0).then_inc(pool_chain, 1)
                pool.wait_ge(raw_in, 15 * 16)

                def free(i, j):
                    if j == 0:
                        wait(pool, coef_moved, i * 2 - 1)
                    if j == SET:
                        wait(pool, coef_moved, i * 2)

                def landed_set(i, j):
                    if j % SET == SET - 1:
                        pool.tensor_copy(coef[:, bass.ds(i * RING + (j - SET + 1), SET), :],
                                         coef_ring[:, j - SET + 1:j + 1, :]).then_inc(coef_moved, 1)

                gather_rounds(pool, ECOLS // RING, comp_in,
                              lambda i, s: ints(raw_rel)[:, bass.ds(i * RING + s * SET, SET)],
                              lambda j: coef_ring[:, j, :], free, coefs_arrived, 0, landed_set)
                pool.wait_ge(coef_moved, 2 * ECOLS // RING)
                pool.wait_ge(pool_chain, 2)
                pool.tensor_tensor(payload_out[:, :, 2:2 + BASES], coef,
                                   weight.unsqueeze(2).to_broadcast([P, ECOLS, BASES]), ALU.mult)
                pool.tensor_copy(ints(payload_out)[:, :, 0], ints(raw_src))
                pool.tensor_copy(ints(payload_out)[:, :, 1], ints(raw_type)).then_inc(payload_made, 1)

            @block.tensor
            def _(pe):
                pe.wait_ge(iotas, 2)
                for n, (source, first) in enumerate(turns):
                    pe.wait_ge(turn, n + 1)
                    if n >= 2:
                        pe.wait_ge(moved, n - 1)
                    for a in range(first, 3):
                        for h in range(2):
                            last = pe.transpose(wide[n % 2][:, a, h * P:(h + 1) * P],
                                                keys[source][:, a * SCOLS + h * P:a * SCOLS + (h + 1) * P], ident[:, :])
                    last.then_inc(turned, 1)
                n = 0
                for c, (a, b, _, _, _) in enumerate(counts):
                    for m in range(a, b):
                        n += 1
                        pe.wait_ge(comparing, n)
                        pe.matmul(bank[c][0:1, 0:NCNT], lhsT=ones[:, 0:1], rhs=before[:, m % 2, :],
                                  start=m == a, stop=m == b - 1).then_inc(compared, 1)

            @block.scalar
            def _(act):
                for n, (source, first) in enumerate(turns):
                    act.wait_ge(turned, n + 1)
                    if n == SPLIT:
                        for a, table in ((DST, table_dst), (SRC, table_src)):
                            act.activation(table.rearrange("q (p h) -> q h p", h=2),
                                           wide[n % 2][:, a, :].rearrange("q (h p) -> q h p", h=2), ACT.Copy)
                    if n < FINAL:
                        act.activation(keys[1 - source][:, first * SCOLS:], wide[n % 2][:, first:3, :].rearrange(
                            "q a c -> q (a c)"), ACT.Copy).then_inc(moved, 1)
                    else:
                        for a, h in ((0, SRC), (1, REV)):
                            last = act.activation(
                                table_all[:, a * SCOLS:(a + 1) * SCOLS].rearrange("q (p h) -> q h p", h=2),
                                wide[n % 2][:, h, :].rearrange("q (h p) -> q h p", h=2), ACT.Copy)
                        last.then_inc(moved, 1)

            @block.vector
            def _(dve):
                chain = [0]

                def then_wait(instruction):
                    chain[0] += 1
                    instruction.then_inc(vector_chain, 1)
                    dve.wait_ge(vector_chain, chain[0])

                def bits(target, source, a, op0, b=None, op1=None):
                    if op1 is None:
                        return dve.tensor_scalar(target, source, a, None, op0)
                    return dve.tensor_scalar(target, source, a, b, op0, op1)

                SHR, SHL, SAR, AND = (ALU.logical_shift_right, ALU.logical_shift_left, ALU.arith_shift_right,
                                      ALU.bitwise_and)
                dve.wait_ge(iotas, 1)
                dve.memset(keys0[:, 0:SCOLS], PAD_D)
                dve.memset(keys0[:, SCOLS:], PAD_S)
                then_wait(bits(ints(gray), ints(position), 1, SHR))
                then_wait(dve.tensor_tensor(ints(gray), ints(gray), ints(position), ALU.bitwise_xor))
                dve.wait_ge(raw_in, 15 * 16)
                t0, t1 = ints(scratch)[:, 0, 0:ECOLS], ints(scratch)[:, 1, 0:ECOLS]
                for n, raw in enumerate((raw_src, raw_dst)):
                    at_place = ints(place)[:, n, :]
                    bits(t0, ints(raw), G - 1, AND, 7, SHL)
                    bits(t1, ints(raw), 3, SHR, P - 1, AND)
                    then_wait(bits(at_place, ints(raw), 10, SHR, 10, SHL))
                    then_wait(dve.tensor_tensor(at_place, at_place, t0, ALU.bitwise_or))
                    then_wait(dve.tensor_tensor(at_place, at_place, t1, ALU.bitwise_or))
                    then_wait(dve.tensor_scalar(t0, ints(edge_no), E, float(LAST), ALU.is_ge, ALU.mult))
                    then_wait(dve.tensor_tensor(at_place, at_place, t0, ALU.add))
                then_wait(dve.tensor_scalar(t0, ints(place)[:, 1, :], float(SHIFT_D), None, ALU.add))
                then_wait(bits(t0, t0, 15, SHL))
                then_wait(dve.tensor_tensor(ints(keys0)[:, 0:ECOLS], t0, ints(edge_no), ALU.bitwise_or))
                for a, own, other in ((SRC, 0, raw_dst), (REV, 1, raw_src)):
                    then_wait(dve.tensor_scalar(t0, ints(place)[:, own, :], float(CENTRE), 2.0 * SHIFT_S, ALU.is_ge,
                                                ALU.mult))
                    then_wait(dve.scalar_tensor_tensor(t1, ints(place)[:, own, :], float(-CENTRE - SHIFT_S), t0,
                                                       ALU.add, ALU.add))
                    then_wait(bits(t1, t1, 16, SHL))
                    then_wait(dve.tensor_tensor(t1, t1, ints(other), ALU.bitwise_or))
                    then_wait(bits(sign_mask[:, 0:ECOLS], t1, 31, SAR, 0x7FFFFFFF, AND))
                    then_wait(dve.tensor_tensor(ints(keys0)[:, a * SCOLS:a * SCOLS + ECOLS], t1,
                                                sign_mask[:, 0:ECOLS], ALU.bitwise_xor))

                n_turn = 0
                for n, (kind, value, first) in enumerate(steps):
                    source, target = keys[n % 2], keys[1 - n % 2]
                    if kind == "flip":
                        number, m = (position, 1) if value is None else (gray, value)
                        if n == 0:
                            then_wait(bits(ints(flips), ints(number), m, SHR, 31, SHL))
                        then_wait(dve.tensor_tensor(ints(target), ints(source), ints(flips), ALU.bitwise_xor))
                    elif kind == "compare":
                        low, high, low_to, high_to = (
                            x[:, first * SCOLS:].rearrange("p (n two d) -> p n two d", two=2, d=value)[:, :, w, :]
                            for x in (source, target) for w in (0, 1))
                        dve.tensor_tensor(low_to, low, high, ALU.min)
                        if steps[n + 1][0] == "flip":
                            bits(ints(flips), ints(gray), steps[n + 1][1], SHR, 31, SHL)
                        then_wait(dve.tensor_tensor(high_to, low, high, ALU.max))
                    else:
                        if n_turn == SPLIT:
                            then_wait(dve.tensor_copy(last_keys[:, 0:4], source[:, 0:2 * SCOLS].rearrange(
                                "p (n c) -> p n c", c=P)[:, :, P - 1]))
                        if n_turn == FINAL:
                            then_wait(dve.tensor_copy(last_keys[:, 4:8], source[:, SCOLS:3 * SCOLS].rearrange(
                                "p (n c) -> p n c", c=P)[:, :, P - 1]))
                        n_turn += 1
                        dve.sem_inc(turn, 1)
                        dve.wait_ge(moved, n_turn)

                def places_of_pairs(target, table, width, other):
                    mask, key, high = sign_mask[:, 0:width], ints(scratch)[:, 0, 0:width], ints(scratch)[:, 1, 0:width]
                    then_wait(bits(mask, ints(table), 31, SAR, 0x7FFFFFFF, AND))
                    then_wait(dve.tensor_tensor(key, ints(table), mask, ALU.bitwise_xor))
                    if other is not None:
                        bits(other, key, 0xFFFF, AND)
                    then_wait(bits(high, key, 16, SAR))
                    then_wait(dve.tensor_scalar(scratch[:, 2, 0:width], high, 0.0, -2.0 * SHIFT_S, ALU.is_ge, ALU.mult))
                    then_wait(dve.scalar_tensor_tensor(target, high, float(CENTRE + SHIFT_S), scratch[:, 2, 0:width],
                                                       ALU.add, ALU.add))

                def places_of_edges(target, table, width, edge):
                    high = ints(scratch)[:, 3, 0:width]
                    if edge is not None:
                        bits(edge, ints(table), 0x7FFF, AND).then_inc(vector_chain, 1)
                        chain[0] += 1
                    then_wait(bits(high, ints(table), 15, SHR))
                    then_wait(dve.tensor_scalar(target, high, float(-SHIFT_D), None, ALU.add))

                places_of_edges(key_dst[:, :], table_dst[:, 0:ETILES], ETILES, at_edge[:, :])
                places_of_pairs(key_src[:, :], table_src[:, 0:ETILES], ETILES, at_dst[:, :])
                places_of_pairs(key_all[:, :], table_all[:, 0:MCOLS], MCOLS, at_all[:, :])
                places_of_edges(last_work[:, 0, 0:2], last_keys[:, 0:2], 2, None)
                places_of_pairs(last_work[:, 0, 2:8], last_keys[:, 2:8], 6, None)
                then_wait(dve.tensor_copy(ints(last_work)[:, 1, :], last_work[:, 0, :]))
                then_wait(bits(ints(last_work)[:, 2, :], ints(last_work)[:, 1, :], 8, SHR))
                then_wait(dve.tensor_copy(last_tile, ints(last_work)[:, 2, :]))
                for m in range(8):
                    if m >= 2:
                        dve.wait_ge(compared, m - 1)
                    dve.tensor_scalar(before[:, m % 2, :], iota[:, 0:NCNT], last_tile[:, m:m + 1], None,
                                      ALU.is_gt).then_inc(comparing, 1)
                first, base, more, so_far, work, zero = (pair_work[0:1, n, :] for n in range(6))
                then_wait(dve.memset(pair_work[0:1, :, :], 0.0))
                for c, (_, b, table, tiles, span) in enumerate(counts):
                    entry = table.rearrange("o (n f) -> o n f", f=ENTRY)
                    dve.wait_ge(compared, b)
                    then_wait(dve.tensor_scalar(first, bank[c][0:1, 0:NCNT], float(tiles - 1), None, ALU.min))
                    then_wait(dve.tensor_scalar(base, first, float(tiles - span), None, ALU.min))
                    then_wait(dve.tensor_tensor(more[:, 0:NCNT - 1], first[:, 1:NCNT], base[:, 0:NCNT - 1],
                                                ALU.subtract))
                    then_wait(dve.tensor_scalar(more, more, float(1 - span), 0.0, ALU.add, ALU.max))
                    then_wait(dve.tensor_tensor_scan(so_far[:, 1:NCNT], more[:, 0:NCNT - 1], zero[:, 1:NCNT], 0.0,
                                                     ALU.add, ALU.max))
                    then_wait(dve.tensor_tensor(work, base, so_far, ALU.subtract))
                    dve.tensor_copy(entry[:, :, 0], so_far)
                    dve.tensor_copy(entry[:, :, 1], base)
                    then_wait(dve.tensor_scalar(entry[:, :, 2], work, float(span), None, ALU.add))
                    then_wait(dve.tensor_tensor(work[:, 0:NCNT - 1], base[:, 1:NCNT], base[:, 0:NCNT - 1],
                                                ALU.subtract))
                    then_wait(dve.tensor_tensor(entry[:, 0:NCNT - 1, 3], work[:, 0:NCNT - 1], more[:, 0:NCNT - 1],
                                                ALU.subtract))


        data_arrived = sem("data_arrived")
        data_moved = sem("data_moved")
        rows_arrived = sem("rows_arrived")
        row_turned = sem("row_turned")
        row_moved = sem("row_moved")
        based = sem("based")
        scaled = sem("scaled")
        summed = sem("summed")
        message_made = sem("message_made")
        hot_chain = sem("hot_chain")
        basis_in_sem = sem("basis_in_sem")
        products = pair[1][:, :, 0:2 * D].rearrange("p q (b d) -> p q b d", b=2)
        sums = pair[2][:, :, 0:2 * D].rearrange("p q (b d) -> p q b d", b=2)
        type_col = key_rel[:, 0, 0:ETILES]

        def each_tile(eng, stage, tiles, lag):
            for j in range(RING):
                stage(0, j)
            with eng.Fori(1, tiles // RING) as i:
                for j in range(RING):
                    stage(i, j)
            for j in range(lag):
                stage(tiles // RING, j)

        def tile_before(i, j):
            return (i, j - 1) if j else (i - 1, RING - 1)

        with nc.Block() as block:

            @block.sync
            def _(sp):
                sp.dma_start(basis[:, :].rearrange("i (b o) -> i b o", b=BASES),
                             basis_in.rearrange("b i o -> i b o")).then_inc(basis_in_sem, 16)
                for c, source in enumerate((bias0_in, gamma_in, beta_in)):
                    sp.dma_start(column[:, c:c + 1], source.rearrange("(p o) -> p o", o=1)).then_inc(basis_in_sem, 16)

            @block.gpsimd
            def _(pool):
                def data_free(i, j):
                    if j == 0:
                        wait(pool, data_moved, i * 2 - 1)
                    if j == SET:
                        wait(pool, data_moved, i * 2)

                def data_landed(i, j):
                    if j % SET == SET - 1:
                        pool.tensor_copy(edge_data[:, bass.ds(i * RING + (j - SET + 1), SET), :],
                                         ring[:, j - SET + 1:j + 1, 0:8]).then_inc(data_moved, 1)

                gather_rounds(pool, ETILES // RING, payload_rows,
                              lambda i, s: at_edge[:, bass.ds(i * RING + s * SET, SET)],
                              lambda j: ring[:, j, 0:8], data_free, data_arrived, ETILES // RING, data_landed)
                pool.wait_ge(data_moved, 2 * ETILES // RING)

                def rows_free(i, j):
                    wait(pool, row_turned, i * RING + (j - RING + 1))

                gather_rounds(pool, ETILES // RING, x_in,
                              lambda i, s: ints(edge_data[:, bass.ds(i * RING + s * SET, SET), 0]),
                              lambda j: ring[:, j, 0:D], rows_free, rows_arrived, 2 * ETILES // RING)

            @block.tensor
            def _(pe):
                pe.wait_ge(basis_in_sem, 64)

                def stage(i, j):
                    if not isinstance(i, int) or i < ETILES // RING:
                        pe.wait_ge(rows_arrived, i * RING + (j + 1))
                        wait(pe, row_moved, i * RING + (j - 1))
                        pe.transpose(bank[j % 2][:, 0:P], ring[:, j, 0:D], ident[:, :]).then_inc(row_turned, 1)
                    if isinstance(i, int) and (i, j) == (0, 0):
                        return
                    q = (j - 1) % 2
                    pe.wait_ge(row_moved, i * RING + j)
                    wait(pe, summed, i * RING + (j - 2))
                    pe.matmul(bank[2 + q][:, :], lhsT=pair[0][:, q, 0:P], rhs=basis[:, :], start=True,
                              stop=True).then_inc(based, 1)

                each_tile(pe, stage, ETILES, 1)

            @block.scalar
            def _(act):
                def stage(i, j):
                    if not isinstance(i, int) or i < ETILES // RING:
                        act.wait_ge(row_turned, i * RING + (j + 1))
                        wait(act, based, i * RING + (j - 1))
                        act.activation(pair[0][:, j % 2, 0:P], bank[j % 2][:, 0:P], ACT.Copy).then_inc(row_moved, 1)
                    if isinstance(i, int) and (i, j) == (0, 0):
                        return
                    ib, jb = tile_before(i, j)
                    act.wait_ge(based, i * RING + j)
                    wait(act, summed, i * RING + (j - 2))
                    for b in range(2):
                        last = act.activation(products[:, jb % 2, b, :], bank[2 + jb % 2][:, b * D:(b + 1) * D], ACT.Copy,
                                              scale=edge_data[:, bass.ds(ib * RING + jb, 1), 2 + b])
                    last.then_inc(scaled, 1)

                act.wait_ge(data_moved, 2 * ETILES // RING)
                each_tile(act, stage, ETILES, 1)

            @block.vector
            def _(dve):
                dve.wait_ge(data_moved, 2 * ETILES // RING)
                dve.tensor_scalar(type_col, ints(edge_data[:, :, 1]), 0.0, float(TYPES - 1), ALU.max,
                                  ALU.min).then_inc(hot_chain, 1)
                dve.wait_ge(hot_chain, 1)
                for t in range(TYPES):
                    dve.tensor_scalar(messages[:, :, D + t], type_col, float(t), None, ALU.is_equal)

                def stage(i, j):
                    q = j % 2
                    dve.wait_ge(scaled, i * RING + (j + 1))
                    wait(dve, message_made, i * RING + (j - 1))
                    for b in range(2):
                        last = dve.scalar_tensor_tensor(
                            sums[:, q, b, :], bank[2 + q][:, (2 + b) * D:(3 + b) * D],
                            edge_data[:, bass.ds(i * RING + j, 1), 4 + b], products[:, q, b, :], ALU.mult, ALU.add)
                    last.then_inc(summed, 1)
                    dve.wait_ge(summed, i * RING + (j + 1))
                    dve.tensor_tensor(messages[:, bass.ds(i * RING + j, 1), 0:D], sums[:, q, 0:1, :],
                                      sums[:, q, 1:2, :], ALU.add).then_inc(message_made, 1)

                each_tile(dve, stage, ETILES, 0)

        keys_made = sem("keys_made")
        pairs_built = sem("pairs_built")
        pairs_used = sem("pairs_used")
        sums_moved = sem("sums_moved")

        class Segments:

            def __init__(self, passes, keys, table, span, source, target, banks=2, arrived=None):
                self.passes = passes
                self.keys, self.table, self.span, self.source = keys, table, span, source
                self.count = keys.shape[1]
                self.target = target
                self.banks = banks
                self.arrived = arrived
                self.passed = sem(f"tiles_passed{passes}") if arrived is not None else None
                self.more_built = sem(f"more_built{passes}")
                self.more_used = sem(f"more_used{passes}")

            def wait_moved(self, eng, halves):
                if not isinstance(halves, int) or halves > 0:
                    eng.wait_ge(sums_moved, halves + self.passes * HALVES)

            def _wait_pair(self, eng, signal, n):
                if not isinstance(n, int) or n > 0:
                    eng.wait_ge(signal, n + self.passes * PAIRS)

            def entries(self, eng, registers, h):
                eng.load(registers, self.table[0:1, bass.ds(h.k * (2 * ENTRY), 2 * ENTRY + 1)])
                got = [eng.snap(r, min_val=0, max_val=self.count - 1) for r in registers]
                for n in (1, ENTRY + 1):
                    got[n] = eng.snap(registers[n], min_val=0, max_val=self.count - self.span)
                return got

            def tile_of(self, value):
                return nc.s_assert_within(
                    value, 0, self.count - 1,
                    skip_runtime_bounds_check_because="phase 1 makes the table with every first tile under the count")

            def build(self, dve, registers, h):
                v = h.u // 2
                if h.u % 2 == 0:
                    self._wait_pair(dve, pairs_built, h.i * 8 + (4 * v - 3))
                    dve.tensor_scalar(key_rel[:, v, 0:self.count], self.keys, block_base[:, bass.ds(h.i * 2 + v, 1)],
                                      None, ALU.subtract).then_inc(keys_made, 1)
                    dve.wait_ge(keys_made, h.i * 2 + (v + 1 + self.passes * BLOCKS))
                entry = self.entries(dve, registers, h)
                for j in range(2):
                    so_far, base, to_tile, _, so_far_next = entry[j * ENTRY:(j + 1) * ENTRY + 1]
                    start = (h.u % 2 * 4 + 2 * j) * P
                    nodes = iota[:, start:start + 2 * P]
                    self._wait_pair(dve, pairs_used, h.k * 2 + (j - 1))
                    dve.tensor_tensor(
                        selector[:, j, 0:self.span * 2 * P].rearrange("p (s n) -> p s n", s=self.span),
                        nodes.unsqueeze(1).to_broadcast([P, self.span, 2 * P]),
                        key_rel[:, v, bass.ds(base, self.span)].unsqueeze(2).to_broadcast([P, self.span, 2 * P]),
                        ALU.is_equal).then_inc(pairs_built, 1)
                    with dve.If(so_far < so_far_next):
                        with dve.Fori(so_far, so_far_next) as m:
                            e = self.tile_of(m + to_tile)
                            dve.wait_ge(self.more_used, m + 1)
                            dve.tensor_scalar(more_selector[:, :], nodes, key_rel[:, v, bass.ds(e, 1)], None,
                                              ALU.is_equal).then_inc(self.more_built, 1)
                return entry[2 * ENTRY]

            def wait_sums(self, eng, h, more):
                self._wait_pair(eng, pairs_used, h.k * 2 + 2)
                eng.wait_ge(self.more_used, more + 1)

            def start(self, pe):
                pe.sem_inc(self.more_used, 1)

            def add_up(self, pe, registers, h):
                entry = self.entries(pe, registers, h)
                self.wait_moved(pe, h.k - 1)
                for j in range(2):
                    so_far, base, to_tile, _, so_far_next = entry[j * ENTRY:(j + 1) * ENTRY + 1]
                    self._wait_pair(pe, pairs_built, h.k * 2 + (j + 1))
                    if self.arrived is not None:
                        pe.wait_ge(self.arrived, base + self.span)
                    for s in range(self.span):
                        for t in range(2):
                            n = (2 * s + t) * P
                            last = pe.matmul(self.target(h.u % 2, 2 * j + t), lhsT=selector[:, j, n:n + P],
                                             rhs=self.source(base + s), start=s + t == 0 and j < self.banks, stop=False,
                                             skip_group_check=True)
                    last.then_inc(pairs_used, 1)
                    with pe.If(so_far < so_far_next):
                        with pe.Fori(so_far, so_far_next) as m:
                            e = self.tile_of(m + to_tile)
                            pe.wait_ge(self.more_built, m + 1)
                            if self.arrived is not None:
                                pe.wait_ge(self.arrived, e + 1)
                            for t in range(2):
                                last = pe.matmul(self.target(h.u % 2, 2 * j + t), lhsT=more_selector[:, t * P:(t + 1) * P],
                                                 rhs=self.source(e), start=False, stop=False,
                                                 skip_group_check=True)
                                if t == 0 and self.arrived is not None:
                                    last.then_inc(self.passed, 1)
                            last.then_inc(self.more_used, 1)
                if self.arrived is not None:
                    self.wait_sums(pe, h, entry[2 * ENTRY])
                    advance = entry[3] + entry[ENTRY + 3]
                    with pe.If(advance > 0):
                        with pe.Fori(0, advance):
                            pe.sem_inc(self.passed, 1)

        def rows_of_block(rows, b, partitions=P):
            if isinstance(b, int):
                return rows[b * BLOCK:b * BLOCK + partitions * G, :].rearrange("(p g) d -> p (g d)", g=G)
            return rows[bass.ds(b * BLOCK, BLOCK), :].rearrange("(p g) d -> p (g d)", g=G)

        def block_view(buffer, v):
            return buffer[:, 2 * v:2 * v + 2, :].rearrange("p h d -> p (h d)")

        def tail_of(h):
            return TAIL if isinstance(h.i, int) and h.k // 2 == BLOCKS - 1 else P

        y_made = sem("y_made")
        stats_made = sem("stats_made")
        stats_seen = sem("stats_seen")
        means_made = sem("means_made")
        rooted = sem("rooted")
        inverted = sem("inverted")
        factors_made = sem("factors_made")
        act_done = sem("act_done")
        dve_done = sem("dve_done")

        class Norm:

            def __init__(self, passes, rows, product_made):
                self.passes = passes
                self.rows, self.product_made = rows, product_made
                self.stored = [sem(f"norm{passes}_stored{v}") for v in range(2)]

            def root(self, act, h):
                self.wait(act, means_made, h.k + 1)
                act.activation(root[:, h.u, :], mean_var[:, h.u, :, 1], ACT.Sqrt,
                               bias=eps_col[:, 0:1]).then_inc(rooted, 1)

            def _out_free(self, eng, h):
                wait(eng, self.stored[h.u // 2], h.i * 16)

            def on_act(self, act, h):
                self.wait(act, factors_made, h.k + 1)
                self._out_free(act, h)
                for t in range(2):
                    last = act.activation(ob[:, h.u, t * D:(t + 1) * D], yb[:, h.u, t * D:(t + 1) * D], ACT.Identity,
                                          scale=inverse[:, h.u, t:t + 1], bias=offset[:, h.u, t:t + 1])
                last.then_inc(act_done, 1)

            def wait(self, eng, signal, halves):
                if not isinstance(halves, int) or halves > 0:
                    eng.wait_ge(signal, halves + self.passes * HALVES)

            def on_vector(self, dve, b, c, product):
                if b.live():
                    self.wait(dve, act_done, b.k - 3)
                    self.wait(dve, dve_done, b.k - 3)
                    dve.wait_ge(self.product_made, b.k + 1)
                    dve.tensor_tensor(yb[:, b.u, :], product(b), xb[:, b.u, :], ALU.add).then_inc(y_made, 1)
                if c.live():
                    self.wait(dve, rooted, c.k + 1)
                    dve.reciprocal(inverse[:, c.u, :], root[:, c.u, :]).then_inc(inverted, 1)
                if b.live():
                    self.wait(dve, y_made, b.k + 1)
                    for t in range(4):
                        last = dve.bn_stats(out=tile_stats[:, b.u, t, :], in_=yb[:, b.u, t * D:(t + 1) * D])
                    last.then_inc(stats_made, 1)
                if c.live():
                    self.wait(dve, inverted, c.k + 1)
                    dve.scalar_tensor_tensor(offset[:, c.u, :], mean_var[:, c.u, :, 0], -1.0, inverse[:, c.u, :],
                                             ALU.mult, ALU.mult).then_inc(factors_made, 1)
                if b.live():
                    self.wait(dve, stats_made, b.k + 1)
                    dve.sem_inc(stats_seen, 1)
                    for t in range(4):
                        last = dve.bn_aggr(out=mean_var[:, b.u, t, :], in_=tile_stats[:, b.u, t, :])
                    last.then_inc(means_made, 1)
                if c.live():
                    self.wait(dve, factors_made, c.k + 1)
                    self._out_free(dve, c)
                    for t in range(2, 4):
                        last = dve.tensor_scalar(ob[:, c.u, t * D:(t + 1) * D], yb[:, c.u, t * D:(t + 1) * D],
                                                 inverse[:, c.u, t:t + 1], offset[:, c.u, t:t + 1], ALU.mult, ALU.add)
                    last.then_inc(dve_done, 1)

            def store(self, sp, h):
                v = h.u // 2
                self.wait(sp, act_done, h.k + 2)
                self.wait(sp, dve_done, h.k + 2)
                tail = P if self.rows.shape[0] == NPAD else tail_of(h)
                sp.dma_start(rows_of_block(self.rows, h.i * 2 + v, tail),
                             block_view(ob, v)[0:tail, :]).then_inc(self.stored[v], 16)

            def finish(self, sp):
                for v in range(2):
                    sp.wait_ge(self.stored[v], 16 * ((BLOCKS + 1 - v) // 2))

        seg0 = Segments(0, key_dst[:, :], pairs_dst, SPAN,
                        lambda e: messages[:, bass.ds(e, 1), :].rearrange("p a f -> p (a f)"),
                        lambda half, t: wide[half][:, t, 0:MSG])
        x0_in = [sem(f"x0_in{v}") for v in range(2)]
        ht_stored = [sem(f"ht_stored{u}") for u in range(4)]
        x0_turned = sem("x0_turned")
        sum_turned = sem("sum_turned")
        relu_made = sem("relu_made")
        ht_made = sem("ht_made")
        moments_made = sem("moments_made")

        first_registers = {}

        with nc.Block() as block:

            @block.sync
            def _(sp):
                def stage(h):
                    v = h.u // 2
                    if h.u % 2 == 0 and h.live():
                        wait(sp, x0_turned, h.k - 2)
                        tail = tail_of(h)
                        sp.dma_start(block_view(xb, v)[0:tail, :],
                                     rows_of_block(x_in, h.i * 2 + v, tail)).then_inc(x0_in[v], 16)
                    b = h.minus(3)
                    if b.live():
                        sp.wait_ge(ht_made, b.k + 1)
                        sp.dma_start(ht_halves[b.k] if isinstance(b.k, int) else
                                     ht_halves[bass.ds(b.k, 1), :, :].rearrange("o p c -> (o p) c"),
                                     yb[:, b.u, :]).then_inc(ht_stored[b.u], 16)

                each_half(sp, stage, 3)
                for u in range(4):
                    sp.wait_ge(ht_stored[u], 16 * len(range(u, HALVES, 4)))

            @block.tensor
            def _(pe):
                registers = first_registers["pe"] = [pe.alloc_register(f"pe_first{n}") for n in range(2 * ENTRY + 1)]
                seg0.start(pe)

                def stage(h):
                    par = h.u % 2
                    if h.live():
                        seg0.add_up(pe, registers, h)
                        pe.wait_ge(x0_in[h.u // 2], h.landed())
                        wait(pe, ht_made, h.k - 1)
                        for t in range(4):
                            last = pe.transpose(bank[par][:, t * P:(t + 1) * P], xb[:, h.u, t * D:(t + 1) * D],
                                                ident[:, :])
                        last.then_inc(x0_turned, 1)
                    b = h.minus(1)
                    if b.live():
                        seg0.wait_moved(pe, b.k + 1)
                        wait(pe, relu_made, b.k - 1)
                        for t in range(4):
                            last = pe.transpose(bank[2 + b.u % 2][:, t * P:(t + 1) * P],
                                                pair[0][:, b.u % 2, t * D:(t + 1) * D], ident[:, :])
                        last.then_inc(sum_turned, 1)

                each_half(pe, stage, 1)

            @block.scalar
            def _(act):
                def stage(h):
                    par = h.u % 2
                    if h.live():
                        act.wait_ge(x0_turned, h.k + 1)
                        wait(act, sum_turned, h.k - 1)
                        act.activation(pair[0][:, par, :].rearrange("p (t d) -> p t d", d=D), wide[par][:, :, 0:D],
                                       ACT.Copy)
                        act.activation(type_counts[:, bass.ds(h.k * 4, 4), :], wide[par][:, :, D:MSG],
                                       ACT.Copy).then_inc(sums_moved, 1)
                    b = h.minus(1)
                    if b.live():
                        act.wait_ge(sum_turned, b.k + 1)
                        wait(act, ht_made, b.k - 1)
                        act.activation(pair[1][:, b.u % 2, :], bank[2 + b.u % 2][:, :], ACT.Relu,
                                       bias=column[:, 0:1]).then_inc(relu_made, 1)

                each_half(act, stage, 1)

            @block.vector
            def _(dve):
                registers = first_registers["dve"] = [dve.alloc_register(f"dve_first{n}") for n in range(2 * ENTRY + 1)]

                def stage(h):
                    if h.live():
                        seg0.build(dve, registers, h)
                    b = h.minus(2)
                    if b.live():
                        dve.wait_ge(relu_made, b.k + 1)
                        wait(dve, ht_stored[b.u], b.i * 16)
                        wait(dve, moments_made, b.k - 3)
                        dve.tensor_tensor(yb[:, b.u, :], bank[b.u % 2][:, :], pair[1][:, b.u % 2, :],
                                          ALU.add).then_inc(ht_made, 1)
                        dve.wait_ge(ht_made, b.k + 1)
                        if tail_of(b) < P:
                            for t in range(4):
                                last = dve.bn_stats(out=moments[:, HALVES - 2 + b.u * 4 + t, :],
                                                    in_=yb[:, b.u, t * P:t * P + TAIL])
                            last.then_inc(moments_made, 1)
                        else:
                            dve.bn_stats(out=moments[:, bass.ds(b.k, 1), :].rearrange("p a s -> p (a s)"),
                                         in_=yb[:, b.u, :]).then_inc(moments_made, 1)

                each_half(dve, stage, 2)

        def load_half(sp, rows, h, signal):
            first = (h.k - h.u % 2) // 2 if isinstance(h.k, int) else h.i * 2 + h.u // 2
            valid = P if rows.shape[0] == NPAD else tail_of(h)
            block_rows = rows_of_block(rows, first, valid)
            part_of = slice(h.u % 2 * 4 * D, (h.u % 2 + 1) * 4 * D)
            sp.dma_start(xb[0:valid, h.u, :], block_rows[:, part_of]).then_inc(signal[h.u], 16)

        norm_scale, norm_offset = column[:, 8:9], column[:, 9:10]
        moments_added = sem("moments_added")
        spread_made = sem("spread_made")
        batch_chain = sem("batch_chain")

        with nc.Block() as block:

            @block.vector
            def _(dve):
                mean, variance = mean_var[:, 0, 0, 0:1], mean_var[:, 0, 0, 1:2]
                dve.bn_aggr(out=mean_var[:, 0, 0, :], in_=moments[:, :, :]).then_inc(moments_added, 1)
                dve.wait_ge(spread_made, 1)
                dve.reciprocal(inverse[:, 0, 0:1], root[:, 0, 0:1]).then_inc(batch_chain, 1)
                dve.wait_ge(batch_chain, 1)
                dve.tensor_tensor(norm_scale, inverse[:, 0, 0:1], column[:, 1:2], ALU.mult).then_inc(batch_chain, 1)
                dve.wait_ge(batch_chain, 2)
                dve.tensor_tensor(offset[:, 0, 0:1], mean, norm_scale, ALU.mult).then_inc(batch_chain, 1)
                dve.wait_ge(batch_chain, 3)
                dve.tensor_tensor(norm_offset, column[:, 2:3], offset[:, 0, 0:1], ALU.subtract)

            @block.scalar
            def _(act):
                act.wait_ge(moments_added, 1)
                act.activation(root[:, 0, 0:1], mean_var[:, 0, 0, 1:2], ACT.Sqrt,
                               bias=eps_col[:, 0:1]).then_inc(spread_made, 1)

        x0_back = [sem(f"x0_back{u}") for u in range(4)]
        ht_back = [sem(f"ht_back{u}") for u in range(4)]
        batch_done = sem("batch_done")
        h_turned = sem("h_turned")
        norm1 = Norm(0, x1_rows, h_turned)
        ht_slot = [pair[1 + u // 2][:, u % 2, :] for u in range(4)]

        with nc.Block() as block:

            @block.sync
            def _(sp):
                def stage(h):
                    if h.live():
                        wait(sp, batch_done, h.k - 3)
                        sp.dma_start(ht_slot[h.u], ht_halves[h.k] if isinstance(h.k, int) else
                                     ht_halves[bass.ds(h.k, 1), :, :].rearrange("o p c -> (o p) c")).then_inc(
                                         ht_back[h.u], 16)
                        norm1.wait(sp, y_made, h.k - 3)
                        load_half(sp, x_in, h, x0_back)
                    if h.u % 2 == 0:
                        b = h.minus(6)
                        if b.live():
                            norm1.store(sp, b)

                each_half(sp, stage, 6)
                norm1.finish(sp)

            @block.scalar
            def _(act):
                def stage(h):
                    if h.live():
                        act.wait_ge(ht_back[h.u], h.landed())
                        wait(act, h_turned, h.k - 1)
                        act.activation(pair[0][:, h.u % 2, :], ht_slot[h.u], ACT.Relu, scale=norm_scale,
                                       bias=norm_offset).then_inc(batch_done, 1)
                    b = h.minus(2)
                    if b.live():
                        norm1.root(act, b)
                    c = h.minus(3)
                    if c.live():
                        norm1.on_act(act, c)

                each_half(act, stage, 3)

            @block.tensor
            def _(pe):
                def stage(h):
                    pe.wait_ge(batch_done, h.k + 1)
                    norm1.wait(pe, y_made, h.k - 3)
                    for t in range(4):
                        last = pe.transpose(bank[h.u][:, t * P:(t + 1) * P], pair[0][:, h.u % 2, t * P:(t + 1) * P],
                                            ident[:, :])
                    last.then_inc(h_turned, 1)

                each_half(pe, stage, 0)

            @block.vector
            def _(dve):
                def stage(h):
                    b = h.minus(1)
                    if b.live():
                        dve.wait_ge(x0_back[b.u], b.landed())
                    norm1.on_vector(dve, b, h.minus(3), lambda h: bank[h.u][:, :])

                each_half(dve, stage, 3)

        SPLIT_ROWS = 3
        w_neigh, at = part(0, D)
        w_self, at = part(at, D)
        row_wide, at = part(at, 4 * D)
        row_rest, at = part(at, 4 * D)
        row_part, at = part(at, 3, 2 * D)
        row_pick, at = part(at, 4 * D)
        row_split, at = part(at, 2 * D)
        row_ones, at = part(at, P // 2)
        bias_wide, bias_rest, bias_pick = (x[0:SPLIT_ROWS, :] for x in (row_wide, row_rest, row_pick))
        bias_part = row_part[0:SPLIT_ROWS, :, :].bitcast(BF16)
        bias_split = row_split[0:SPLIT_ROWS, :].bitcast(BF16)
        ones_split = row_ones[0:SPLIT_ROWS, :].bitcast(BF16)
        degree = sb("degree", [P, 2, 4])
        share = sb("share", [P, 2, 4])

        def split_rows(dve, chain, counted):
            def then_wait(instruction):
                instruction.then_inc(chain, 1)
                counted[0] += 1
                dve.wait_ge(chain, counted[0])

            then_wait(dve.tensor_copy(bias_part[:, 0, :], bias_wide[:, :]))
            then_wait(dve.tensor_tensor(bias_rest[:, :], bias_wide[:, :], bias_part[:, 0, :], ALU.subtract))
            then_wait(dve.tensor_copy(bias_part[:, 1, :], bias_rest[:, :]))
            then_wait(dve.tensor_tensor(bias_rest[:, :], bias_rest[:, :], bias_part[:, 1, :], ALU.subtract))
            then_wait(dve.tensor_copy(bias_part[:, 2, :], bias_rest[:, :]))
            then_wait(dve.tensor_scalar(bias_pick[:, :], bias_part[:, 0, :], ident[0:3, 0:1], None, ALU.mult))
            then_wait(dve.scalar_tensor_tensor(bias_pick[:, :], bias_part[:, 1, :], ident[0:3, 1:2], bias_pick[:, :],
                                               ALU.mult, ALU.add))
            then_wait(dve.scalar_tensor_tensor(bias_split[:, :], bias_part[:, 2, :], ident[0:3, 2:3], bias_pick[:, :],
                                               ALU.mult, ALU.add))

        weights1_in = sem("weights1_in")
        split1_chain = sem("split1_chain")

        with nc.Block() as block:

            @block.sync
            def _(sp):
                sp.dma_start(w_neigh[:, :], wneigh_in).then_inc(weights1_in, 16)
                sp.dma_start(w_self[:, :], wself_in).then_inc(weights1_in, 16)
                for t in range(4):
                    for r in range(SPLIT_ROWS):
                        sp.dma_start(bias_wide[r:r + 1, t * D:(t + 1) * D],
                                     b1_in.rearrange("(o d) -> o d", o=1)).then_inc(weights1_in, 16)
                sp.wait_ge(weights1_in, 14 * 16)

            @block.vector
            def _(dve):
                dve.wait_ge(weights1_in, 14 * 16)
                dve.memset(ones_split[:, :], 1.0)
                split_rows(dve, split1_chain, [0])

        rows1_arrived = sem("rows1_arrived")
        seg1 = Segments(1, key_all[:, :], pairs_all, SPAN_ALL,
                        lambda e: ring[:, bass.ds(e % RING, 1), :].rearrange("p a f -> p (a f)"),
                        lambda half, t: wide[half][:, t, 0:XROW], arrived=rows1_arrived)
        x1_back = [sem(f"x1_back{u}") for u in range(4)]
        degree_made = sem("degree_made")
        share_made = sem("share_made")
        mean_turned = sem("mean_turned")
        mean_moved = sem("mean_moved")
        x1_turned = sem("x1_turned")
        x1_moved = sem("x1_moved")
        update_made = sem("update_made")
        norm2 = Norm(1, x2_rows, update_made)

        with nc.Block() as block:

            @block.gpsimd
            def _(pool):
                def rows_free(i, j):
                    wait(pool, seg1.passed, i * RING + (j - RING + 1))

                gather_rounds(pool, MCOLS // RING, x1_rows,
                              lambda i, s: at_all[:, bass.ds(i * RING + s * SET, SET)],
                              lambda j: ring[:, j, 0:D], rows_free, rows1_arrived, 3 * ETILES // RING)

            @block.sync
            def _(sp):
                def stage(h):
                    if h.live():
                        norm2.wait(sp, y_made, h.k - 3)
                        load_half(sp, x1_rows, h, x1_back)
                    b = h.minus(6)
                    if h.u % 2 == 0 and b.live():
                        norm2.store(sp, b)

                each_half(sp, stage, 6)
                norm2.finish(sp)

            @block.tensor
            def _(pe):
                registers = first_registers["pe"]
                seg1.start(pe)

                def stage(h):
                    par = h.u % 2
                    if h.live():
                        seg1.add_up(pe, registers, h)
                        pe.wait_ge(x1_back[h.u], h.landed())
                        wait(pe, x1_moved, h.k)
                        for t in range(4):
                            last = pe.transpose(bank[0][:, t * P:(t + 1) * P], xb[:, h.u, t * D:(t + 1) * D],
                                                ident[:, :])
                        last.then_inc(x1_turned, 1)
                    b = h.minus(1)
                    if b.live():
                        seg1.wait_moved(pe, b.k + 1)
                        wait(pe, mean_moved, b.k)
                        for t in range(4):
                            last = pe.transpose(bank[1][:, t * P:(t + 1) * P],
                                                pair[0][:, b.u % 2, t * D:(t + 1) * D], ident[:, :])
                        last.then_inc(mean_turned, 1)
                    c = h.minus(2)
                    if c.live():
                        q = c.u % 2
                        norm2.wait(pe, y_made, c.k - 1)
                        pe.matmul(bank[2 + q][:, :], lhsT=ones_split[:, :], rhs=bias_split[:, :], start=True,
                                  stop=False, skip_group_check=True)
                        pe.wait_ge(x1_moved, c.k + 1)
                        for t in range(4):
                            pe.matmul(bank[2 + q][:, t * D:(t + 1) * D], lhsT=pair[2][:, q, t * P:(t + 1) * P],
                                      rhs=w_self[:, :], start=False, stop=False, skip_group_check=True)
                        pe.wait_ge(mean_moved, c.k + 1)
                        for t in range(4):
                            last = pe.matmul(bank[2 + q][:, t * D:(t + 1) * D], lhsT=pair[1][:, q, t * P:(t + 1) * P],
                                             rhs=w_neigh[:, :], start=False, stop=t == 3, skip_group_check=True)
                        last.then_inc(update_made, 1)

                each_half(pe, stage, 2)

            @block.scalar
            def _(act):
                def stage(h):
                    par = h.u % 2
                    if h.live():
                        act.wait_ge(share_made, h.k + 1)
                        wait(act, mean_turned, h.k - 1)
                        for t in range(4):
                            last = act.activation(pair[0][:, par, t * D:(t + 1) * D], wide[par][:, t, 0:D], ACT.Copy,
                                                  scale=share[:, par, t:t + 1])
                        last.then_inc(sums_moved, 1)
                        wait(act, update_made, h.k - 1)
                        act.wait_ge(x1_turned, h.k + 1)
                        act.activation(pair[2][:, par, :], bank[0][:, :], ACT.Copy).then_inc(x1_moved, 1)
                    b = h.minus(1)
                    if b.live():
                        act.wait_ge(mean_turned, b.k + 1)
                        wait(act, update_made, b.k - 1)
                        act.activation(pair[1][:, b.u % 2, :], bank[1][:, :], ACT.Copy).then_inc(mean_moved, 1)
                    c = h.minus(3)
                    if c.live():
                        norm2.root(act, c)
                    d = h.minus(4)
                    if d.live():
                        norm2.on_act(act, d)

                each_half(act, stage, 4)

            @block.vector
            def _(dve):
                registers = first_registers["dve"]

                def stage(h):
                    par = h.u % 2
                    if h.live():
                        seg1.build(dve, registers, h)
                    norm2.on_vector(dve, h.minus(3), h.minus(4), lambda h: bank[2 + h.u % 2][:, :])
                    if h.live():
                        dve.wait_ge(x1_turned, h.k + 1)
                        seg1.wait_moved(dve, h.k - 1)
                        dve.tensor_scalar(degree[:, par, :], wide[par][:, :, D], 1.0, None,
                                          ALU.max).then_inc(degree_made, 1)
                        dve.wait_ge(degree_made, h.k + 1)
                        dve.reciprocal(share[:, par, :], degree[:, par, :]).then_inc(share_made, 1)

                each_half(dve, stage, 4)

        w_rows, at = part(0, 7, D)
        w_turned, at = part(at, 7, D)
        W_MSG, W_I, W_H = 0, 1, 4
        RESET, UPDATE, NEW = 0, 1, 2
        type_rows, at = part(at, D)
        msg_bias, at = part(at, D)
        gate_bias, at = part(at, 6)
        x_t, at = part(at, 4, 512)
        counts_t, at = part(at, 2, 512)
        counts_now, at = part(at, 2 * 4 * TYPES)
        counts_now = counts_now.rearrange("p (n t c) -> p n t c", n=2, t=4)
        agg_t, at = part(at, 2, 512)
        msg_t, at = part(at, 2, 512)
        reset_t, at = part(at, 2, 512)
        update_t, at = part(at, 2, 512)
        before_tanh, at = part(at, 2, 512)
        new_t, at = part(at, 2, 512)
        h_t, at = part(at, 2, 512)
        between, at = part(at, 4, 512)
        between = between.rearrange("p (a b) c -> p a b c", a=2)
        reset_bias, update_bias = column[:, 3:4], column[:, 4:5]
        new_i_bias, new_h_bias = gate_bias[:, 2:3], gate_bias[:, 5:6]
        wide_bank = [wide[n][:, 2 * m:2 * m + 2, :].rearrange("p a b -> p (a b)") for n in range(2) for m in range(2)]
        sum_banks = [wide_bank[0], wide_bank[2]]
        bank_sums_t, bank_x_t, bank_reset, bank_update = bank
        bank_new_i, bank_new_h = wide_bank[1], wide_bank[3]

        weights2_in = sem("weights2_in")
        weights2_turned = sem("weights2_turned")

        with nc.Block() as block:

            @block.sync
            def _(sp):
                sp.dma_start(w_rows[:, W_MSG, :], wmsg_in).then_inc(weights2_in, 16)
                sp.dma_start(w_rows[:, W_I:W_I + 3, :], wih_in.rearrange("(g o) i -> o g i", g=3)).then_inc(weights2_in, 16)
                sp.dma_start(w_rows[:, W_H:W_H + 3, :], whh_in.rearrange("(g o) i -> o g i", g=3)).then_inc(weights2_in, 16)
                sp.dma_start(type_rows[0:TYPES, :], emb_in).then_inc(weights2_in, 16)
                for t in range(TYPES):
                    sp.dma_start(msg_bias[t:t + 1, :], bmsg_in.rearrange("(o d) -> o d", o=1)).then_inc(weights2_in, 16)
                for g in range(3):
                    for n, source in enumerate((bih_in, bhh_in)):
                        sp.dma_start(gate_bias[:, 3 * n + g:3 * n + g + 1],
                                     source[g * D:(g + 1) * D].rearrange("(p o) -> p o", o=1)).then_inc(weights2_in, 16)

            @block.tensor
            def _(pe):
                pe.wait_ge(weights2_in, 19 * 16)
                for w in range(7):
                    last = pe.transpose(bank[w // 4][:, w % 4 * D:(w % 4 + 1) * D], w_rows[:, w, :], ident[:, :])
                last.then_inc(weights2_turned, 1)

            @block.scalar
            def _(act):
                act.wait_ge(weights2_turned, 1)
                for b, count in enumerate((4, 3)):
                    act.activation(w_turned[:, 4 * b:4 * b + count, :].rearrange("p w o -> p (w o)"),
                                   bank[b][:, 0:count * D], ACT.Copy)

            @block.vector
            def _(dve):
                dve.wait_ge(weights2_in, 19 * 16)
                dve.tensor_tensor(type_rows[0:TYPES, :], type_rows[0:TYPES, :], msg_bias[0:TYPES, :], ALU.add)
                dve.tensor_tensor(reset_bias, gate_bias[:, 0:1], gate_bias[:, 3:4], ALU.add)
                dve.tensor_tensor(update_bias, gate_bias[:, 1:2], gate_bias[:, 4:5], ALU.add)

        rows2_arrived = sem("rows2_arrived")
        seg2 = Segments(2, key_dst[:, :], pairs_dst, SPAN,
                        lambda e: ring[:, bass.ds(e % RING, 1), 0:D].rearrange("p a f -> p (a f)"),
                        lambda half, t: sum_banks[half][:, t * D:(t + 1) * D], banks=1, arrived=rows2_arrived)
        x2_back = [sem(f"x2_back{u}") for u in range(4)]
        x2_turned = sem("x2_turned")
        x2_moved = sem("x2_moved")
        counts_copied = sem("counts_copied")
        counts_turned = sem("counts_turned")
        counts_moved = sem("counts_moved")
        agg2_turned = sem("agg2_turned")
        agg2_moved = sem("agg2_moved")
        msgs_made = sem("msgs_made")
        msgs_moved = sem("msgs_moved")
        gates_made = sem("gates_made")
        reset_made = sem("reset_made")
        update_gate_made = sem("update_gate_made")
        new_h_used = sem("new_h_used")
        tanh_ready = sem("tanh_ready")
        new_made = sem("new_made")
        gru_chain = sem("gru_chain")
        h_made = sem("h_made")
        h_back = sem("h_back")
        norm3 = Norm(2, x3_rows, h_back)

        with nc.Block() as block:

            @block.gpsimd
            def _(pool):
                def rows_free(i, j):
                    wait(pool, seg2.passed, i * RING + (j - RING + 1))

                gather_rounds(pool, ETILES // RING, x2_rows,
                              lambda i, s: ints(edge_data[:, bass.ds(i * RING + s * SET, SET), 0]),
                              lambda j: ring[:, j, 0:D], rows_free, rows2_arrived,
                              (3 * ETILES + MCOLS) // RING)

            @block.sync
            def _(sp):
                def stage(h):
                    if h.live():
                        norm3.wait(sp, y_made, h.k - 3)
                        load_half(sp, x2_rows, h, x2_back)
                    b = h.minus(6)
                    if h.u % 2 == 0 and b.live():
                        norm3.store(sp, b)

                each_half(sp, stage, 6)
                norm3.finish(sp)

            @block.tensor
            def _(pe):
                registers = first_registers["pe"]
                seg2.start(pe)

                def stage(h):
                    b, c = h.minus(1), h.minus(2)
                    q = b.u % 2
                    if h.live():
                        seg2.add_up(pe, registers, h)
                        pe.wait_ge(x2_back[h.u], h.landed())
                        norm3.wait(pe, y_made, h.k - 2)
                        wait(pe, x2_moved, h.k)
                        for t in range(4):
                            last = pe.transpose(bank_x_t[:, t * P:(t + 1) * P], xb[:, h.u, t * D:(t + 1) * D], ident[:, :])
                        last.then_inc(x2_turned, 1)
                    if b.live():
                        seg2.wait_moved(pe, b.k + 1)
                        wait(pe, msgs_moved, b.k)
                        for t in range(4):
                            last = pe.transpose(bank_sums_t[:, t * P:(t + 1) * P],
                                                pair[0][:, q, t * D:(t + 1) * D], ident[:, :])
                        last.then_inc(agg2_turned, 1)
                        pe.wait_ge(x2_moved, b.k + 1)
                        wait(pe, reset_made, b.k)
                        pe.matmul(bank_reset[:, :], lhsT=w_turned[:, W_H + RESET, :], rhs=x_t[:, b.u, :], start=True,
                                  stop=False, skip_group_check=True)
                        wait(pe, update_gate_made, b.k)
                        pe.matmul(bank_update[:, :], lhsT=w_turned[:, W_H + UPDATE, :], rhs=x_t[:, b.u, :], start=True,
                                  stop=False, skip_group_check=True)
                        wait(pe, new_h_used, b.k)
                        pe.matmul(bank_new_h, lhsT=w_turned[:, W_H + NEW, :], rhs=x_t[:, b.u, :], start=True,
                                  stop=True, skip_group_check=True)
                    if h.live():
                        pe.wait_ge(counts_copied, h.k + 1)
                        wait(pe, tanh_ready, h.k - 1)
                        wait(pe, counts_moved, h.k)
                        for t in range(4):
                            last = pe.transpose(
                                bank_new_i[0:TYPES, t * P:(t + 1) * P], counts_now[:, h.u % 2, t, :], ident[:, :])
                        last.then_inc(counts_turned, 1)
                    if b.live():
                        pe.wait_ge(agg2_moved, b.k + 1)
                        pe.matmul(bank_sums_t[:, :], lhsT=w_turned[:, W_MSG, :], rhs=agg_t[:, q, :], start=True,
                                  stop=False, skip_group_check=True)
                        pe.wait_ge(counts_moved, b.k + 1)
                        pe.matmul(bank_sums_t[:, :], lhsT=type_rows[0:TYPES, :], rhs=counts_t[0:TYPES, q, :],
                                  start=False, stop=True, skip_group_check=True).then_inc(msgs_made, 1)
                    if c.live():
                        pe.wait_ge(h_made, c.k + 1)
                        norm3.wait(pe, y_made, c.k)
                        if h.live():
                            pe.wait_ge(x2_moved, h.k + 1)
                        for t in range(4):
                            last = pe.transpose(bank_x_t[:, t * D:(t + 1) * D], h_t[:, c.u % 2, t * P:(t + 1) * P],
                                                ident[:, :])
                        last.then_inc(h_back, 1)
                    if b.live():
                        pe.wait_ge(msgs_moved, b.k + 1)
                        pe.matmul(bank_reset[:, :], lhsT=w_turned[:, W_I + RESET, :], rhs=msg_t[:, q, :], start=False,
                                  stop=True, skip_group_check=True).then_inc(gates_made, 1)
                        wait(pe, tanh_ready, b.k)
                        if h.live():
                            pe.wait_ge(counts_moved, h.k + 1)
                        pe.matmul(bank_new_i, lhsT=w_turned[:, W_I + NEW, :], rhs=msg_t[:, q, :], start=True,
                                  stop=True, skip_group_check=True).then_inc(gates_made, 1)
                        pe.matmul(bank_update[:, :], lhsT=w_turned[:, W_I + UPDATE, :], rhs=msg_t[:, q, :], start=False,
                                  stop=True, skip_group_check=True).then_inc(gates_made, 1)

                each_half(pe, stage, 2)

            @block.scalar
            def _(act):
                def stage(h):
                    b, c = h.minus(1), h.minus(2)
                    q = b.u % 2
                    if c.live():
                        act.wait_ge(tanh_ready, c.k + 1)
                        wait(act, h_made, c.k - 1)
                        act.activation(new_t[:, c.u % 2, :], before_tanh[:, c.u % 2, :], ACT.Tanh,
                                       bias=new_i_bias).then_inc(new_made, 1)
                    if h.live():
                        act.wait_ge(x2_turned, h.k + 1)
                        wait(act, agg2_turned, h.k - 1)
                        act.activation(pair[0][:, h.u % 2, :], sum_banks[h.u % 2], ACT.Copy).then_inc(sums_moved, 1)
                        wait(act, h_made, h.k - 3)
                        act.activation(x_t[:, h.u, :], bank_x_t[:, :], ACT.Copy).then_inc(x2_moved, 1)
                    if b.live():
                        act.wait_ge(agg2_turned, b.k + 1)
                        wait(act, msgs_made, b.k - 1)
                        act.activation(agg_t[:, q, :], bank_sums_t[:, :], ACT.Copy).then_inc(agg2_moved, 1)
                    if h.live():
                        act.wait_ge(counts_turned, h.k + 1)
                        wait(act, msgs_made, h.k - 1)
                        act.activation(counts_t[0:TYPES, h.u % 2, :], bank_new_i[0:TYPES, :],
                                       ACT.Copy).then_inc(counts_moved, 1)
                    if b.live():
                        act.wait_ge(msgs_made, b.k + 1)
                        wait(act, gates_made, h.k * 3 - 6)
                        act.activation(msg_t[:, q, :], bank_sums_t[:, :], ACT.Copy).then_inc(msgs_moved, 1)
                    d, e = h.minus(3), h.minus(4)
                    if d.live():
                        norm3.root(act, d)
                    if e.live():
                        norm3.on_act(act, e)
                    if b.live():
                        act.wait_ge(gates_made, h.k * 3 - 2)
                        wait(act, new_h_used, b.k - 1)
                        act.activation(reset_t[:, q, :], bank_reset[:, :], ACT.Sigmoid,
                                       bias=reset_bias).then_inc(reset_made, 1)
                        act.wait_ge(gates_made, h.k * 3)
                        wait(act, h_made, b.k - 1)
                        act.activation(update_t[:, q, :], bank_update[:, :], ACT.Sigmoid,
                                       bias=update_bias).then_inc(update_gate_made, 1)

                each_half(act, stage, 4)

            @block.vector
            def _(dve):
                registers = first_registers["dve"]

                def stage(h):
                    if h.live():
                        wait(dve, counts_turned, h.k - 1)
                        dve.tensor_copy(counts_now[:, h.u % 2, :, :],
                                        type_counts[:, bass.ds(h.k * 4, 4), :]).then_inc(counts_copied, 1)
                        seg2.build(dve, registers, h)
                    norm3.on_vector(dve, h.minus(3), h.minus(4), lambda h: bank_x_t[:, :])
                    c = h.minus(2)
                    q = c.u % 2
                    if c.live():
                        dve.wait_ge(reset_made, c.k + 1)
                        wait(dve, new_made, c.k - 1)
                        dve.scalar_tensor_tensor(between[:, 0, q, :], bank_new_h, new_h_bias, reset_t[:, q, :],
                                                 ALU.add, ALU.mult).then_inc(new_h_used, 1)
                        dve.wait_ge(new_h_used, c.k + 1)
                        dve.wait_ge(update_gate_made, c.k + 1)
                        dve.tensor_tensor(before_tanh[:, q, :], bank_new_i, between[:, 0, q, :],
                                          ALU.add).then_inc(tanh_ready, 1)
                        dve.wait_ge(new_made, c.k + 1)
                        dve.tensor_tensor(between[:, 1, q, :], x_t[:, c.u, :], new_t[:, q, :],
                                          ALU.subtract).then_inc(gru_chain, 1)
                        dve.wait_ge(gru_chain, c.k * 2 + 1)
                        dve.tensor_tensor(between[:, 0, q, :], between[:, 1, q, :], update_t[:, q, :],
                                          ALU.mult).then_inc(gru_chain, 1)
                        dve.wait_ge(gru_chain, c.k * 2 + 2)
                        wait(dve, h_back, c.k - 1)
                        dve.tensor_tensor(h_t[:, q, :], between[:, 0, q, :], new_t[:, q, :], ALU.add).then_inc(h_made, 1)

                each_half(dve, stage, 4)

        pooled_rows = big[:, 0:ETILES * XROW].rearrange("p (e f) -> p e f", f=XROW)
        at = ETILES * XROW
        w_pool, at = part(at, D)
        bias_diag, at = part(at, 4 * D)
        attention, at = part(at, 2 * P)
        has_edges, at = part(at, 2, 5)
        has_edges_t, at = part(at, 2, P)
        assert at <= ETILES * MSG

        def pieces_of(buffer, *sizes):
            flat, start, pieces = buffer[:, :, :].rearrange("p a b -> p (a b)"), 0, []
            for size in sizes:
                pieces.append(flat[:, start:start + size])
                start += size
            assert start <= flat.shape[1]
            return pieces

        w_lin, w_out, w_out_t, b_lin, b_out_rows, bias_rows = pieces_of(pair[0], D, D, D, 5, D, D)
        gate_row, gate_all = pieces_of(pair[1], XROW, XROW)
        gate, gate_key = pieces_of(pair[2], 2 * P, 2 * P)
        gated = yb[:, :, :].rearrange("p a b -> p (a b)")[:, 0:SET * D].rearrange("p (s d) -> p s d", d=D)
        changes, links, whole, add_up_to, add_from, best_up_to, best_from = pieces_of(
            yb, 2 * (P + 1), 2 * P + 1, 2 * P, 2 * P, 2 * P, 2 * P, 2 * P)
        by_tile, up_to, from_on, highest, other_key, far_columns = pieces_of(ob, 4 * P, 2 * P, 2 * P, 2 * P, P, 4)
        tile_ends, far = pieces_of(xb, 4 * 2 * P, 2 * 2 * P)
        NEVER = -1e30

        def two(piece):
            return piece.rearrange("p (a b) -> p a b", a=2)

        weights3_in = sem("weights3_in")
        gate_spread = sem("gate_spread")
        gate_all_made = sem("gate_all_made")
        w_out_turned = sem("w_out_turned")
        w_out_moved = sem("w_out_moved")
        pool_made = sem("pool_made")
        rows3_arrived = sem("rows3_arrived")
        gate_products = sem("gate_products")
        rows3_kept = sem("rows3_kept")
        gates_added = sem("gates_added")
        pool3_chain = sem("pool3_chain")
        max_ready = sem("max_ready")
        max_turned = sem("max_turned")
        max_moved = sem("max_moved")
        max_chain = sem("max_chain")

        with nc.Block() as block:

            @block.sync
            def _(sp):
                sp.dma_start(w_lin, wlin_in).then_inc(weights3_in, 16)
                sp.dma_start(w_out, wout_in).then_inc(weights3_in, 16)
                for r in range(5):
                    sp.dma_start(b_lin[:, r:r + 1], blin_in.rearrange("(p o) -> p o", o=1)).then_inc(weights3_in, 16)
                    sp.dma_start(b_out_rows[r:r + 1, :], bout_in.rearrange("(o d) -> o d", o=1)).then_inc(weights3_in, 16)
                sp.dma_start(gate_row[0:1, 0:D], wgate_in).then_inc(weights3_in, 16)
                sp.dma_start(gate_row[0:1, D:XROW], bgate_in.rearrange("(o d) -> o d", o=1)).then_inc(weights3_in, 16)

            @block.gpsimd
            def _(pool):
                pool.memset(gate, 0.0)
                pool.memset(has_edges, 1.0)
                pool.memset(gate_key, float(LAST)).then_inc(pool3_chain, 1)

                def rows_free(i, j):
                    if j == 0:
                        wait(pool, rows3_kept, i * 2 - 1)
                        wait(pool, gates_added, i * 2 - 1)
                    if j == SET:
                        wait(pool, rows3_kept, i * 2)
                        wait(pool, gates_added, i * 2)

                gather_rounds(pool, ETILES // RING, x3_rows,
                              lambda i, s: at_dst[:, bass.ds(i * RING + s * SET, SET)],
                              lambda j: ring[:, j, 0:D], rows_free, rows3_arrived,
                              (4 * ETILES + MCOLS) // RING)

            @block.tensor
            def _(pe):
                pe.wait_ge(weights3_in, 14 * 16)
                pe.matmul(bank[3][:, 0:XROW], lhsT=ones[0:1, :], rhs=gate_row[0:1, :], start=True,
                          stop=True).then_inc(gate_spread, 1)
                pe.transpose(bank[0][:, 0:D], w_out, ident[:, :]).then_inc(w_out_turned, 1)
                pe.wait_ge(w_out_moved, 1)
                pe.matmul(bank[1][:, 0:D], lhsT=w_lin, rhs=w_out_t, start=True, stop=True)
                pe.matmul(bank[2][0:5, 0:D], lhsT=b_lin, rhs=w_out_t, start=True, stop=True).then_inc(pool_made, 1)
                pe.wait_ge(max_ready, 1)
                for n, source in enumerate((gate, gate_key)):
                    for h in range(2):
                        last = pe.transpose(bank[0][:, (2 * n + h) * P:(2 * n + h + 1) * P],
                                            source[:, h * P:(h + 1) * P], ident[:, :])
                last.then_inc(max_turned, 1)
                pe.wait_ge(max_ready, 2)
                for h in range(2):
                    for n, column_of in enumerate((two(by_tile[:, 2 * P:])[:, h, 0:1],
                                                   two(by_tile[:, 2 * P:])[:, h, P - 1:P],
                                                   two(from_on)[:, h, 0:1], two(up_to)[:, h, P - 1:P])):
                        last = pe.transpose(wide[n // 2][0:1, n % 2, h * P:(h + 1) * P], column_of, ident[:, :])
                last.then_inc(max_turned, 1)
                pe.wait_ge(max_ready, 3)
                for n in range(4):
                    last = pe.transpose(bank[1][:, n:n + 1], far[0:1, n * P:(n + 1) * P], ident[0:1, 0:1])
                last.then_inc(max_turned, 1)
                pe.wait_ge(max_ready, 4)
                for h in range(2):
                    last = pe.transpose(bank[2][:, h * P:(h + 1) * P], two(highest)[:, h, :], ident[:, :])
                last.then_inc(max_turned, 1)

            @block.scalar
            def _(act):
                act.wait_ge(w_out_turned, 1)
                act.activation(w_out_t, bank[0][:, 0:D], ACT.Copy).then_inc(w_out_moved, 1)

                def keep(i, s):
                    act.wait_ge(rows3_arrived, i * RING + (s + 1) * SET)
                    act.activation(pooled_rows[:, bass.ds(i * RING + s * SET, SET), :],
                                   ring[:, s * SET:(s + 1) * SET, :], ACT.Copy).then_inc(rows3_kept, 1)

                with act.Fori(0, ETILES // RING) as i:
                    for s in range(2):
                        keep(i, s)
                act.wait_ge(max_turned, 1)
                act.activation(by_tile, bank[0][:, :], ACT.Copy).then_inc(max_moved, 1)
                act.wait_ge(max_turned, 2)
                for n in range(2):
                    last = act.activation(tile_ends[0:1, n * 4 * P:(n + 1) * 4 * P],
                                          wide[n][0:1, 0:2, :].rearrange("p a b -> p (a b)"), ACT.Copy)
                last.then_inc(max_moved, 1)
                act.wait_ge(max_turned, 3)
                act.activation(far_columns, bank[1][:, 0:4], ACT.Copy).then_inc(max_moved, 1)
                act.wait_ge(max_turned, 4)
                act.activation(attention, bank[2][:, 0:2 * P], ACT.Exp)

            @block.vector
            def _(dve):
                dve.wait_ge(gate_spread, 1)
                dve.tensor_copy(gate_all, bank[3][:, 0:XROW]).then_inc(gate_all_made, 1)
                dve.wait_ge(pool_made, 1)
                dve.tensor_copy(w_pool, bank[1][:, 0:D])
                dve.tensor_copy(bias_rows[0:5, :], bank[2][0:5, 0:D]).then_inc(gate_all_made, 1)
                dve.wait_ge(gate_all_made, 2)
                for t in range(4):
                    dve.tensor_scalar(bias_diag[0:5, t * D:(t + 1) * D], bias_rows[0:5, :], ident[0:5, t:t + 1], None,
                                      ALU.mult).then_inc(gate_all_made, 1)
                dve.wait_ge(gate_all_made, 6)
                for t in range(4):
                    dve.scalar_tensor_tensor(bias_diag[0:5, t * D:(t + 1) * D], b_out_rows[0:5, :], ident[0:5, 4:5],
                                             bias_diag[0:5, t * D:(t + 1) * D], ALU.mult, ALU.add)
                dve.wait_ge(pool3_chain, 1)
                chain = [0]

                def then_wait(instruction):
                    chain[0] += 1
                    instruction.then_inc(max_chain, 1)
                    dve.wait_ge(max_chain, chain[0])

                def add_gates(i, s):
                    dve.wait_ge(rows3_arrived, i * RING + (s + 1) * SET)
                    wait(dve, gates_added, i * 2 + s)
                    dve.tensor_tensor(gated, ring[:, s * SET:(s + 1) * SET, 0:D],
                                      gate_all[:, 0:D].unsqueeze(1).to_broadcast([P, SET, D]),
                                      ALU.mult).then_inc(gate_products, 1)
                    dve.wait_ge(gate_products, i * 2 + (s + 1))
                    dve.tensor_reduce(gate[:, bass.ds(i * RING + s * SET, SET)], gated, mybir.AxisListType.X,
                                      ALU.add).then_inc(gates_added, 1)

                for s in range(2):
                    add_gates(0, s)
                with dve.Fori(1, ETILES // RING) as i:
                    for s in range(2):
                        add_gates(i, s)
                dve.wait_ge(gates_added, 2 * ETILES // RING)
                dve.tensor_copy(gate_key[:, 0:ETILES], key_src[:, :])
                then_wait(dve.tensor_scalar(gate[:, 0:ETILES], gate[:, 0:ETILES], gate_all[:, D:XROW], None, ALU.add))
                dve.sem_inc(max_ready, 1)
                dve.wait_ge(max_moved, 1)
                g_t, key_t, change = two(by_tile[:, 0:2 * P]), two(by_tile[:, 2 * P:]), two(changes)
                dve.memset(change[:, :, 0:1], NEVER)
                dve.memset(change[:, :, P:P + 1], NEVER)
                then_wait(dve.tensor_tensor(change[:, :, 1:P], key_t[:, :, 1:P], key_t[:, :, 0:P - 1], ALU.not_equal))
                then_wait(dve.tensor_scalar(change[:, :, 1:P], change[:, :, 1:P], NEVER, None, ALU.mult))
                for h in range(2):
                    dve.tensor_tensor_scan(two(up_to)[:, h, :], change[:, h, 0:P], g_t[:, h, :], NEVER, ALU.add, ALU.max)
                    last = dve.tensor_tensor_scan(two(from_on)[:, h, ::-1], change[:, h, 1:P + 1][:, ::-1],
                                                  g_t[:, h, ::-1], NEVER, ALU.add, ALU.max)
                then_wait(last)
                dve.sem_inc(max_ready, 1)
                dve.wait_ge(max_moved, 2)
                first_key, last_key, of_first, of_last = (tile_ends[0:1, n * 2 * P:(n + 1) * 2 * P] for n in range(4))
                link, one_node = links[0:1, :], whole[0:1, :]
                dve.memset(link[:, 0:1], NEVER)
                dve.memset(link[:, 2 * P:2 * P + 1], NEVER)
                dve.memset(far[0:1, :], NEVER)
                dve.tensor_tensor(link[:, 1:2 * P], first_key[:, 1:2 * P], last_key[:, 0:2 * P - 1], ALU.not_equal)
                then_wait(dve.tensor_tensor(one_node, first_key, last_key, ALU.not_equal))
                dve.tensor_scalar(link[:, 1:2 * P], link[:, 1:2 * P], NEVER, None, ALU.mult)
                then_wait(dve.tensor_scalar(one_node, one_node, NEVER, None, ALU.mult))
                dve.tensor_tensor(add_up_to[0:1, :], link[:, 0:2 * P], one_node, ALU.add)
                then_wait(dve.tensor_tensor(add_from[0:1, :], link[:, 1:2 * P + 1], one_node, ALU.add))
                dve.tensor_tensor_scan(best_up_to[0:1, :], add_up_to[0:1, :], of_last, NEVER, ALU.add, ALU.max)
                then_wait(dve.tensor_tensor_scan(best_from[0:1, ::-1], add_from[0:1, ::-1], of_first[:, ::-1], NEVER,
                                                 ALU.add, ALU.max))
                dve.tensor_tensor(far[0:1, 1:2 * P], best_up_to[0:1, 0:2 * P - 1], link[:, 1:2 * P], ALU.add)
                then_wait(dve.tensor_tensor(far[0:1, 2 * P:4 * P - 1], best_from[0:1, 1:2 * P], link[:, 1:2 * P],
                                            ALU.add))
                dve.sem_inc(max_ready, 1)
                dve.wait_ge(max_moved, 3)
                then_wait(dve.tensor_tensor(highest, up_to, from_on, ALU.max))
                for h in range(2):
                    most = two(highest)[:, h, :]
                    for end, from_far in ((0, far_columns[:, h:h + 1]), (P - 1, far_columns[:, 2 + h:3 + h])):
                        then_wait(dve.tensor_scalar(other_key, key_t[:, h, :], key_t[:, h, end:end + 1], NEVER,
                                                    ALU.not_equal, ALU.mult))
                        then_wait(dve.scalar_tensor_tensor(most, other_key, from_far, most, ALU.add, ALU.max))
                then_wait(dve.tensor_tensor(two(highest), g_t, two(highest), ALU.subtract))
                dve.sem_inc(max_ready, 1)

        with nc.Block() as block:

            @block.vector
            def _(dve):
                with dve.Fori(0, ETILES // SET) as n:
                    rows = pooled_rows[:, bass.ds(n * SET, SET), :]
                    dve.tensor_tensor(rows, rows, attention[:, bass.ds(n * SET, SET)].unsqueeze(2).to_broadcast(
                        [P, SET, XROW]), ALU.mult)

        seg3 = Segments(3, key_src[:, :], pairs_src, SPAN,
                        lambda e: pooled_rows[:, bass.ds(e, 1), :].rearrange("p a f -> p (a f)"),
                        lambda half, t: wide[half][:, t, 0:XROW])
        x3_back = [sem(f"x3_back{u}") for u in range(4)]
        denominator_made = sem("denominator_made")
        share3_made = sem("share3_made")
        has_edges_made = sem("has_edges_made")
        pooled_turned = sem("pooled_turned")
        pooled_moved = sem("pooled_moved")
        update3_made = sem("update3_made")
        norm4 = Norm(3, out, update3_made)

        with nc.Block() as block:

            @block.sync
            def _(sp):
                def stage(h):
                    if h.live():
                        norm4.wait(sp, y_made, h.k - 3)
                        load_half(sp, x3_rows, h, x3_back)
                    b = h.minus(6)
                    if h.u % 2 == 0 and b.live():
                        norm4.store(sp, b)

                each_half(sp, stage, 6)
                norm4.finish(sp)

            @block.tensor
            def _(pe):
                registers = first_registers["pe"]
                seg3.start(pe)

                def stage(h):
                    if h.live():
                        seg3.add_up(pe, registers, h)
                    b = h.minus(1)
                    if b.live():
                        seg3.wait_moved(pe, b.k + 1)
                        pe.wait_ge(has_edges_made, b.k + 1)
                        wait(pe, pooled_moved, b.k)
                        for t in range(4):
                            pe.transpose(bank[1][:, t * P:(t + 1) * P], pair[0][:, b.u % 2, t * D:(t + 1) * D],
                                         ident[:, :])
                        pe.transpose(bank[0][0:5, 0:P], has_edges[:, b.u % 2, :], ident[:, :]).then_inc(pooled_turned, 1)
                    c = h.minus(2)
                    if c.live():
                        q = c.u % 2
                        norm4.wait(pe, y_made, c.k - 1)
                        pe.wait_ge(pooled_moved, c.k + 1)
                        pe.matmul(bank[2 + q][:, :], lhsT=has_edges_t[0:5, q, :], rhs=bias_diag[0:5, :], start=True,
                                  stop=False, skip_group_check=True)
                        for t in range(4):
                            last = pe.matmul(bank[2 + q][:, t * D:(t + 1) * D], lhsT=pair[1][:, q, t * P:(t + 1) * P],
                                             rhs=w_pool, start=False, stop=t == 3, skip_group_check=True)
                        last.then_inc(update3_made, 1)

                each_half(pe, stage, 2)

            @block.scalar
            def _(act):
                def stage(h):
                    par = h.u % 2
                    if h.live():
                        act.wait_ge(has_edges_made, h.k + 1)
                        wait(act, pooled_turned, h.k - 1)
                        for t in range(4):
                            last = act.activation(pair[0][:, par, t * D:(t + 1) * D], wide[par][:, t, 0:D], ACT.Copy,
                                                  scale=share[:, par, t:t + 1])
                        last.then_inc(sums_moved, 1)
                    b = h.minus(1)
                    if b.live():
                        act.wait_ge(pooled_turned, b.k + 1)
                        wait(act, update3_made, b.k - 1)
                        act.activation(pair[1][:, b.u % 2, :], bank[1][:, :], ACT.Copy)
                        act.activation(has_edges_t[0:5, b.u % 2, :], bank[0][0:5, 0:P],
                                       ACT.Copy).then_inc(pooled_moved, 1)
                    c = h.minus(3)
                    if c.live():
                        norm4.root(act, c)
                    d = h.minus(4)
                    if d.live():
                        norm4.on_act(act, d)

                each_half(act, stage, 4)

            @block.vector
            def _(dve):
                registers = first_registers["dve"]

                def stage(h):
                    par = h.u % 2
                    if h.live():
                        more = seg3.build(dve, registers, h)
                    b = h.minus(3)
                    if b.live():
                        dve.wait_ge(x3_back[b.u], b.landed())
                    norm4.on_vector(dve, b, h.minus(4), lambda h: bank[2 + h.u % 2][:, :])
                    if h.live():
                        seg3.wait_sums(dve, h, more)
                        seg3.wait_moved(dve, h.k - 1)
                        wait(dve, has_edges_made, h.k - 1)
                        dve.tensor_scalar(degree[:, par, :], wide[par][:, :, D], 1e-16, None,
                                          ALU.add).then_inc(denominator_made, 1)
                        dve.wait_ge(denominator_made, h.k + 1)
                        dve.reciprocal(share[:, par, :], degree[:, par, :]).then_inc(share3_made, 1)
                        dve.wait_ge(share3_made, h.k + 1)
                        wait(dve, pooled_turned, h.k - 1)
                        dve.tensor_tensor(has_edges[:, par, 0:4], wide[par][:, :, D], share[:, par, :],
                                          ALU.mult).then_inc(has_edges_made, 1)

                each_half(dve, stage, 4)


_INS = ["x", "src", "dst", "edge_type_1344", "edge_type_9", "edge_weight1", "L0_gnn_basis", "L0_gnn_comp",
        "L0_gnn_bias", "L0_gnn_gamma", "L0_gnn_beta", "L1_gnn_W_neigh", "L1_gnn_W_self", "L1_gnn_b",
        "L2_gnn_W_msg", "L2_gnn_b_msg", "L2_gnn_edge_embed", "L2_gnn_W_ih", "L2_gnn_W_hh", "L2_gnn_b_ih",
        "L2_gnn_b_hh", "L3_gnn_W_lin", "L3_gnn_b_lin", "L3_gnn_W_gate", "L3_gnn_b_gate", "L3_gnn_W_out",
        "L3_gnn_b_out"]
_OUTS = [((50000, 128), "float32")]


def kernel(**inputs):
    import numpy as _np
    import concourse.bacc as _bacc
    from concourse import mybir as _mybir
    from concourse.bass_utils import run_bass_kernel_spmd as _run

    nc = _bacc.Bacc("TRN2", target_bir_lowering=False, num_devices=1)
    arrays, args = {}, []
    for name in _INS:
        a = _np.ascontiguousarray(inputs[name])
        arrays[f"in_{name}_dram"] = a
        args.append(nc.dram_tensor(f"in_{name}_dram", a.shape, _mybir.dt.from_np(a.dtype), kind="ExternalInput").ap())
    for i, (shape, dtype) in enumerate(_OUTS):
        dt = _mybir.dt.from_np(_np.dtype(dtype))
        args.append(nc.dram_tensor(f"out_{i}_dram", shape, dt, kind="ExternalOutput").ap())
    build(nc, *args)
    r = _run(nc, [arrays], core_ids=[0])
    got = tuple(r.results[0][f"out_{i}_dram"] for i in range(len(_OUTS)))
    return got[0]
```

```python
import struct
from contextlib import ExitStack

import concourse.bass as bass
from concourse import mybir

F32 = mybir.dt.float32
BF16 = mybir.dt.bfloat16
I32 = mybir.dt.int32
U16 = mybir.dt.uint16
ALU = mybir.AluOpType
ACT = mybir.ActivationFunctionType

P = 128
N = 50000
E = 25000
D = 128
EPS = 1e-5
TYPES = 9
RELS, BASES = 1344, 4

G = 8
BLOCK = P * G
BLOCKS = -(-N // BLOCK)
NPAD = BLOCKS * BLOCK
TILES = BLOCKS * G
HALVES = TILES // 4
TAIL = (N - (BLOCKS - 1) * BLOCK) // G
LAST = NPAD - 1

ECOLS = -(-E // P)
ELAST = E - (P - 1) * ECOLS
ETILES = ECOLS
MTILES = -(-2 * E // P)
MCOLS = 392

SCOLS = 256
DST, SRC, REV = 0, 1, 2
SHIFT_D = 512
CENTRE, SHIFT_S = 25088, 256

RING = 28
SET = RING // 2
LAG = 6
FLIGHT = 7
MSG = D + TYPES
XROW = D + 1
PAIRS = TILES // 2
SPAN = 2
SPAN_ALL = 3
NCNT = 200
ENTRY = 4


def float_of(bits):
    return struct.unpack("<f", struct.pack("<I", bits))[0]


PAD_D = float_of((LAST + SHIFT_D) << 15)
PAD_S = float_of((LAST - CENTRE + SHIFT_S) << 16)


def runs(count):
    whole = count // 16 * 16
    return [(a, b) for a, b in ((0, whole), (whole, count)) if b > a]


class Half:

    def __init__(self, i, u):
        self.i, self.u = i, u

    @property
    def k(self):
        return self.i * 4 + self.u

    def minus(self, lag):
        return Half(self.i + (self.u - lag) // 4, (self.u - lag) % 4)

    def live(self):
        return not isinstance(self.i, int) or 0 <= self.k < HALVES

    def landed(self):
        return self.i * 16 + 16


def each_half(eng, stage, lag):
    peeled = -(-(lag + 4) // 4)
    for k in range(4 * peeled):
        stage(Half(k // 4, k % 4))
    with eng.Fori(peeled, HALVES // 4) as i:
        for u in range(4):
            stage(Half(i, u))
    for k in range(HALVES // 4 * 4, HALVES + lag):
        stage(Half(k // 4, k % 4))


def wait(eng, sem, value):
    if not isinstance(value, int) or value > 0:
        eng.wait_ge(sem, value)


def build(nc, x_in, src_in, dst_in, rel_in, type_in, weight_in, basis_in, comp_in, bias0_in, gamma_in,
          beta_in, wneigh_in, wself_in, b1_in, wmsg_in, bmsg_in, emb_in, wih_in, whh_in, bih_in, bhh_in,
          wlin_in, blin_in, wgate_in, bgate_in, wout_in, bout_in, out):
    with ExitStack() as ctx:
        def sb(name, shape, dt=F32):
            return ctx.enter_context(nc.sbuf_tensor(name, shape, dt))

        def sem(name):
            return ctx.enter_context(nc.semaphore(name))

        x1_rows = nc.dram_tensor("x1_rows", [NPAD, D], F32).ap()
        x2_rows = nc.dram_tensor("x2_rows", [NPAD, D], F32).ap()
        x3_rows = nc.dram_tensor("x3_rows", [NPAD, D], F32).ap()
        ht_halves = nc.dram_tensor("ht_halves", [HALVES, P, 512], F32).ap()
        message_rows = nc.dram_tensor("message_rows", [P * ECOLS, MSG], F32).ap()

        wide = [ctx.enter_context(nc.psum_tensor(f"wide{n}", [P, 4, 256], F32)) for n in range(2)]
        bank = [ctx.enter_context(nc.psum_tensor(f"bank{n}", [P, 512], F32)) for n in range(4)]

        ident = sb("ident", [P, P])
        ones = sb("ones", [P, P])
        iota = sb("iota", [P, BLOCK])
        block_base = sb("block_base", [P, 64])
        eps_col = sb("eps_col", [P, 1])
        key_dst = sb("key_dst", [P, ETILES])
        key_src = sb("key_src", [P, ETILES])
        key_all = sb("key_all", [P, MCOLS])
        at_edge = sb("at_edge", [P, ETILES], I32)
        edge_data = sb("edge_data", [P, ECOLS, 6])
        at_src = sb("at_src", [P, ETILES], I32)
        at_dst = sb("at_dst", [P, ETILES], I32)
        at_all = sb("at_all", [P, MCOLS], I32)
        pairs_dst = sb("pairs_dst", [1, NCNT * ENTRY], U16)
        pairs_src = sb("pairs_src", [1, NCNT * ENTRY], U16)
        pairs_all = sb("pairs_all", [1, NCNT * ENTRY], U16)
        type_counts = sb("type_counts", [P, TILES, TYPES])
        ring = sb("ring", [P, RING, MSG])
        ring_at = sb("ring_at", [P, RING], I32)
        basis = sb("basis", [P, BASES * D])
        column = sb("column", [P, 16])
        xb = sb("xb", [P, 4, 4 * D])
        yb = sb("yb", [P, 4, 4 * D])
        ob = sb("ob", [P, 4, 4 * D])
        pair = [sb(f"pair{n}", [P, 2, 4 * D]) for n in range(3)]
        selector = sb("selector", [P, 2, SPAN_ALL * 2 * P])
        more_selector = sb("more_selector", [P, 2 * P])
        key_rel = sb("key_rel", [P, 2, MCOLS])
        moments = ob[:, :, :].rearrange("p a b -> p (a b)")[:, 0:(HALVES - 2 + 8) * 6].rearrange(
            "p (n s) -> p n s", s=6)
        tile_stats = sb("tile_stats", [P, 4, 4, 6])
        mean_var = sb("mean_var", [P, 4, 4, 2])
        root = sb("root", [P, 4, 4])
        inverse = sb("inverse", [P, 4, 4])
        offset = sb("offset", [P, 4, 4])
        big = sb("big", [P, ETILES * MSG])
        messages = big[:, :].rearrange("p (e f) -> p e f", f=MSG)

        def part(offset, *shape):
            size = 1
            for n in shape:
                size *= n
            piece = big[:, offset:offset + size]
            if len(shape) == 2:
                piece = piece.rearrange("p (a b) -> p a b", a=shape[0])
            if len(shape) == 3:
                piece = piece.rearrange("p (a b c) -> p a b c", a=shape[0], b=shape[1])
            return piece, offset + size

        landed = [sem(f"landed{j}") for j in range(FLIGHT)]

        raw_rel, at = part(0, ECOLS)
        raw_src, at = part(at, ECOLS)
        raw_dst, at = part(at, ECOLS)
        raw_type, at = part(at, ECOLS)
        weight, at = part(at, ECOLS)
        coef, at = part(at, ECOLS, BASES)
        keys0, at = part(at, 3 * SCOLS)
        keys1, at = part(at, 3 * SCOLS)
        position, at = part(at, 3 * SCOLS)
        gray, at = part(at, 3 * SCOLS)
        flips, at = part(at, 3 * SCOLS)
        edge_no, at = part(at, ECOLS)
        place, at = part(at, 2, ECOLS)
        scratch, at = part(at, 4, MCOLS)
        table_dst, at = part(at, SCOLS)
        table_src, at = part(at, SCOLS)
        table_rev, at = part(at, SCOLS)
        table_all, at = part(at, 2 * SCOLS)
        last_keys, at = part(at, 8)
        last_tile, at = part(at, 8)
        last_work, at = part(at, 3, 8)
        before, at = part(at, 2, NCNT)
        pair_work, at = part(at, 6, NCNT)
        coef_ring, at = part(at, RING, BASES)
        assert at <= ETILES * MSG
        turn_over = ob[:, 0, 0:P]
        sources = ob[:, 1, 0:SCOLS]
        sign_mask = sb("sign_mask", [P, MCOLS], I32)
        keys = [keys0, keys1]

        def ints(piece):
            return piece.bitcast(I32)

        zeroed = sem("zeroed")
        raw_in = sem("raw_in")
        iotas = sem("iotas")
        vector_chain = sem("vector_chain")
        turn = sem("turn")
        turned = sem("turned")
        moved = sem("moved")
        tables = sem("tables")
        comparing = sem("comparing")
        compared = sem("compared")
        indices = sem("indices")
        coefs_arrived = sem("coefs_arrived")
        coef_moved = sem("coef_moved")
        sources_made = sem("sources_made")
        sources_reversed = sem("sources_reversed")
        pool_chain = sem("pool_chain")

        steps = [("flip", None, DST)]
        for m in range(1, 17):
            first = DST if m < 16 else SRC
            if m > 8:
                steps.append(("turn", None, DST))
                for bit in range(m - 1, 6, -1):
                    steps.append(("compare", 256 if bit == 15 else 1 << (bit - 8) if bit > 7 else P, first))
                steps.append(("turn", None, first))
            for bit in range(min(m - 1, 7 if m < 9 else 6), -1, -1):
                steps.append(("compare", 1 << bit, first))
            if m < 16:
                steps.append(("flip", m, DST))
        steps.append(("turn", None, SRC))
        turns = [(n % 2, first) for n, (kind, _, first) in enumerate(steps) if kind == "turn"]
        SPLIT = len(turns) - 3
        FINAL = len(turns) - 1

        counts = ((0, 2, pairs_dst, ETILES, SPAN), (2, 4, pairs_src, ETILES, SPAN),
                  (4, 8, pairs_all, MTILES, SPAN_ALL))

        TURNS = RING // FLIGHT

        def gather_rounds(pool, rounds, rows, index_of, slot_of, free, arrived, base, after=None):
            def one_round(i):
                for j in range(RING):
                    first = isinstance(i, int)
                    if j % SET == 0:
                        s = j // SET
                        pool.tensor_copy(ring_at[:, j:j + SET], index_of(i, s)).then_inc(indices, 1)
                        pool.wait_ge(indices, i * 2 + (2 * base + s + 1))
                    free(i, j)
                    if j >= LAG or not first:
                        pool.wait_ge(landed[(j - LAG) % FLIGHT],
                                     i * (16 * TURNS) + 16 * (base * TURNS + (j - LAG) // FLIGHT + 1))
                        pool.sem_inc(arrived, 1)
                    pool.indirect_dma_start(
                        out=slot_of(j), out_offset=None, in_=rows,
                        in_offset=bass.IndirectOffsetOnAxis(ap=ring_at[:, j:j + 1], axis=0),
                    ).then_inc(landed[j % FLIGHT], 16)
                    if after and j >= LAG:
                        after(i, j - LAG)
                    elif after and not first:
                        after(i - 1, j - LAG + RING)

            one_round(0)
            with pool.Fori(1, rounds) as i:
                one_round(i)
            for j in range(RING - LAG, RING):
                pool.wait_ge(landed[j % FLIGHT], 16 * ((rounds - 1 + base) * TURNS + j // FLIGHT + 1))
                pool.sem_inc(arrived, 1)
                if after:
                    after(rounds - 1, j)

        with nc.Block() as block:

            @block.sync
            def _(sp):
                sp.wait_ge(zeroed, 1)
                for piece, source in ((raw_rel, rel_in), (raw_src, src_in), (raw_dst, dst_in), (raw_type, type_in),
                                      (weight, weight_in.rearrange("e o -> (e o)"))):
                    piece = piece if source.dtype == F32 else ints(piece)
                    for a, b in runs(P - 1):
                        sp.dma_start(piece[a:b, :],
                                     source[a * ECOLS:b * ECOLS].rearrange("(p c) -> p c", c=ECOLS)).then_inc(raw_in, 16)
                    sp.dma_start(piece[P - 1:P, 0:ELAST],
                                 source[(P - 1) * ECOLS:E].rearrange("(p c) -> p c", p=1)).then_inc(raw_in, 16)

            @block.gpsimd
            def _(pool):
                pool.memset(big[:, 0:5 * ECOLS], 0.0).then_inc(zeroed, 1)
                pool.iota(ints(position)[:, 0:SCOLS], [[1, SCOLS]], base=0, channel_multiplier=SCOLS)
                pool.iota(ints(position)[:, SCOLS:2 * SCOLS], [[1, SCOLS]], base=0, channel_multiplier=SCOLS)
                pool.iota(ints(position)[:, 2 * SCOLS:3 * SCOLS], [[1, SCOLS]], base=P * SCOLS,
                          channel_multiplier=SCOLS)
                pool.iota(ints(edge_no), [[1, ECOLS]], base=0, channel_multiplier=ECOLS).then_inc(iotas, 1)
                pool.memset(ident[:, :], 0.0).then_inc(pool_chain, 1)
                pool.wait_ge(pool_chain, 1)
                pool.affine_select(out=ident[:, :], in_=ident[:, :], compare_op=ALU.not_equal, fill=1.0, base=0,
                                   pattern=[[-1, P]], channel_multiplier=1)
                pool.memset(turn_over, 0.0).then_inc(pool_chain, 1)
                pool.wait_ge(pool_chain, 2)
                pool.affine_select(out=turn_over, in_=turn_over, compare_op=ALU.not_equal, fill=1.0, base=1 - P,
                                   pattern=[[1, P]], channel_multiplier=1).then_inc(pool_chain, 1)
                pool.memset(ones[:, :], 1.0)
                pool.memset(eps_col[:, :], EPS)
                pool.iota(iota[:, :], [[1, BLOCK]], base=0, channel_multiplier=0,
                          allow_small_or_imprecise_dtypes=True)
                pool.iota(block_base[:, :], [[BLOCK, 64]], base=0, channel_multiplier=0,
                          allow_small_or_imprecise_dtypes=True).then_inc(iotas, 1)
                pool.wait_ge(raw_in, 15 * 16)

                def free(i, j):
                    if j == 0:
                        wait(pool, coef_moved, i * 2 - 1)
                    if j == SET:
                        wait(pool, coef_moved, i * 2)

                def landed_set(i, j):
                    if j % SET == SET - 1:
                        pool.tensor_copy(coef[:, bass.ds(i * RING + (j - SET + 1), SET), :],
                                         coef_ring[:, j - SET + 1:j + 1, :]).then_inc(coef_moved, 1)

                gather_rounds(pool, ECOLS // RING, comp_in,
                              lambda i, s: ints(raw_rel)[:, bass.ds(i * RING + s * SET, SET)],
                              lambda j: coef_ring[:, j, :], free, coefs_arrived, 0, landed_set)
                pool.wait_ge(coef_moved, 2 * ECOLS // RING)
                pool.tensor_tensor(edge_data[:, :, 2:2 + BASES], coef,
                                   weight.unsqueeze(2).to_broadcast([P, ECOLS, BASES]), ALU.mult)
                pool.tensor_copy(ints(edge_data[:, :, 0]), ints(raw_src))
                pool.tensor_copy(ints(edge_data[:, :, 1]), ints(raw_type))

            @block.tensor
            def _(pe):
                pe.wait_ge(iotas, 2)
                for n, (source, first) in enumerate(turns):
                    pe.wait_ge(turn, n + 1)
                    if n >= 2:
                        pe.wait_ge(moved, n - 1)
                    for a in range(first, 3):
                        for h in range(2):
                            last = pe.transpose(wide[n % 2][:, a, h * P:(h + 1) * P],
                                                keys[source][:, a * SCOLS + h * P:a * SCOLS + (h + 1) * P], ident[:, :])
                    last.then_inc(turned, 1)
                pe.wait_ge(pool_chain, 3)
                pe.wait_ge(sources_made, 1)
                pe.matmul(bank[3][:, 0:SCOLS], lhsT=turn_over, rhs=sources, start=True,
                          stop=True).then_inc(sources_reversed, 1)
                n = 0
                for c, (a, b, _, _, _) in enumerate(counts):
                    for m in range(a, b):
                        n += 1
                        pe.wait_ge(comparing, n)
                        pe.matmul(bank[c][0:1, 0:NCNT], lhsT=ones[:, 0:1], rhs=before[:, m % 2, :],
                                  start=m == a, stop=m == b - 1).then_inc(compared, 1)

            @block.scalar
            def _(act):
                for n, (source, first) in enumerate(turns):
                    act.wait_ge(turned, n + 1)
                    if n == SPLIT:
                        for a, table in ((DST, table_dst), (SRC, table_src), (REV, table_rev)):
                            act.activation(table.rearrange("q (p h) -> q h p", h=2),
                                           wide[n % 2][:, a, :].rearrange("q (h p) -> q h p", h=2), ACT.Copy)
                    if n < FINAL:
                        act.activation(keys[1 - source][:, first * SCOLS:], wide[n % 2][:, first:3, :].rearrange(
                            "q a c -> q (a c)"), ACT.Copy).then_inc(moved, 1)
                    else:
                        for a, h in ((0, SRC), (1, REV)):
                            last = act.activation(
                                table_all[:, a * SCOLS:(a + 1) * SCOLS].rearrange("q (p h) -> q h p", h=2),
                                wide[n % 2][:, h, :].rearrange("q (h p) -> q h p", h=2), ACT.Copy)
                        last.then_inc(moved, 1)

            @block.vector
            def _(dve):
                chain = [0]

                def then_wait(instruction):
                    chain[0] += 1
                    instruction.then_inc(vector_chain, 1)
                    dve.wait_ge(vector_chain, chain[0])

                def bits(target, source, a, op0, b=None, op1=None):
                    if op1 is None:
                        return dve.tensor_scalar(target, source, a, None, op0)
                    return dve.tensor_scalar(target, source, a, b, op0, op1)

                SHR, SHL, SAR, AND = (ALU.logical_shift_right, ALU.logical_shift_left, ALU.arith_shift_right,
                                      ALU.bitwise_and)
                dve.wait_ge(iotas, 1)
                dve.memset(keys0[:, 0:SCOLS], PAD_D)
                dve.memset(keys0[:, SCOLS:], PAD_S)
                then_wait(bits(ints(gray), ints(position), 1, SHR))
                then_wait(dve.tensor_tensor(ints(gray), ints(gray), ints(position), ALU.bitwise_xor))
                dve.wait_ge(raw_in, 15 * 16)
                t0, t1 = ints(scratch)[:, 0, 0:ECOLS], ints(scratch)[:, 1, 0:ECOLS]
                for n, raw in enumerate((raw_src, raw_dst)):
                    at_place = ints(place)[:, n, :]
                    bits(t0, ints(raw), G - 1, AND, 7, SHL)
                    bits(t1, ints(raw), 3, SHR, P - 1, AND)
                    then_wait(bits(at_place, ints(raw), 10, SHR, 10, SHL))
                    then_wait(dve.tensor_tensor(at_place, at_place, t0, ALU.bitwise_or))
                    then_wait(dve.tensor_tensor(at_place, at_place, t1, ALU.bitwise_or))
                    then_wait(dve.tensor_scalar(t0, ints(edge_no), E, float(LAST), ALU.is_ge, ALU.mult))
                    then_wait(dve.tensor_tensor(at_place, at_place, t0, ALU.add))
                then_wait(dve.tensor_scalar(t0, ints(place)[:, 1, :], float(SHIFT_D), None, ALU.add))
                then_wait(bits(t0, t0, 15, SHL))
                then_wait(dve.tensor_tensor(ints(keys0)[:, 0:ECOLS], t0, ints(edge_no), ALU.bitwise_or))
                for a, own, other in ((SRC, 0, raw_dst), (REV, 1, raw_src)):
                    then_wait(dve.tensor_scalar(t0, ints(place)[:, own, :], float(CENTRE), 2.0 * SHIFT_S, ALU.is_ge,
                                                ALU.mult))
                    then_wait(dve.scalar_tensor_tensor(t1, ints(place)[:, own, :], float(-CENTRE - SHIFT_S), t0,
                                                       ALU.add, ALU.add))
                    then_wait(bits(t1, t1, 16, SHL))
                    then_wait(dve.tensor_tensor(t1, t1, ints(other), ALU.bitwise_or))
                    then_wait(bits(sign_mask[:, 0:ECOLS], t1, 31, SAR, 0x7FFFFFFF, AND))
                    then_wait(dve.tensor_tensor(ints(keys0)[:, a * SCOLS:a * SCOLS + ECOLS], t1,
                                                sign_mask[:, 0:ECOLS], ALU.bitwise_xor))

                n_turn = 0
                for n, (kind, value, first) in enumerate(steps):
                    source, target = keys[n % 2], keys[1 - n % 2]
                    if kind == "flip":
                        number, m = (position, 1) if value is None else (gray, value)
                        if n == 0:
                            then_wait(bits(ints(flips), ints(number), m, SHR, 31, SHL))
                        then_wait(dve.tensor_tensor(ints(target), ints(source), ints(flips), ALU.bitwise_xor))
                    elif kind == "compare":
                        low, high, low_to, high_to = (
                            x[:, first * SCOLS:].rearrange("p (n two d) -> p n two d", two=2, d=value)[:, :, w, :]
                            for x in (source, target) for w in (0, 1))
                        dve.tensor_tensor(low_to, low, high, ALU.min)
                        if steps[n + 1][0] == "flip":
                            bits(ints(flips), ints(gray), steps[n + 1][1], SHR, 31, SHL)
                        then_wait(dve.tensor_tensor(high_to, low, high, ALU.max))
                    else:
                        if n_turn == SPLIT:
                            then_wait(dve.tensor_copy(last_keys[:, 0:4], source[:, 0:2 * SCOLS].rearrange(
                                "p (n c) -> p n c", c=P)[:, :, P - 1]))
                        if n_turn == FINAL:
                            then_wait(dve.tensor_copy(last_keys[:, 4:8], source[:, SCOLS:3 * SCOLS].rearrange(
                                "p (n c) -> p n c", c=P)[:, :, P - 1]))
                        n_turn += 1
                        dve.sem_inc(turn, 1)
                        dve.wait_ge(moved, n_turn)

                def places_of_pairs(target, table, width, other):
                    mask, key, high = sign_mask[:, 0:width], ints(scratch)[:, 0, 0:width], ints(scratch)[:, 1, 0:width]
                    then_wait(bits(mask, ints(table), 31, SAR, 0x7FFFFFFF, AND))
                    then_wait(dve.tensor_tensor(key, ints(table), mask, ALU.bitwise_xor))
                    if other is not None:
                        last = bits(other, key, 0xFFFF, AND)
                        if target is None:
                            then_wait(last)
                    if target is None:
                        return
                    then_wait(bits(high, key, 16, SAR))
                    then_wait(dve.tensor_scalar(scratch[:, 2, 0:width], high, 0.0, -2.0 * SHIFT_S, ALU.is_ge, ALU.mult))
                    then_wait(dve.scalar_tensor_tensor(target, high, float(CENTRE + SHIFT_S), scratch[:, 2, 0:width],
                                                       ALU.add, ALU.add))

                def places_of_edges(target, table, width, edge):
                    high = ints(scratch)[:, 3, 0:width]
                    if edge is not None:
                        bits(edge, ints(table), 0x7FFF, AND).then_inc(vector_chain, 1)
                        chain[0] += 1
                    then_wait(bits(high, ints(table), 15, SHR))
                    then_wait(dve.tensor_scalar(target, high, float(-SHIFT_D), None, ALU.add))

                places_of_edges(key_dst[:, :], table_dst[:, 0:ETILES], ETILES, at_edge[:, :])
                found = ints(scratch)[:, 2, 0:SCOLS]
                places_of_pairs(None, table_rev, SCOLS, found)
                then_wait(dve.tensor_copy(sources, found))
                dve.sem_inc(sources_made, 1)
                places_of_pairs(key_src[:, :], table_src[:, 0:ETILES], ETILES, at_dst[:, :])
                places_of_pairs(key_all[:, :], table_all[:, 0:MCOLS], MCOLS, at_all[:, :])
                dve.wait_ge(sources_reversed, 1)
                dve.tensor_copy(at_src[:, :], bank[3][:, SCOLS - ETILES:SCOLS][:, ::-1])
                places_of_edges(last_work[:, 0, 0:2], last_keys[:, 0:2], 2, None)
                places_of_pairs(last_work[:, 0, 2:8], last_keys[:, 2:8], 6, None)
                then_wait(dve.tensor_copy(ints(last_work)[:, 1, :], last_work[:, 0, :]))
                then_wait(bits(ints(last_work)[:, 2, :], ints(last_work)[:, 1, :], 8, SHR))
                then_wait(dve.tensor_copy(last_tile, ints(last_work)[:, 2, :]))
                for m in range(8):
                    if m >= 2:
                        dve.wait_ge(compared, m - 1)
                    dve.tensor_scalar(before[:, m % 2, :], iota[:, 0:NCNT], last_tile[:, m:m + 1], None,
                                      ALU.is_gt).then_inc(comparing, 1)
                first, base, more, so_far, work, zero = (pair_work[0:1, n, :] for n in range(6))
                then_wait(dve.memset(pair_work[0:1, :, :], 0.0))
                for c, (_, b, table, tiles, span) in enumerate(counts):
                    entry = table.rearrange("o (n f) -> o n f", f=ENTRY)
                    dve.wait_ge(compared, b)
                    then_wait(dve.tensor_scalar(first, bank[c][0:1, 0:NCNT], float(tiles - 1), None, ALU.min))
                    then_wait(dve.tensor_scalar(base, first, float(tiles - span), None, ALU.min))
                    then_wait(dve.tensor_tensor(more[:, 0:NCNT - 1], first[:, 1:NCNT], base[:, 0:NCNT - 1],
                                                ALU.subtract))
                    then_wait(dve.tensor_scalar(more, more, float(1 - span), 0.0, ALU.add, ALU.max))
                    then_wait(dve.tensor_tensor_scan(so_far[:, 1:NCNT], more[:, 0:NCNT - 1], zero[:, 1:NCNT], 0.0,
                                                     ALU.add, ALU.max))
                    then_wait(dve.tensor_tensor(work, base, so_far, ALU.subtract))
                    dve.tensor_copy(entry[:, :, 0], so_far)
                    dve.tensor_copy(entry[:, :, 1], base)
                    then_wait(dve.tensor_scalar(entry[:, :, 2], work, float(span), None, ALU.add))
                    then_wait(dve.tensor_tensor(work[:, 0:NCNT - 1], base[:, 1:NCNT], base[:, 0:NCNT - 1],
                                                ALU.subtract))
                    then_wait(dve.tensor_tensor(entry[:, 0:NCNT - 1, 3], work[:, 0:NCNT - 1], more[:, 0:NCNT - 1],
                                                ALU.subtract))


        rows_arrived = sem("rows_arrived")
        row_turned = sem("row_turned")
        row_moved = sem("row_moved")
        based = sem("based")
        scaled = sem("scaled")
        summed = sem("summed")
        message_made = sem("message_made")
        hot_chain = sem("hot_chain")
        basis_in_sem = sem("basis_in_sem")
        hot_made = sem("hot_made")
        messages_stored = sem("messages_stored")
        products = pair[1][:, :, 0:2 * D].rearrange("p q (b d) -> p q b d", b=2)
        sums = pair[2][:, :, 0:2 * D].rearrange("p q (b d) -> p q b d", b=2)
        type_col = key_rel[:, 0, 0:ETILES]

        def each_tile(eng, stage, tiles, lag):
            for j in range(RING):
                stage(0, j)
            with eng.Fori(1, tiles // RING) as i:
                for j in range(RING):
                    stage(i, j)
            for j in range(lag):
                stage(tiles // RING, j)

        def tile_before(i, j):
            return (i, j - 1) if j else (i - 1, RING - 1)

        with nc.Block() as block:

            @block.sync
            def _(sp):
                sp.dma_start(basis[:, :].rearrange("i (b o) -> i b o", b=BASES),
                             basis_in.rearrange("b i o -> i b o")).then_inc(basis_in_sem, 16)
                for c, source in enumerate((bias0_in, gamma_in, beta_in)):
                    sp.dma_start(column[:, c:c + 1], source.rearrange("(p o) -> p o", o=1)).then_inc(basis_in_sem, 16)
                sp.wait_ge(hot_made, 1)
                row = message_rows.rearrange("(p c) f -> p c f", c=ECOLS)
                for n in range(ETILES // SET):
                    sp.wait_ge(message_made, (n + 1) * SET)
                    sp.dma_start(row[:, n * SET:(n + 1) * SET, :],
                                 messages[:, n * SET:(n + 1) * SET, :]).then_inc(messages_stored, 16)
                sp.wait_ge(messages_stored, ETILES // SET * 16)

            @block.gpsimd
            def _(pool):
                def rows_free(i, j):
                    wait(pool, row_turned, i * RING + (j - RING + 1))

                gather_rounds(pool, ETILES // RING, x_in,
                              lambda i, s: ints(edge_data[:, bass.ds(i * RING + s * SET, SET), 0]),
                              lambda j: ring[:, j, 0:D], rows_free, rows_arrived, ETILES // RING)

            @block.tensor
            def _(pe):
                pe.wait_ge(basis_in_sem, 64)

                def stage(i, j):
                    if not isinstance(i, int) or i < ETILES // RING:
                        pe.wait_ge(rows_arrived, i * RING + (j + 1))
                        wait(pe, row_moved, i * RING + (j - 1))
                        pe.transpose(bank[j % 2][:, 0:P], ring[:, j, 0:D], ident[:, :]).then_inc(row_turned, 1)
                    if isinstance(i, int) and (i, j) == (0, 0):
                        return
                    q = (j - 1) % 2
                    pe.wait_ge(row_moved, i * RING + j)
                    wait(pe, summed, i * RING + (j - 2))
                    pe.matmul(bank[2 + q][:, :], lhsT=pair[0][:, q, 0:P], rhs=basis[:, :], start=True,
                              stop=True).then_inc(based, 1)

                each_tile(pe, stage, ETILES, 1)

            @block.scalar
            def _(act):
                def stage(i, j):
                    if not isinstance(i, int) or i < ETILES // RING:
                        act.wait_ge(row_turned, i * RING + (j + 1))
                        wait(act, based, i * RING + (j - 1))
                        act.activation(pair[0][:, j % 2, 0:P], bank[j % 2][:, 0:P], ACT.Copy).then_inc(row_moved, 1)
                    if isinstance(i, int) and (i, j) == (0, 0):
                        return
                    ib, jb = tile_before(i, j)
                    act.wait_ge(based, i * RING + j)
                    wait(act, summed, i * RING + (j - 2))
                    for b in range(2):
                        last = act.activation(products[:, jb % 2, b, :], bank[2 + jb % 2][:, b * D:(b + 1) * D], ACT.Copy,
                                              scale=edge_data[:, bass.ds(ib * RING + jb, 1), 2 + b])
                    last.then_inc(scaled, 1)

                each_tile(act, stage, ETILES, 1)

            @block.vector
            def _(dve):
                dve.tensor_scalar(type_col, ints(edge_data[:, :, 1]), 0.0, float(TYPES - 1), ALU.max,
                                  ALU.min).then_inc(hot_chain, 1)
                dve.wait_ge(hot_chain, 1)
                for t in range(TYPES):
                    last = dve.tensor_scalar(messages[:, :, D + t], type_col, float(t), None, ALU.is_equal)
                last.then_inc(hot_made, 1)

                def stage(i, j):
                    q = j % 2
                    dve.wait_ge(scaled, i * RING + (j + 1))
                    wait(dve, message_made, i * RING + (j - 1))
                    for b in range(2):
                        last = dve.scalar_tensor_tensor(
                            sums[:, q, b, :], bank[2 + q][:, (2 + b) * D:(3 + b) * D],
                            edge_data[:, bass.ds(i * RING + j, 1), 4 + b], products[:, q, b, :], ALU.mult, ALU.add)
                    last.then_inc(summed, 1)
                    dve.wait_ge(summed, i * RING + (j + 1))
                    dve.tensor_tensor(messages[:, bass.ds(i * RING + j, 1), 0:D], sums[:, q, 0:1, :],
                                      sums[:, q, 1:2, :], ALU.add).then_inc(message_made, 1)

                each_tile(dve, stage, ETILES, 0)

        keys_made = sem("keys_made")
        pairs_built = sem("pairs_built")
        pairs_used = sem("pairs_used")
        halves_seen = sem("halves_seen")
        sums_moved = sem("sums_moved")

        class Segments:

            def __init__(self, passes, keys, table, span, source, target, banks=2, arrived=None):
                self.passes = passes
                self.keys, self.table, self.span, self.source = keys, table, span, source
                self.count = keys.shape[1]
                self.target = target
                self.banks = banks
                self.arrived = arrived
                self.passed = sem(f"tiles_passed{passes}") if arrived is not None else None
                self.more_built = sem(f"more_built{passes}")
                self.more_used = sem(f"more_used{passes}")

            def wait_moved(self, eng, halves):
                if not isinstance(halves, int) or halves > 0:
                    eng.wait_ge(sums_moved, halves + self.passes * HALVES)

            def _wait_pair(self, eng, signal, n):
                if not isinstance(n, int) or n > 0:
                    eng.wait_ge(signal, n + self.passes * PAIRS)

            def entries(self, eng, registers, h):
                eng.load(registers, self.table[0:1, bass.ds(h.k * (2 * ENTRY), 2 * ENTRY + 1)])

                def number(n):
                    most = self.count - (self.span if n % ENTRY == 1 else 1)
                    return eng.snap(registers[n], min_val=0, max_val=most)

                return number

            def tile_of(self, value):
                return nc.s_assert_within(
                    value, 0, self.count - 1,
                    skip_runtime_bounds_check_because="phase 1 makes the table with every first tile under the count")

            def build(self, dve, registers, h):
                v = h.u // 2
                if h.u % 2 == 0:
                    self._wait_pair(dve, pairs_built, h.i * 8 + (4 * v - 3))
                    dve.tensor_scalar(key_rel[:, v, 0:self.count], self.keys, block_base[:, bass.ds(h.i * 2 + v, 1)],
                                      None, ALU.subtract).then_inc(keys_made, 1)
                    dve.wait_ge(keys_made, h.i * 2 + (v + 1 + self.passes * BLOCKS))
                number = self.entries(dve, registers, h)
                start_of_half = so_far_next = number(0)
                for j in range(2):
                    so_far, base, so_far_next = so_far_next, number(j * ENTRY + 1), number((j + 1) * ENTRY)
                    start = (h.u % 2 * 4 + 2 * j) * P
                    nodes = iota[:, start:start + 2 * P]
                    self._wait_pair(dve, pairs_used, h.k * 2 + (j - 1))
                    dve.tensor_tensor(
                        selector[:, j, 0:self.span * 2 * P].rearrange("p (s n) -> p s n", s=self.span),
                        nodes.unsqueeze(1).to_broadcast([P, self.span, 2 * P]),
                        key_rel[:, v, bass.ds(base, self.span)].unsqueeze(2).to_broadcast([P, self.span, 2 * P]),
                        ALU.is_equal).then_inc(pairs_built, 1)
                    with dve.If(so_far < so_far_next):
                        to_tile = number(j * ENTRY + 2)
                        with dve.Fori(so_far, so_far_next) as m:
                            e = self.tile_of(m + to_tile)
                            dve.wait_ge(self.more_used, m + 1)
                            dve.tensor_scalar(more_selector[:, :], nodes, key_rel[:, v, bass.ds(e, 1)], None,
                                              ALU.is_equal).then_inc(self.more_built, 1)
                return start_of_half

            def wait_sums(self, eng, h, more):
                self._wait_pair(eng, pairs_used, h.k * 2 + 2)
                eng.wait_ge(self.more_used, more + 1)

            def start(self, pe):
                pe.sem_inc(self.more_used, 1)

            def add_up(self, pe, registers, h):
                number = self.entries(pe, registers, h)
                so_far_next = number(0)
                self.wait_moved(pe, h.k - 1)
                for j in range(2):
                    so_far, base, so_far_next = so_far_next, number(j * ENTRY + 1), number((j + 1) * ENTRY)
                    self._wait_pair(pe, pairs_built, h.k * 2 + (j + 1))
                    if self.arrived is not None:
                        pe.wait_ge(self.arrived, base + self.span)
                    for s in range(self.span):
                        for t in range(2):
                            n = (2 * s + t) * P
                            last = pe.matmul(self.target(h.u % 2, 2 * j + t), lhsT=selector[:, j, n:n + P],
                                             rhs=self.source(base + s), start=s + t == 0 and j < self.banks, stop=False,
                                             skip_group_check=True)
                    last.then_inc(pairs_used, 1)
                    with pe.If(so_far < so_far_next):
                        to_tile = number(j * ENTRY + 2)
                        with pe.Fori(so_far, so_far_next) as m:
                            e = self.tile_of(m + to_tile)
                            pe.wait_ge(self.more_built, m + 1)
                            if self.arrived is not None:
                                pe.wait_ge(self.arrived, e + 1)
                            for t in range(2):
                                last = pe.matmul(self.target(h.u % 2, 2 * j + t), lhsT=more_selector[:, t * P:(t + 1) * P],
                                                 rhs=self.source(e), start=False, stop=False,
                                                 skip_group_check=True)
                            last.then_inc(self.more_used, 1)

            def pass_on(self, eng, registers, h):
                number = self.entries(eng, registers, h)
                so_far, so_far_next = number(0), number(2 * ENTRY)
                advance = eng.snap(number(3) + number(ENTRY + 3))
                with eng.If(so_far < so_far_next):
                    with eng.Fori(so_far, so_far_next) as m:
                        eng.wait_ge(self.more_used, m + 2)
                        eng.sem_inc(self.passed, 1)
                self._wait_pair(eng, pairs_used, h.k * 2 + 2)
                eng.sem_inc(halves_seen, 1)
                with eng.If(advance > 0):
                    with eng.Fori(0, advance):
                        eng.sem_inc(self.passed, 1)

        def rows_of_block(rows, b, partitions=P):
            if isinstance(b, int):
                return rows[b * BLOCK:b * BLOCK + partitions * G, :].rearrange("(p g) d -> p (g d)", g=G)
            return rows[bass.ds(b * BLOCK, BLOCK), :].rearrange("(p g) d -> p (g d)", g=G)

        def block_view(buffer, v):
            return buffer[:, 2 * v:2 * v + 2, :].rearrange("p h d -> p (h d)")

        def tail_of(h):
            return TAIL if isinstance(h.i, int) and h.k // 2 == BLOCKS - 1 else P

        y_made = sem("y_made")
        stats_made = sem("stats_made")
        stats_seen = sem("stats_seen")
        means_made = sem("means_made")
        rooted = sem("rooted")
        inverted = sem("inverted")
        factors_made = sem("factors_made")
        act_done = sem("act_done")
        dve_done = sem("dve_done")

        class Norm:

            def __init__(self, passes, rows, product_made, with_x=False, act_tiles=2, dve_passes=0):
                self.act_tiles = act_tiles
                self.dve_passes = dve_passes
                self.with_x = with_x
                self.passes = passes
                self.rows, self.product_made = rows, product_made
                self.stored = [sem(f"norm{passes}_stored{v}") for v in range(2)]

            def root(self, act, h):
                self.wait(act, means_made, h.k + 1)
                act.activation(root[:, h.u, :], mean_var[:, h.u, :, 1], ACT.Sqrt,
                               bias=eps_col[:, 0:1]).then_inc(rooted, 1)

            def _out_free(self, eng, h):
                wait(eng, self.stored[h.u // 2], h.i * 16)

            def on_act(self, act, h):
                self.wait(act, factors_made, h.k + 1)
                self._out_free(act, h)
                for t in range(self.act_tiles):
                    last = act.activation(ob[:, h.u, t * D:(t + 1) * D], yb[:, h.u, t * D:(t + 1) * D], ACT.Identity,
                                          scale=inverse[:, h.u, t:t + 1], bias=offset[:, h.u, t:t + 1])
                last.then_inc(act_done, 1)

            def wait(self, eng, signal, halves):
                if not isinstance(halves, int) or halves > 0:
                    eng.wait_ge(signal, halves + self.passes * HALVES)

            def wait_dve(self, eng, halves):
                if self.act_tiles < 4 and (not isinstance(halves, int) or halves > 0):
                    eng.wait_ge(dve_done, halves + self.dve_passes * HALVES)

            def on_vector(self, dve, b, c, product):
                if b.live():
                    self.wait(dve, act_done, b.k - 3)
                    self.wait_dve(dve, b.k - 3)
                    dve.wait_ge(self.product_made, b.k + 1)
                    if self.with_x:
                        dve.tensor_copy(yb[:, b.u, :], product(b)).then_inc(y_made, 1)
                    else:
                        dve.tensor_tensor(yb[:, b.u, :], product(b), xb[:, b.u, :], ALU.add).then_inc(y_made, 1)
                if c.live():
                    self.wait(dve, rooted, c.k + 1)
                    dve.reciprocal(inverse[:, c.u, :], root[:, c.u, :]).then_inc(inverted, 1)
                if b.live():
                    self.wait(dve, y_made, b.k + 1)
                    for t in range(4):
                        last = dve.bn_stats(out=tile_stats[:, b.u, t, :], in_=yb[:, b.u, t * D:(t + 1) * D])
                    last.then_inc(stats_made, 1)
                if c.live():
                    self.wait(dve, inverted, c.k + 1)
                    dve.scalar_tensor_tensor(offset[:, c.u, :], mean_var[:, c.u, :, 0], -1.0, inverse[:, c.u, :],
                                             ALU.mult, ALU.mult).then_inc(factors_made, 1)
                if b.live():
                    self.wait(dve, stats_made, b.k + 1)
                    dve.sem_inc(stats_seen, 1)
                    for t in range(4):
                        last = dve.bn_aggr(out=mean_var[:, b.u, t, :], in_=tile_stats[:, b.u, t, :])
                    last.then_inc(means_made, 1)
                if c.live() and self.act_tiles < 4:
                    self.wait(dve, factors_made, c.k + 1)
                    self._out_free(dve, c)
                    for t in range(self.act_tiles, 4):
                        last = dve.tensor_scalar(ob[:, c.u, t * D:(t + 1) * D], yb[:, c.u, t * D:(t + 1) * D],
                                                 inverse[:, c.u, t:t + 1], offset[:, c.u, t:t + 1], ALU.mult, ALU.add)
                    last.then_inc(dve_done, 1)

            def store(self, sp, h):
                v = h.u // 2
                self.wait(sp, act_done, h.k + 2)
                sp.sem_inc(halves_seen, 1)
                self.wait_dve(sp, h.k + 2)
                sp.sem_inc(halves_seen, 1)
                tail = P if self.rows.shape[0] == NPAD else tail_of(h)
                sp.dma_start(rows_of_block(self.rows, h.i * 2 + v, tail),
                             block_view(ob, v)[0:tail, :]).then_inc(self.stored[v], 16)

            def finish(self, sp):
                for v in range(2):
                    sp.wait_ge(self.stored[v], 16 * ((BLOCKS + 1 - v) // 2))

        messages_arrived = sem("messages_arrived")
        seg0 = Segments(0, key_dst[:, :], pairs_dst, SPAN,
                        lambda e: ring[:, bass.ds(e % RING, 1), :].rearrange("p a f -> p (a f)"),
                        lambda half, t: wide[half][:, t, 0:MSG], arrived=messages_arrived)
        x0_in = [sem(f"x0_in{v}") for v in range(2)]
        ht_stored = [sem(f"ht_stored{u}") for u in range(4)]
        x0_turned = sem("x0_turned")
        sum_turned = sem("sum_turned")
        relu_made = sem("relu_made")
        ht_made = sem("ht_made")
        moments_made = sem("moments_made")

        first_registers = {}

        with nc.Block() as block:

            @block.gpsimd
            def _(pool):
                def rows_free(i, j):
                    wait(pool, seg0.passed, i * RING + (j - RING + 1))

                gather_rounds(pool, ETILES // RING, message_rows,
                              lambda i, s: at_edge[:, bass.ds(i * RING + s * SET, SET)],
                              lambda j: ring[:, j, :], rows_free, messages_arrived, 2 * ETILES // RING)

            @block.sync
            def _(sp):
                registers = first_registers["sp"] = [sp.alloc_register(f"sp_first{n}") for n in range(2 * ENTRY + 1)]

                def stage(h):
                    a = h.minus(3)
                    if a.live():
                        seg0.pass_on(sp, registers, a)
                    v = h.u // 2
                    if h.u % 2 == 0 and h.live():
                        wait(sp, x0_turned, h.k - 2)
                        tail = tail_of(h)
                        sp.dma_start(block_view(xb, v)[0:tail, :],
                                     rows_of_block(x_in, h.i * 2 + v, tail)).then_inc(x0_in[v], 16)
                    b = h.minus(5)
                    if b.live():
                        sp.wait_ge(ht_made, b.k + 1)
                        sp.dma_start(ht_halves[b.k] if isinstance(b.k, int) else
                                     ht_halves[bass.ds(b.k, 1), :, :].rearrange("o p c -> (o p) c"),
                                     yb[:, b.u, :]).then_inc(ht_stored[b.u], 16)

                each_half(sp, stage, 5)
                for u in range(4):
                    sp.wait_ge(ht_stored[u], 16 * len(range(u, HALVES, 4)))

            @block.tensor
            def _(pe):
                registers = first_registers["pe"] = [pe.alloc_register(f"pe_first{n}") for n in range(2 * ENTRY + 1)]
                seg0.start(pe)

                def stage(h):
                    par = h.u % 2
                    if h.live():
                        seg0.add_up(pe, registers, h)
                        pe.wait_ge(x0_in[h.u // 2], h.landed())
                        wait(pe, ht_made, h.k - 1)
                        for t in range(4):
                            last = pe.transpose(bank[par][:, t * P:(t + 1) * P], xb[:, h.u, t * D:(t + 1) * D],
                                                ident[:, :])
                        last.then_inc(x0_turned, 1)
                    b = h.minus(1)
                    if b.live():
                        seg0.wait_moved(pe, b.k + 1)
                        wait(pe, relu_made, b.k - 1)
                        for t in range(4):
                            last = pe.transpose(bank[2 + b.u % 2][:, t * P:(t + 1) * P],
                                                pair[0][:, b.u % 2, t * D:(t + 1) * D], ident[:, :])
                        last.then_inc(sum_turned, 1)

                each_half(pe, stage, 1)

            @block.scalar
            def _(act):
                def stage(h):
                    par = h.u % 2
                    if h.live():
                        act.wait_ge(x0_turned, h.k + 1)
                        wait(act, sum_turned, h.k - 1)
                        act.activation(pair[0][:, par, :].rearrange("p (t d) -> p t d", d=D), wide[par][:, :, 0:D],
                                       ACT.Copy)
                        act.activation(type_counts[:, bass.ds(h.k * 4, 4), :], wide[par][:, :, D:MSG],
                                       ACT.Copy).then_inc(sums_moved, 1)
                    b = h.minus(1)
                    if b.live():
                        act.wait_ge(sum_turned, b.k + 1)
                        wait(act, ht_made, b.k - 1)
                        act.activation(pair[1][:, b.u % 2, :], bank[2 + b.u % 2][:, :], ACT.Relu,
                                       bias=column[:, 0:1]).then_inc(relu_made, 1)

                each_half(act, stage, 1)

            @block.vector
            def _(dve):
                registers = first_registers["dve"] = [dve.alloc_register(f"dve_first{n}") for n in range(2 * ENTRY + 1)]

                def stage(h):
                    if h.live():
                        seg0.build(dve, registers, h)
                    b = h.minus(2)
                    if b.live():
                        dve.wait_ge(relu_made, b.k + 1)
                        wait(dve, ht_stored[b.u], b.i * 16)
                        wait(dve, moments_made, b.k - 3)
                        dve.tensor_tensor(yb[:, b.u, :], bank[b.u % 2][:, :], pair[1][:, b.u % 2, :],
                                          ALU.add).then_inc(ht_made, 1)
                    b = h.minus(3)
                    if b.live():
                        dve.wait_ge(ht_made, b.k + 1)
                        if tail_of(b) < P:
                            for t in range(4):
                                last = dve.bn_stats(out=moments[:, HALVES - 2 + b.u * 4 + t, :],
                                                    in_=yb[:, b.u, t * P:t * P + TAIL])
                            last.then_inc(moments_made, 1)
                        else:
                            dve.bn_stats(out=moments[:, bass.ds(b.k, 1), :].rearrange("p a s -> p (a s)"),
                                         in_=yb[:, b.u, :]).then_inc(moments_made, 1)

                each_half(dve, stage, 3)

        def load_half(sp, rows, h, signal):
            first = (h.k - h.u % 2) // 2 if isinstance(h.k, int) else h.i * 2 + h.u // 2
            valid = P if rows.shape[0] == NPAD else tail_of(h)
            block_rows = rows_of_block(rows, first, valid)
            part_of = slice(h.u % 2 * 4 * D, (h.u % 2 + 1) * 4 * D)
            sp.dma_start(xb[0:valid, h.u, :], block_rows[:, part_of]).then_inc(signal[h.u], 16)

        norm_scale, norm_offset = column[:, 8:9], column[:, 9:10]
        moments_added = sem("moments_added")
        spread_made = sem("spread_made")
        batch_chain = sem("batch_chain")

        with nc.Block() as block:

            @block.vector
            def _(dve):
                mean, variance = mean_var[:, 0, 0, 0:1], mean_var[:, 0, 0, 1:2]
                dve.bn_aggr(out=mean_var[:, 0, 0, :], in_=moments[:, :, :]).then_inc(moments_added, 1)
                dve.wait_ge(spread_made, 1)
                dve.reciprocal(inverse[:, 0, 0:1], root[:, 0, 0:1]).then_inc(batch_chain, 1)
                dve.wait_ge(batch_chain, 1)
                dve.tensor_tensor(norm_scale, inverse[:, 0, 0:1], column[:, 1:2], ALU.mult).then_inc(batch_chain, 1)
                dve.wait_ge(batch_chain, 2)
                dve.tensor_tensor(offset[:, 0, 0:1], mean, norm_scale, ALU.mult).then_inc(batch_chain, 1)
                dve.wait_ge(batch_chain, 3)
                dve.tensor_tensor(norm_offset, column[:, 2:3], offset[:, 0, 0:1], ALU.subtract)

            @block.scalar
            def _(act):
                act.wait_ge(moments_added, 1)
                act.activation(root[:, 0, 0:1], mean_var[:, 0, 0, 1:2], ACT.Sqrt,
                               bias=eps_col[:, 0:1]).then_inc(spread_made, 1)

        x0_back = [sem(f"x0_back{u}") for u in range(4)]
        ht_back = [sem(f"ht_back{u}") for u in range(4)]
        batch_done = sem("batch_done")
        h_turned = sem("h_turned")
        norm1 = Norm(0, x1_rows, h_turned)
        ht_slot = [pair[1 + u // 2][:, u % 2, :] for u in range(4)]

        with nc.Block() as block:

            @block.sync
            def _(sp):
                def stage(h):
                    if h.live():
                        wait(sp, batch_done, h.k - 3)
                        sp.dma_start(ht_slot[h.u], ht_halves[h.k] if isinstance(h.k, int) else
                                     ht_halves[bass.ds(h.k, 1), :, :].rearrange("o p c -> (o p) c")).then_inc(
                                         ht_back[h.u], 16)
                        norm1.wait(sp, y_made, h.k - 3)
                        load_half(sp, x_in, h, x0_back)
                    if h.u % 2 == 0:
                        b = h.minus(6)
                        if b.live():
                            norm1.store(sp, b)

                each_half(sp, stage, 6)
                norm1.finish(sp)

            @block.scalar
            def _(act):
                def stage(h):
                    if h.live():
                        act.wait_ge(ht_back[h.u], h.landed())
                        wait(act, h_turned, h.k - 1)
                        act.activation(pair[0][:, h.u % 2, :], ht_slot[h.u], ACT.Relu, scale=norm_scale,
                                       bias=norm_offset).then_inc(batch_done, 1)
                    b = h.minus(2)
                    if b.live():
                        norm1.root(act, b)
                    c = h.minus(3)
                    if c.live():
                        norm1.on_act(act, c)

                each_half(act, stage, 3)

            @block.tensor
            def _(pe):
                def stage(h):
                    pe.wait_ge(batch_done, h.k + 1)
                    norm1.wait(pe, y_made, h.k - 3)
                    for t in range(4):
                        last = pe.transpose(bank[h.u][:, t * P:(t + 1) * P], pair[0][:, h.u % 2, t * P:(t + 1) * P],
                                            ident[:, :])
                    last.then_inc(h_turned, 1)

                each_half(pe, stage, 0)

            @block.vector
            def _(dve):
                def stage(h):
                    b = h.minus(1)
                    if b.live():
                        dve.wait_ge(x0_back[b.u], b.landed())
                    norm1.on_vector(dve, b, h.minus(3), lambda h: bank[h.u][:, :])

                each_half(dve, stage, 3)

        SPLIT_ROWS = 3
        w_neigh, at = part(0, D)
        w_self, at = part(at, D)
        row_wide, at = part(at, 4 * D)
        row_rest, at = part(at, 4 * D)
        row_part, at = part(at, 3, 2 * D)
        row_pick, at = part(at, 4 * D)
        row_split, at = part(at, 2 * D)
        row_ones, at = part(at, P // 2)
        x1_t, at = part(at, 4, 512)
        bias_wide, bias_rest, bias_pick = (x[0:SPLIT_ROWS, :] for x in (row_wide, row_rest, row_pick))
        bias_part = row_part[0:SPLIT_ROWS, :, :].bitcast(BF16)
        bias_split = row_split[0:SPLIT_ROWS, :].bitcast(BF16)
        ones_split = row_ones[0:SPLIT_ROWS, :].bitcast(BF16)
        degree = sb("degree", [P, 2, 4])
        share = sb("share", [P, 2, 4])

        def split_rows(dve, chain, counted):
            def then_wait(instruction):
                instruction.then_inc(chain, 1)
                counted[0] += 1
                dve.wait_ge(chain, counted[0])

            then_wait(dve.tensor_copy(bias_part[:, 0, :], bias_wide[:, :]))
            then_wait(dve.tensor_tensor(bias_rest[:, :], bias_wide[:, :], bias_part[:, 0, :], ALU.subtract))
            then_wait(dve.tensor_copy(bias_part[:, 1, :], bias_rest[:, :]))
            then_wait(dve.tensor_tensor(bias_rest[:, :], bias_rest[:, :], bias_part[:, 1, :], ALU.subtract))
            then_wait(dve.tensor_copy(bias_part[:, 2, :], bias_rest[:, :]))
            then_wait(dve.tensor_scalar(bias_pick[:, :], bias_part[:, 0, :], ident[0:3, 0:1], None, ALU.mult))
            then_wait(dve.scalar_tensor_tensor(bias_pick[:, :], bias_part[:, 1, :], ident[0:3, 1:2], bias_pick[:, :],
                                               ALU.mult, ALU.add))
            then_wait(dve.scalar_tensor_tensor(bias_split[:, :], bias_part[:, 2, :], ident[0:3, 2:3], bias_pick[:, :],
                                               ALU.mult, ALU.add))

        weights1_in = sem("weights1_in")
        split1_chain = sem("split1_chain")

        with nc.Block() as block:

            @block.sync
            def _(sp):
                sp.dma_start(w_neigh[:, :], wneigh_in).then_inc(weights1_in, 16)
                sp.dma_start(w_self[:, :], wself_in).then_inc(weights1_in, 16)
                for t in range(4):
                    for r in range(SPLIT_ROWS):
                        sp.dma_start(bias_wide[r:r + 1, t * D:(t + 1) * D],
                                     b1_in.rearrange("(o d) -> o d", o=1)).then_inc(weights1_in, 16)
                sp.wait_ge(weights1_in, 14 * 16)

            @block.gpsimd
            def _(pool):
                pool.memset(ring[:, :, D:XROW], 1.0)

            @block.vector
            def _(dve):
                dve.wait_ge(weights1_in, 14 * 16)
                dve.memset(ones_split[:, :], 1.0)
                dve.tensor_tensor(w_self, w_self, ident[:, :], ALU.add)
                split_rows(dve, split1_chain, [0])

        rows1_arrived = sem("rows1_arrived")
        seg1 = Segments(1, key_all[:, :], pairs_all, SPAN_ALL,
                        lambda e: ring[:, bass.ds(e % RING, 1), 0:XROW].rearrange("p a f -> p (a f)"),
                        lambda half, t: wide[half][:, t, 0:XROW], arrived=rows1_arrived)
        x1_back = [sem(f"x1_back{u}") for u in range(4)]
        degree_made = sem("degree_made")
        share_made = sem("share_made")
        mean_turned = sem("mean_turned")
        mean_moved = sem("mean_moved")
        x1_turned = sem("x1_turned")
        x1_moved = sem("x1_moved")
        update_made = sem("update_made")
        norm2 = Norm(1, x2_rows, update_made, with_x=True, act_tiles=4)

        with nc.Block() as block:

            @block.gpsimd
            def _(pool):
                def rows_free(i, j):
                    wait(pool, seg1.passed, i * RING + (j - RING + 1))

                gather_rounds(pool, MCOLS // RING, x1_rows,
                              lambda i, s: at_all[:, bass.ds(i * RING + s * SET, SET)],
                              lambda j: ring[:, j, 0:D], rows_free, rows1_arrived, 3 * ETILES // RING)

            @block.sync
            def _(sp):
                registers = first_registers["sp"]

                def stage(h):
                    a = h.minus(4)
                    if a.live():
                        seg1.pass_on(sp, registers, a)
                    if h.live():
                        wait(sp, x1_turned, h.k - 3)
                        load_half(sp, x1_rows, h, x1_back)
                    b = h.minus(10)
                    if h.u % 2 == 0 and b.live():
                        norm2.store(sp, b)

                each_half(sp, stage, 10)
                norm2.finish(sp)

            @block.tensor
            def _(pe):
                registers = first_registers["pe"]
                seg1.start(pe)

                def stage(h):
                    par = h.u % 2
                    if h.live():
                        seg1.add_up(pe, registers, h)
                        pe.wait_ge(x1_back[h.u], h.landed())
                        wait(pe, x1_moved, h.k)
                        for t in range(4):
                            last = pe.transpose(bank[0][:, t * P:(t + 1) * P], xb[:, h.u, t * D:(t + 1) * D],
                                                ident[:, :])
                        last.then_inc(x1_turned, 1)
                    b = h.minus(2)
                    if b.live():
                        seg1.wait_moved(pe, b.k + 1)
                        wait(pe, mean_moved, b.k)
                        for t in range(4):
                            last = pe.transpose(bank[1][:, t * P:(t + 1) * P],
                                                pair[0][:, b.u % 2, t * D:(t + 1) * D], ident[:, :])
                        last.then_inc(mean_turned, 1)
                    c = h.minus(3)
                    if c.live():
                        q = c.u % 2
                        norm2.wait(pe, y_made, c.k - 1)
                        pe.matmul(bank[2 + q][:, :], lhsT=ones_split[:, :], rhs=bias_split[:, :], start=True,
                                  stop=False, skip_group_check=True)
                        pe.wait_ge(x1_moved, c.k + 1)
                        for t in range(4):
                            pe.matmul(bank[2 + q][:, t * D:(t + 1) * D], lhsT=x1_t[:, c.u, t * P:(t + 1) * P],
                                      rhs=w_self[:, :], start=False, stop=False, skip_group_check=True)
                        pe.wait_ge(mean_moved, c.k + 1)
                        for t in range(4):
                            last = pe.matmul(bank[2 + q][:, t * D:(t + 1) * D], lhsT=pair[1][:, q, t * P:(t + 1) * P],
                                             rhs=w_neigh[:, :], start=False, stop=t == 3, skip_group_check=True)
                        last.then_inc(update_made, 1)

                each_half(pe, stage, 3)

            @block.scalar
            def _(act):
                def stage(h):
                    a = h.minus(1)
                    par = a.u % 2
                    if a.live():
                        act.wait_ge(share_made, a.k + 1)
                        wait(act, mean_turned, a.k - 1)
                        for t in range(4):
                            last = act.activation(pair[0][:, par, t * D:(t + 1) * D], wide[par][:, t, 0:D], ACT.Copy,
                                                  scale=share[:, par, t:t + 1])
                        last.then_inc(sums_moved, 1)
                    if h.live():
                        wait(act, update_made, h.k - 3)
                        act.wait_ge(x1_turned, h.k + 1)
                        act.activation(x1_t[:, h.u, :], bank[0][:, :], ACT.Copy).then_inc(x1_moved, 1)
                    b = h.minus(2)
                    if b.live():
                        act.wait_ge(mean_turned, b.k + 1)
                        wait(act, update_made, b.k - 1)
                        act.activation(pair[1][:, b.u % 2, :], bank[1][:, :], ACT.Copy).then_inc(mean_moved, 1)
                    c = h.minus(4)
                    if c.live():
                        norm2.root(act, c)
                    d = h.minus(5)
                    if d.live():
                        norm2.on_act(act, d)

                each_half(act, stage, 5)

            @block.vector
            def _(dve):
                registers = first_registers["dve"]

                def stage(h):
                    if h.live():
                        seg1.build(dve, registers, h)
                    a = h.minus(1)
                    par = a.u % 2
                    if a.live():
                        dve.wait_ge(x1_turned, a.k + 1)
                        seg1.wait_moved(dve, a.k - 1)
                        dve.tensor_scalar(degree[:, par, :], wide[par][:, :, D], 1.0, None,
                                          ALU.max).then_inc(degree_made, 1)
                    norm2.on_vector(dve, h.minus(4), h.minus(5), lambda h: bank[2 + h.u % 2][:, :])
                    if a.live():
                        dve.wait_ge(degree_made, a.k + 1)
                        dve.reciprocal(share[:, par, :], degree[:, par, :]).then_inc(share_made, 1)

                each_half(dve, stage, 5)

        w_rows, at = part(0, 7, D)
        w_turned, at = part(at, 7, D)
        W_MSG, W_I, W_H = 0, 1, 4
        RESET, UPDATE, NEW = 0, 1, 2
        type_rows, at = part(at, D)
        msg_bias, at = part(at, D)
        COPIES = 6
        ROWS = COPIES * TYPES
        w_fold, at = part(at, 3, D)
        type_cols, at = part(at, ROWS)
        picks, at = part(at, COPIES + 3)
        type_rest, at = part(at, 3 * D)
        type_part, at = part(at, 3, 3 * D // 2)
        type_pick, at = part(at, 3 * D)
        type_split, at = part(at, 3 * D // 2)
        type_part, type_split = type_part.bitcast(BF16), type_split.bitcast(BF16)
        counts_low, at = part(at, TILES, TYPES)
        counts_high, at = part(at, TILES, TYPES)
        gate_bias, at = part(at, 6)
        x_t, at = part(at, 4, 512)
        counts_t, at = part(at, 2, 256)
        counts_t = counts_t.bitcast(BF16)
        counts_now, at = part(at, 2 * 4 * ROWS)
        counts_now = counts_now.rearrange("p (n t c) -> p n t c", n=2, t=4)
        agg_t, at = part(at, 2, 512)
        reset_t, at = part(at, 2, 512)
        update_t, at = part(at, 2, 512)
        before_tanh, at = part(at, 2, 512)
        new_t, at = part(at, 2, 512)
        h_t, at = part(at, 2, 512)
        between, at = part(at, 4, 512)
        between = between.rearrange("p (a b) c -> p a b c", a=2)
        reset_bias, update_bias = column[:, 3:4], column[:, 4:5]
        new_i_bias, new_h_bias = gate_bias[:, 2:3], gate_bias[:, 5:6]
        wide_bank = [wide[n][:, 2 * m:2 * m + 2, :].rearrange("p a b -> p (a b)") for n in range(2) for m in range(2)]
        sum_banks = [wide_bank[0], wide_bank[2]]
        bank_sums_t, bank_x_t, bank_reset, bank_update = bank
        bank_new_i, bank_new_h = wide_bank[1], wide_bank[3]

        weights2_in = sem("weights2_in")
        weights2_turned = sem("weights2_turned")
        weights2_moved = sem("weights2_moved")
        fold_chain = sem("fold_chain")
        folded = sem("folded")

        with nc.Block() as block:

            @block.sync
            def _(sp):
                sp.dma_start(w_rows[:, W_MSG, :], wmsg_in).then_inc(weights2_in, 16)
                sp.dma_start(w_rows[:, W_I:W_I + 3, :], wih_in.rearrange("(g o) i -> o g i", g=3)).then_inc(weights2_in, 16)
                sp.dma_start(w_rows[:, W_H:W_H + 3, :], whh_in.rearrange("(g o) i -> o g i", g=3)).then_inc(weights2_in, 16)
                sp.dma_start(type_rows[0:TYPES, :], emb_in).then_inc(weights2_in, 16)
                for t in range(TYPES):
                    sp.dma_start(msg_bias[t:t + 1, :], bmsg_in.rearrange("(o d) -> o d", o=1)).then_inc(weights2_in, 16)
                for g in range(3):
                    for n, source in enumerate((bih_in, bhh_in)):
                        sp.dma_start(gate_bias[:, 3 * n + g:3 * n + g + 1],
                                     source[g * D:(g + 1) * D].rearrange("(p o) -> p o", o=1)).then_inc(weights2_in, 16)

            @block.tensor
            def _(pe):
                pe.wait_ge(weights2_in, 19 * 16)
                for w in range(7):
                    last = pe.transpose(bank[w // 4][:, w % 4 * D:(w % 4 + 1) * D], w_rows[:, w, :], ident[:, :])
                last.then_inc(weights2_turned, 1)
                pe.wait_ge(fold_chain, 1)
                pe.transpose(bank[2][:, 0:TYPES], type_rows[0:TYPES, :], ident[0:TYPES, 0:TYPES]).then_inc(folded, 1)
                pe.wait_ge(weights2_moved, 1)
                gates = w_turned[:, W_I:W_I + 3, :].rearrange("p w o -> p (w o)")
                pe.matmul(bank[3][:, 0:3 * D], lhsT=w_rows[:, W_MSG, :], rhs=gates, start=True, stop=True)
                pe.wait_ge(fold_chain, 2)
                pe.matmul(bank[0][0:ROWS, 0:3 * D], lhsT=type_cols, rhs=gates, start=True, stop=True).then_inc(folded, 1)

            @block.scalar
            def _(act):
                act.wait_ge(weights2_turned, 1)
                for b, count in enumerate((4, 3)):
                    last = act.activation(w_turned[:, 4 * b:4 * b + count, :].rearrange("p w o -> p (w o)"),
                                          bank[b][:, 0:count * D], ACT.Copy)
                last.then_inc(weights2_moved, 1)
                act.wait_ge(folded, 2)
                act.activation(w_fold.rearrange("p w o -> p (w o)"), bank[3][:, 0:3 * D], ACT.Copy)

            @block.vector
            def _(dve):
                dve.wait_ge(weights2_in, 19 * 16)
                chain = [0]

                def then_wait(instruction):
                    chain[0] += 1
                    instruction.then_inc(fold_chain, 1)
                    dve.wait_ge(fold_chain, chain[0])

                then_wait(dve.tensor_tensor(type_rows[0:TYPES, :], type_rows[0:TYPES, :], msg_bias[0:TYPES, :], ALU.add))
                dve.wait_ge(folded, 1)
                then_wait(dve.tensor_copy(type_cols.rearrange("p (c t) -> p c t", t=TYPES),
                                          bank[2][:, 0:TYPES].unsqueeze(1).to_broadcast([P, COPIES, TYPES])))
                then_wait(dve.tensor_copy(ints(counts_high), type_counts[:, :, :]))
                then_wait(dve.tensor_scalar(ints(counts_high), ints(counts_high), 255, None, ALU.bitwise_and))
                then_wait(dve.tensor_copy(counts_low, ints(counts_high)))
                dve.tensor_tensor(counts_high, type_counts[:, :, :], counts_low, ALU.subtract)
                then_wait(dve.tensor_reduce(picks[:, 0:COPIES], ident[:, 0:ROWS].rearrange("p (c t) -> p c t", t=TYPES),
                                            mybir.AxisListType.X, ALU.add))
                then_wait(dve.tensor_tensor(picks[:, COPIES:], picks[:, 0:3], picks[:, 3:6], ALU.add))
                dve.wait_ge(folded, 2)
                rest, pick = type_rest[0:ROWS, :], type_pick[0:ROWS, :]
                parts = [type_part[0:ROWS, n, :] for n in range(3)]
                mask = [picks[0:ROWS, COPIES + n:COPIES + n + 1] for n in range(3)]
                then_wait(dve.tensor_copy(rest, bank[0][0:ROWS, 0:3 * D]))
                for n in range(2):
                    then_wait(dve.tensor_copy(parts[n], rest))
                    then_wait(dve.tensor_tensor(rest, rest, parts[n], ALU.subtract))
                then_wait(dve.tensor_copy(parts[2], rest))
                then_wait(dve.tensor_scalar(pick, parts[0], mask[0], None, ALU.mult))
                then_wait(dve.scalar_tensor_tensor(pick, parts[1], mask[1], pick, ALU.mult, ALU.add))
                dve.scalar_tensor_tensor(type_split[0:ROWS, :], parts[2], mask[2], pick, ALU.mult, ALU.add)
                dve.tensor_tensor(reset_bias, gate_bias[:, 0:1], gate_bias[:, 3:4], ALU.add)
                dve.tensor_tensor(update_bias, gate_bias[:, 1:2], gate_bias[:, 4:5], ALU.add)

        rows2_arrived = sem("rows2_arrived")
        seg2 = Segments(2, key_dst[:, :], pairs_dst, SPAN,
                        lambda e: ring[:, bass.ds(e % RING, 1), 0:D].rearrange("p a f -> p (a f)"),
                        lambda half, t: sum_banks[half][:, t * D:(t + 1) * D], banks=1, arrived=rows2_arrived)
        x2_back = [sem(f"x2_back{u}") for u in range(4)]
        x2_turned = sem("x2_turned")
        x2_moved = sem("x2_moved")
        counts_copied = sem("counts_copied")
        counts_turned = sem("counts_turned")
        counts_moved = sem("counts_moved")
        agg2_turned = sem("agg2_turned")
        agg2_moved = sem("agg2_moved")
        gates_made = sem("gates_made")
        reset_made = sem("reset_made")
        update_gate_made = sem("update_gate_made")
        new_h_used = sem("new_h_used")
        tanh_ready = sem("tanh_ready")
        new_made = sem("new_made")
        gru_chain = sem("gru_chain")
        h_made = sem("h_made")
        h_back = sem("h_back")
        norm3 = Norm(2, x3_rows, h_back, with_x=True, dve_passes=1)

        with nc.Block() as block:

            @block.gpsimd
            def _(pool):
                def rows_free(i, j):
                    wait(pool, seg2.passed, i * RING + (j - RING + 1))

                gather_rounds(pool, ETILES // RING, x2_rows,
                              lambda i, s: at_src[:, bass.ds(i * RING + s * SET, SET)],
                              lambda j: ring[:, j, 0:D], rows_free, rows2_arrived,
                              (3 * ETILES + MCOLS) // RING)

            @block.sync
            def _(sp):
                registers = first_registers["sp"]

                def stage(h):
                    a = h.minus(4)
                    if a.live():
                        seg2.pass_on(sp, registers, a)
                    if h.live():
                        wait(sp, x2_turned, h.k - 3)
                        load_half(sp, x2_rows, h, x2_back)
                    b = h.minus(10)
                    if h.u % 2 == 0 and b.live():
                        norm3.store(sp, b)

                each_half(sp, stage, 10)
                norm3.finish(sp)

            @block.tensor
            def _(pe):
                registers = first_registers["pe"]
                seg2.start(pe)

                def stage(h):
                    b, c = h.minus(1), h.minus(2)
                    q = b.u % 2
                    if h.live():
                        seg2.add_up(pe, registers, h)
                        pe.wait_ge(x2_back[h.u], h.landed())
                        norm3.wait(pe, y_made, h.k - 2)
                        wait(pe, x2_moved, h.k)
                        for t in range(4):
                            last = pe.transpose(bank_x_t[:, t * P:(t + 1) * P], xb[:, h.u, t * D:(t + 1) * D], ident[:, :])
                        last.then_inc(x2_turned, 1)
                    if b.live():
                        seg2.wait_moved(pe, b.k + 1)
                        wait(pe, agg2_moved, b.k)
                        for t in range(4):
                            last = pe.transpose(bank_sums_t[:, t * P:(t + 1) * P],
                                                pair[0][:, q, t * D:(t + 1) * D], ident[:, :])
                        last.then_inc(agg2_turned, 1)
                        pe.wait_ge(x2_moved, b.k + 1)
                        wait(pe, reset_made, b.k)
                        pe.matmul(bank_reset[:, :], lhsT=w_turned[:, W_H + RESET, :], rhs=x_t[:, b.u, :], start=True,
                                  stop=False, skip_group_check=True)
                        wait(pe, update_gate_made, b.k)
                        pe.matmul(bank_update[:, :], lhsT=w_turned[:, W_H + UPDATE, :], rhs=x_t[:, b.u, :], start=True,
                                  stop=False, skip_group_check=True)
                        wait(pe, new_h_used, b.k)
                        pe.matmul(bank_new_h, lhsT=w_turned[:, W_H + NEW, :], rhs=x_t[:, b.u, :], start=True,
                                  stop=True, skip_group_check=True)
                    if h.live():
                        pe.wait_ge(counts_copied, h.k + 1)
                        wait(pe, tanh_ready, h.k - 1)
                        wait(pe, counts_moved, h.k)
                        pe.sem_inc(halves_seen, 1)
                        for t in range(4):
                            last = pe.transpose(
                                bank_new_i[0:ROWS, t * P:(t + 1) * P], counts_now[:, h.u % 2, t, :], ident[:, :])
                        last.then_inc(counts_turned, 1)
                    if c.live():
                        pe.wait_ge(h_made, c.k + 1)
                        norm3.wait(pe, y_made, c.k)
                        if h.live():
                            pe.wait_ge(x2_moved, h.k + 1)
                        for t in range(4):
                            last = pe.transpose(bank_x_t[:, t * D:(t + 1) * D], h_t[:, c.u % 2, t * P:(t + 1) * P],
                                                ident[:, :])
                        last.then_inc(h_back, 1)
                    if b.live():
                        pe.wait_ge(agg2_moved, b.k + 1)
                        pe.wait_ge(counts_moved, b.k + 1)

                        def from_messages(target, gate, start):
                            pe.matmul(target, lhsT=w_fold[:, gate, :], rhs=agg_t[:, q, :], start=start, stop=False,
                                      skip_group_check=True)
                            pe.matmul(target, lhsT=type_split[0:ROWS, gate * D:(gate + 1) * D],
                                      rhs=counts_t[0:ROWS, q, :], start=False, stop=True,
                                      skip_group_check=True).then_inc(gates_made, 1)

                        from_messages(bank_reset[:, :], RESET, False)
                        wait(pe, tanh_ready, b.k)
                        if h.live():
                            pe.wait_ge(counts_moved, h.k + 1)
                        from_messages(bank_new_i, NEW, True)
                        from_messages(bank_update[:, :], UPDATE, False)

                each_half(pe, stage, 2)

            @block.scalar
            def _(act):
                def stage(h):
                    b, c = h.minus(1), h.minus(2)
                    q = b.u % 2
                    if c.live():
                        act.wait_ge(tanh_ready, c.k + 1)
                        wait(act, h_made, c.k - 1)
                        act.activation(new_t[:, c.u % 2, :], before_tanh[:, c.u % 2, :], ACT.Tanh,
                                       bias=new_i_bias).then_inc(new_made, 1)
                    if h.live():
                        act.wait_ge(x2_turned, h.k + 1)
                        wait(act, agg2_turned, h.k - 1)
                        act.activation(pair[0][:, h.u % 2, :], sum_banks[h.u % 2], ACT.Copy).then_inc(sums_moved, 1)
                        wait(act, h_made, h.k - 3)
                        act.activation(x_t[:, h.u, :], bank_x_t[:, :], ACT.Copy).then_inc(x2_moved, 1)
                    if b.live():
                        act.wait_ge(agg2_turned, b.k + 1)
                        wait(act, gates_made, h.k * 3 - 6)
                        act.activation(agg_t[:, q, :], bank_sums_t[:, :], ACT.Copy).then_inc(agg2_moved, 1)
                    if h.live():
                        act.wait_ge(counts_turned, h.k + 1)
                        wait(act, gates_made, h.k * 3 - 3)
                        act.activation(counts_t[0:ROWS, h.u % 2, :], bank_new_i[0:ROWS, :],
                                       ACT.Copy).then_inc(counts_moved, 1)
                    d, e = h.minus(3), h.minus(4)
                    if d.live():
                        norm3.root(act, d)
                    if e.live():
                        norm3.on_act(act, e)
                    if b.live():
                        act.wait_ge(gates_made, h.k * 3 - 2)
                        wait(act, new_h_used, b.k - 1)
                        act.activation(reset_t[:, q, :], bank_reset[:, :], ACT.Sigmoid,
                                       bias=reset_bias).then_inc(reset_made, 1)
                        act.wait_ge(gates_made, h.k * 3)
                        wait(act, h_made, b.k - 1)
                        act.activation(update_t[:, q, :], bank_update[:, :], ACT.Sigmoid,
                                       bias=update_bias).then_inc(update_gate_made, 1)

                each_half(act, stage, 4)

            @block.vector
            def _(dve):
                registers = first_registers["dve"]

                def stage(h):
                    if h.live():
                        wait(dve, counts_turned, h.k - 1)
                        for n, counts_of in enumerate((counts_low, counts_high)):
                            last = dve.tensor_copy(
                                counts_now[:, h.u % 2, :, n * 3 * TYPES:(n + 1) * 3 * TYPES].rearrange(
                                    "p t (c y) -> p t c y", y=TYPES),
                                counts_of[:, bass.ds(h.k * 4, 4), :].unsqueeze(2).to_broadcast([P, 4, 3, TYPES]))
                        last.then_inc(counts_copied, 1)
                        seg2.build(dve, registers, h)
                    norm3.on_vector(dve, h.minus(3), h.minus(4), lambda h: bank_x_t[:, :])
                    c = h.minus(2)
                    q = c.u % 2
                    if c.live():
                        dve.wait_ge(reset_made, c.k + 1)
                        wait(dve, new_made, c.k - 1)
                        dve.scalar_tensor_tensor(between[:, 0, q, :], bank_new_h, new_h_bias, reset_t[:, q, :],
                                                 ALU.add, ALU.mult).then_inc(new_h_used, 1)
                        dve.wait_ge(new_h_used, c.k + 1)
                        dve.wait_ge(update_gate_made, c.k + 1)
                        dve.tensor_tensor(before_tanh[:, q, :], bank_new_i, between[:, 0, q, :],
                                          ALU.add).then_inc(tanh_ready, 1)
                        dve.wait_ge(new_made, c.k + 1)
                        dve.tensor_tensor(between[:, 1, q, :], x_t[:, c.u, :], new_t[:, q, :],
                                          ALU.subtract).then_inc(gru_chain, 1)
                        dve.wait_ge(gru_chain, c.k * 2 + 1)
                        dve.scalar_tensor_tensor(between[:, 0, q, :], update_t[:, q, :], 1.0, between[:, 1, q, :],
                                                 ALU.add, ALU.mult).then_inc(gru_chain, 1)
                        dve.wait_ge(gru_chain, c.k * 2 + 2)
                        wait(dve, h_back, c.k - 1)
                        dve.scalar_tensor_tensor(h_t[:, q, :], new_t[:, q, :], 2.0, between[:, 0, q, :],
                                                 ALU.mult, ALU.add).then_inc(h_made, 1)

                each_half(dve, stage, 4)

        pooled_rows = big[:, 0:ETILES * XROW].rearrange("p (e f) -> p e f", f=XROW)
        at = ETILES * XROW
        w_pool, at = part(at, D)
        bias_diag, at = part(at, 4 * D)
        attention, at = part(at, 2 * P)
        has_edges, at = part(at, 2, 5)
        has_edges_t, at = part(at, 2, P)
        assert at <= ETILES * MSG

        def pieces_of(buffer, *sizes):
            flat, start, pieces = buffer[:, :, :].rearrange("p a b -> p (a b)"), 0, []
            for size in sizes:
                pieces.append(flat[:, start:start + size])
                start += size
            assert start <= flat.shape[1]
            return pieces

        w_lin, w_out, w_out_t, b_lin, b_out_rows, bias_rows = pieces_of(pair[0], D, D, D, 5, D, D)
        gate_row, gate_all = pieces_of(pair[1], XROW, XROW)
        gate, gate_key = pieces_of(pair[2], 2 * P, 2 * P)
        gated = yb[:, :, :].rearrange("p a b -> p (a b)")[:, 0:SET * D].rearrange("p (s d) -> p s d", d=D)
        changes, links, whole, add_up_to, add_from, best_up_to, best_from = pieces_of(
            yb, 2 * (P + 1), 2 * P + 1, 2 * P, 2 * P, 2 * P, 2 * P, 2 * P)
        by_tile, up_to, from_on, highest, other_key, far_columns = pieces_of(ob, 4 * P, 2 * P, 2 * P, 2 * P, P, 4)
        tile_ends, far = pieces_of(xb, 4 * 2 * P, 2 * 2 * P)
        NEVER = -1e30

        def two(piece):
            return piece.rearrange("p (a b) -> p a b", a=2)

        weights3_in = sem("weights3_in")
        gate_spread = sem("gate_spread")
        gate_all_made = sem("gate_all_made")
        w_out_turned = sem("w_out_turned")
        w_out_moved = sem("w_out_moved")
        pool_made = sem("pool_made")
        rows3_arrived = sem("rows3_arrived")
        gate_products = sem("gate_products")
        rows3_kept = sem("rows3_kept")
        gates_added = sem("gates_added")
        pool3_chain = sem("pool3_chain")
        max_ready = sem("max_ready")
        max_turned = sem("max_turned")
        max_moved = sem("max_moved")
        max_chain = sem("max_chain")

        with nc.Block() as block:

            @block.sync
            def _(sp):
                sp.dma_start(w_lin, wlin_in).then_inc(weights3_in, 16)
                sp.dma_start(w_out, wout_in).then_inc(weights3_in, 16)
                for r in range(5):
                    sp.dma_start(b_lin[:, r:r + 1], blin_in.rearrange("(p o) -> p o", o=1)).then_inc(weights3_in, 16)
                    sp.dma_start(b_out_rows[r:r + 1, :], bout_in.rearrange("(o d) -> o d", o=1)).then_inc(weights3_in, 16)
                sp.dma_start(gate_row[0:1, 0:D], wgate_in).then_inc(weights3_in, 16)
                sp.dma_start(gate_row[0:1, D:XROW], bgate_in.rearrange("(o d) -> o d", o=1)).then_inc(weights3_in, 16)

            @block.gpsimd
            def _(pool):
                pool.memset(gate, 0.0)
                pool.memset(has_edges, 1.0)
                pool.memset(gate_key, float(LAST)).then_inc(pool3_chain, 1)

                def rows_free(i, j):
                    if j == 0:
                        wait(pool, rows3_kept, i * 2 - 1)
                        wait(pool, gates_added, i * 2 - 1)
                    if j == SET:
                        wait(pool, rows3_kept, i * 2)
                        wait(pool, gates_added, i * 2)

                gather_rounds(pool, ETILES // RING, x3_rows,
                              lambda i, s: at_dst[:, bass.ds(i * RING + s * SET, SET)],
                              lambda j: ring[:, j, 0:D], rows_free, rows3_arrived,
                              (4 * ETILES + MCOLS) // RING)

            @block.tensor
            def _(pe):
                pe.wait_ge(weights3_in, 14 * 16)
                pe.matmul(bank[3][:, 0:XROW], lhsT=ones[0:1, :], rhs=gate_row[0:1, :], start=True,
                          stop=True).then_inc(gate_spread, 1)
                pe.transpose(bank[0][:, 0:D], w_out, ident[:, :]).then_inc(w_out_turned, 1)
                pe.wait_ge(w_out_moved, 1)
                pe.matmul(bank[1][:, 0:D], lhsT=w_lin, rhs=w_out_t, start=True, stop=True)
                pe.matmul(bank[2][0:5, 0:D], lhsT=b_lin, rhs=w_out_t, start=True, stop=True).then_inc(pool_made, 1)
                pe.wait_ge(max_ready, 1)
                for n, source in enumerate((gate, gate_key)):
                    for h in range(2):
                        last = pe.transpose(bank[0][:, (2 * n + h) * P:(2 * n + h + 1) * P],
                                            source[:, h * P:(h + 1) * P], ident[:, :])
                last.then_inc(max_turned, 1)
                pe.wait_ge(max_ready, 2)
                for h in range(2):
                    for n, column_of in enumerate((two(by_tile[:, 2 * P:])[:, h, 0:1],
                                                   two(by_tile[:, 2 * P:])[:, h, P - 1:P],
                                                   two(from_on)[:, h, 0:1], two(up_to)[:, h, P - 1:P])):
                        last = pe.transpose(wide[n // 2][0:1, n % 2, h * P:(h + 1) * P], column_of, ident[:, :])
                last.then_inc(max_turned, 1)
                pe.wait_ge(max_ready, 3)
                for n in range(4):
                    last = pe.transpose(bank[1][:, n:n + 1], far[0:1, n * P:(n + 1) * P], ident[0:1, 0:1])
                last.then_inc(max_turned, 1)
                pe.wait_ge(max_ready, 4)
                for h in range(2):
                    last = pe.transpose(bank[2][:, h * P:(h + 1) * P], two(highest)[:, h, :], ident[:, :])
                last.then_inc(max_turned, 1)

            @block.scalar
            def _(act):
                act.wait_ge(w_out_turned, 1)
                act.activation(w_out_t, bank[0][:, 0:D], ACT.Copy).then_inc(w_out_moved, 1)

                def keep(i, s):
                    act.wait_ge(rows3_arrived, i * RING + (s + 1) * SET)
                    act.activation(pooled_rows[:, bass.ds(i * RING + s * SET, SET), :],
                                   ring[:, s * SET:(s + 1) * SET, 0:XROW], ACT.Copy).then_inc(rows3_kept, 1)

                with act.Fori(0, ETILES // RING) as i:
                    for s in range(2):
                        keep(i, s)
                act.wait_ge(max_turned, 1)
                act.activation(by_tile, bank[0][:, :], ACT.Copy).then_inc(max_moved, 1)
                act.wait_ge(max_turned, 2)
                for n in range(2):
                    last = act.activation(tile_ends[0:1, n * 4 * P:(n + 1) * 4 * P],
                                          wide[n][0:1, 0:2, :].rearrange("p a b -> p (a b)"), ACT.Copy)
                last.then_inc(max_moved, 1)
                act.wait_ge(max_turned, 3)
                act.activation(far_columns, bank[1][:, 0:4], ACT.Copy).then_inc(max_moved, 1)
                act.wait_ge(max_turned, 4)
                act.activation(attention, bank[2][:, 0:2 * P], ACT.Exp)

            @block.vector
            def _(dve):
                dve.wait_ge(gate_spread, 1)
                dve.tensor_copy(gate_all, bank[3][:, 0:XROW]).then_inc(gate_all_made, 1)
                dve.wait_ge(pool_made, 1)
                dve.tensor_copy(w_pool, bank[1][:, 0:D])
                dve.tensor_copy(bias_rows[0:5, :], bank[2][0:5, 0:D]).then_inc(gate_all_made, 1)
                dve.wait_ge(gate_all_made, 2)
                for t in range(4):
                    dve.tensor_scalar(bias_diag[0:5, t * D:(t + 1) * D], bias_rows[0:5, :], ident[0:5, t:t + 1], None,
                                      ALU.mult).then_inc(gate_all_made, 1)
                dve.wait_ge(gate_all_made, 6)
                for t in range(4):
                    dve.scalar_tensor_tensor(bias_diag[0:5, t * D:(t + 1) * D], b_out_rows[0:5, :], ident[0:5, 4:5],
                                             bias_diag[0:5, t * D:(t + 1) * D], ALU.mult, ALU.add)
                dve.wait_ge(pool3_chain, 1)
                chain = [0]

                def then_wait(instruction):
                    chain[0] += 1
                    instruction.then_inc(max_chain, 1)
                    dve.wait_ge(max_chain, chain[0])

                def add_gates(i, s):
                    dve.wait_ge(rows3_arrived, i * RING + (s + 1) * SET)
                    wait(dve, gates_added, i * 2 + s)
                    dve.tensor_tensor(gated, ring[:, s * SET:(s + 1) * SET, 0:D],
                                      gate_all[:, 0:D].unsqueeze(1).to_broadcast([P, SET, D]),
                                      ALU.mult).then_inc(gate_products, 1)
                    dve.wait_ge(gate_products, i * 2 + (s + 1))
                    dve.tensor_reduce(gate[:, bass.ds(i * RING + s * SET, SET)], gated, mybir.AxisListType.X,
                                      ALU.add).then_inc(gates_added, 1)

                for s in range(2):
                    add_gates(0, s)
                with dve.Fori(1, ETILES // RING) as i:
                    for s in range(2):
                        add_gates(i, s)
                dve.wait_ge(gates_added, 2 * ETILES // RING)
                dve.tensor_copy(gate_key[:, 0:ETILES], key_src[:, :])
                then_wait(dve.tensor_scalar(gate[:, 0:ETILES], gate[:, 0:ETILES], gate_all[:, D:XROW], None, ALU.add))
                dve.sem_inc(max_ready, 1)
                dve.wait_ge(max_moved, 1)
                g_t, key_t, change = two(by_tile[:, 0:2 * P]), two(by_tile[:, 2 * P:]), two(changes)
                dve.memset(change[:, :, 0:1], NEVER)
                dve.memset(change[:, :, P:P + 1], NEVER)
                then_wait(dve.tensor_tensor(change[:, :, 1:P], key_t[:, :, 1:P], key_t[:, :, 0:P - 1], ALU.not_equal))
                then_wait(dve.tensor_scalar(change[:, :, 1:P], change[:, :, 1:P], NEVER, None, ALU.mult))
                for h in range(2):
                    dve.tensor_tensor_scan(two(up_to)[:, h, :], change[:, h, 0:P], g_t[:, h, :], NEVER, ALU.add, ALU.max)
                    last = dve.tensor_tensor_scan(two(from_on)[:, h, ::-1], change[:, h, 1:P + 1][:, ::-1],
                                                  g_t[:, h, ::-1], NEVER, ALU.add, ALU.max)
                then_wait(last)
                dve.sem_inc(max_ready, 1)
                dve.wait_ge(max_moved, 2)
                first_key, last_key, of_first, of_last = (tile_ends[0:1, n * 2 * P:(n + 1) * 2 * P] for n in range(4))
                link, one_node = links[0:1, :], whole[0:1, :]
                dve.memset(link[:, 0:1], NEVER)
                dve.memset(link[:, 2 * P:2 * P + 1], NEVER)
                dve.memset(far[0:1, :], NEVER)
                dve.tensor_tensor(link[:, 1:2 * P], first_key[:, 1:2 * P], last_key[:, 0:2 * P - 1], ALU.not_equal)
                then_wait(dve.tensor_tensor(one_node, first_key, last_key, ALU.not_equal))
                dve.tensor_scalar(link[:, 1:2 * P], link[:, 1:2 * P], NEVER, None, ALU.mult)
                then_wait(dve.tensor_scalar(one_node, one_node, NEVER, None, ALU.mult))
                dve.tensor_tensor(add_up_to[0:1, :], link[:, 0:2 * P], one_node, ALU.add)
                then_wait(dve.tensor_tensor(add_from[0:1, :], link[:, 1:2 * P + 1], one_node, ALU.add))
                dve.tensor_tensor_scan(best_up_to[0:1, :], add_up_to[0:1, :], of_last, NEVER, ALU.add, ALU.max)
                then_wait(dve.tensor_tensor_scan(best_from[0:1, ::-1], add_from[0:1, ::-1], of_first[:, ::-1], NEVER,
                                                 ALU.add, ALU.max))
                dve.tensor_tensor(far[0:1, 1:2 * P], best_up_to[0:1, 0:2 * P - 1], link[:, 1:2 * P], ALU.add)
                then_wait(dve.tensor_tensor(far[0:1, 2 * P:4 * P - 1], best_from[0:1, 1:2 * P], link[:, 1:2 * P],
                                            ALU.add))
                dve.sem_inc(max_ready, 1)
                dve.wait_ge(max_moved, 3)
                then_wait(dve.tensor_tensor(highest, up_to, from_on, ALU.max))
                for h in range(2):
                    most = two(highest)[:, h, :]
                    for end, from_far in ((0, far_columns[:, h:h + 1]), (P - 1, far_columns[:, 2 + h:3 + h])):
                        then_wait(dve.tensor_scalar(other_key, key_t[:, h, :], key_t[:, h, end:end + 1], NEVER,
                                                    ALU.not_equal, ALU.mult))
                        then_wait(dve.scalar_tensor_tensor(most, other_key, from_far, most, ALU.add, ALU.max))
                then_wait(dve.tensor_tensor(two(highest), g_t, two(highest), ALU.subtract))
                dve.sem_inc(max_ready, 1)

        with nc.Block() as block:

            @block.vector
            def _(dve):
                with dve.Fori(0, ETILES // SET) as n:
                    rows = pooled_rows[:, bass.ds(n * SET, SET), :]
                    dve.tensor_tensor(rows, rows, attention[:, bass.ds(n * SET, SET)].unsqueeze(2).to_broadcast(
                        [P, SET, XROW]), ALU.mult)

        seg3 = Segments(3, key_src[:, :], pairs_src, SPAN,
                        lambda e: pooled_rows[:, bass.ds(e, 1), :].rearrange("p a f -> p (a f)"),
                        lambda half, t: wide[half][:, t, 0:XROW])
        x3_back = [sem(f"x3_back{u}") for u in range(4)]
        denominator_made = sem("denominator_made")
        share3_made = sem("share3_made")
        has_edges_made = sem("has_edges_made")
        pooled_turned = sem("pooled_turned")
        pooled_moved = sem("pooled_moved")
        update3_made = sem("update3_made")
        norm4 = Norm(3, out, update3_made, act_tiles=4)

        with nc.Block() as block:

            @block.sync
            def _(sp):
                def stage(h):
                    if h.live():
                        norm4.wait(sp, y_made, h.k - 3)
                        load_half(sp, x3_rows, h, x3_back)
                    b = h.minus(8)
                    if h.u % 2 == 0 and b.live():
                        norm4.store(sp, b)

                each_half(sp, stage, 8)
                norm4.finish(sp)

            @block.tensor
            def _(pe):
                registers = first_registers["pe"]
                seg3.start(pe)

                def stage(h):
                    if h.live():
                        seg3.add_up(pe, registers, h)
                    b = h.minus(2)
                    if b.live():
                        seg3.wait_moved(pe, b.k + 1)
                        pe.wait_ge(has_edges_made, b.k + 1)
                        wait(pe, pooled_moved, b.k)
                        for t in range(4):
                            pe.transpose(bank[1][:, t * P:(t + 1) * P], pair[0][:, b.u % 2, t * D:(t + 1) * D],
                                         ident[:, :])
                        pe.transpose(bank[0][0:5, 0:P], has_edges[:, b.u % 2, :], ident[:, :]).then_inc(pooled_turned, 1)
                    c = h.minus(3)
                    if c.live():
                        q = c.u % 2
                        norm4.wait(pe, y_made, c.k - 1)
                        pe.wait_ge(pooled_moved, c.k + 1)
                        pe.matmul(bank[2 + q][:, :], lhsT=has_edges_t[0:5, q, :], rhs=bias_diag[0:5, :], start=True,
                                  stop=False, skip_group_check=True)
                        for t in range(4):
                            last = pe.matmul(bank[2 + q][:, t * D:(t + 1) * D], lhsT=pair[1][:, q, t * P:(t + 1) * P],
                                             rhs=w_pool, start=False, stop=t == 3, skip_group_check=True)
                        last.then_inc(update3_made, 1)

                each_half(pe, stage, 3)

            @block.scalar
            def _(act):
                def stage(h):
                    a = h.minus(1)
                    par = a.u % 2
                    if a.live():
                        act.wait_ge(has_edges_made, a.k + 1)
                        wait(act, pooled_turned, a.k - 1)
                        for t in range(4):
                            last = act.activation(pair[0][:, par, t * D:(t + 1) * D], wide[par][:, t, 0:D], ACT.Copy,
                                                  scale=share[:, par, t:t + 1])
                        last.then_inc(sums_moved, 1)
                    b = h.minus(2)
                    if b.live():
                        act.wait_ge(pooled_turned, b.k + 1)
                        wait(act, update3_made, b.k - 1)
                        act.activation(pair[1][:, b.u % 2, :], bank[1][:, :], ACT.Copy)
                        act.activation(has_edges_t[0:5, b.u % 2, :], bank[0][0:5, 0:P],
                                       ACT.Copy).then_inc(pooled_moved, 1)
                    c = h.minus(4)
                    if c.live():
                        norm4.root(act, c)
                    d = h.minus(5)
                    if d.live():
                        norm4.on_act(act, d)

                each_half(act, stage, 5)

            @block.vector
            def _(dve):
                registers = first_registers["dve"]

                def stage(h):
                    if h.live():
                        more = seg3.build(dve, registers, h)
                    elif h.k == HALVES:
                        more = seg3.entries(dve, registers, h)(0)
                    b = h.minus(4)
                    if b.live():
                        dve.wait_ge(x3_back[b.u], b.landed())
                    norm4.on_vector(dve, b, h.minus(5), lambda h: bank[2 + h.u % 2][:, :])
                    a = h.minus(1)
                    par = a.u % 2
                    if a.live():
                        seg3.wait_sums(dve, a, more)
                        seg3.wait_moved(dve, a.k - 1)
                        wait(dve, has_edges_made, a.k - 1)
                        dve.tensor_scalar(degree[:, par, :], wide[par][:, :, D], 1e-16, None,
                                          ALU.add).then_inc(denominator_made, 1)
                        dve.wait_ge(denominator_made, a.k + 1)
                        dve.reciprocal(share[:, par, :], degree[:, par, :]).then_inc(share3_made, 1)
                        dve.wait_ge(share3_made, a.k + 1)
                        wait(dve, pooled_turned, a.k - 1)
                        dve.tensor_tensor(has_edges[:, par, 0:4], wide[par][:, :, D], share[:, par, :],
                                          ALU.mult).then_inc(has_edges_made, 1)

                each_half(dve, stage, 5)


_INS = ["x", "src", "dst", "edge_type_1344", "edge_type_9", "edge_weight1", "L0_gnn_basis", "L0_gnn_comp",
        "L0_gnn_bias", "L0_gnn_gamma", "L0_gnn_beta", "L1_gnn_W_neigh", "L1_gnn_W_self", "L1_gnn_b",
        "L2_gnn_W_msg", "L2_gnn_b_msg", "L2_gnn_edge_embed", "L2_gnn_W_ih", "L2_gnn_W_hh", "L2_gnn_b_ih",
        "L2_gnn_b_hh", "L3_gnn_W_lin", "L3_gnn_b_lin", "L3_gnn_W_gate", "L3_gnn_b_gate", "L3_gnn_W_out",
        "L3_gnn_b_out"]
_OUTS = [((50000, 128), "float32")]


def kernel(**inputs):
    import numpy as _np
    import concourse.bacc as _bacc
    from concourse import mybir as _mybir
    from concourse.bass_utils import run_bass_kernel_spmd as _run

    nc = _bacc.Bacc("TRN2", target_bir_lowering=False, num_devices=1)
    arrays, args = {}, []
    for name in _INS:
        a = _np.ascontiguousarray(inputs[name])
        arrays[f"in_{name}_dram"] = a
        args.append(nc.dram_tensor(f"in_{name}_dram", a.shape, _mybir.dt.from_np(a.dtype), kind="ExternalInput").ap())
    for i, (shape, dtype) in enumerate(_OUTS):
        dt = _mybir.dt.from_np(_np.dtype(dtype))
        args.append(nc.dram_tensor(f"out_{i}_dram", shape, dt, kind="ExternalOutput").ap())
    build(nc, *args)
    r = _run(nc, [arrays], core_ids=[0])
    got = tuple(r.results[0][f"out_{i}_dram"] for i in range(len(_OUTS)))
    return got[0]
```
